# Optimizing a Trainium2 kernel written in Bass

```python
import numpy as np
import jax
import jax.numpy as jnp

def _softmax(x, axis=-1):
    return jax.nn.softmax(x, axis=axis)

def _gelu(x):
    return jax.nn.gelu(x, approximate=True)

def _silu(x):
    return jax.nn.silu(x)

def _sigmoid(x):
    return jax.nn.sigmoid(x)

def _layernorm(x, axis=-1, eps=1e-05):
    m = jnp.mean(x, axis=axis, keepdims=True)
    v = jnp.var(x, axis=axis, keepdims=True)
    return (x - m) / jnp.sqrt(v + eps)

def _scatter_add(tgt, idx, src, axis=0):
    return tgt.at[idx].add(src)

def _segment_sum(src, seg, n):
    return jax.ops.segment_sum(src, seg, n)
kernel_name = 'mk_gnn_ffn_d2_gnn_r16_515367'

def setup_inputs(seed: int=0):
    np.random.seed(seed)
    _w = jnp.asarray

    def _rec_inputs():
        import jax
        import jax.numpy as jnp
        _gk = jax.random.key(seed)
        x = -0.0003929 + 0.9999 * jax.random.normal(jax.random.fold_in(_gk, 1), (6250, 256), jnp.float32)
        src = jax.random.randint(jax.random.fold_in(_gk, 2), (100000,), 0, 6250, jnp.int32)
        dst = jax.random.randint(jax.random.fold_in(_gk, 3), (100000,), 0, 6250, jnp.int32)
        _o = jnp.argsort(dst, stable=True)
        src = src[_o]
        dst = dst[_o]
        edge_weight = jax.random.uniform(jax.random.fold_in(_gk, 13), (100000,), jnp.float32, 0.0, 0.999999)
        return (x, src, dst, edge_weight)
    x, src, dst, edge_weight = _rec_inputs()

    def _L0_gnn_setup():
        import jax, jax.numpy as jnp
        import numpy as np
        N_NODES = 4096
        N_EDGES = 65536
        HEADS = 4
        HEAD_DIM = 64
        DIM = 256
        BN_EPS = 1e-05
        key = jax.random.key(seed)
        k1, k2, k3, k4 = jax.random.split(key, 4)
        features = jax.random.normal(k1, (N_NODES, DIM), dtype=jnp.float32)
        src = jax.random.randint(k2, (N_EDGES,), 0, N_NODES, dtype=jnp.int64)
        dst = jax.random.randint(k3, (N_EDGES,), 0, N_NODES, dtype=jnp.int64)
        W_src = jax.random.normal(k4, (DIM, HEADS * HEAD_DIM), dtype=jnp.float32) * (1.0 / np.sqrt(DIM))
        gamma = jnp.ones((DIM,), dtype=jnp.float32)
        beta = jnp.zeros((DIM,), dtype=jnp.float32)
        return {'features': features, 'src': src, 'dst': dst, 'W_src': W_src, 'gamma': gamma, 'beta': beta}
    _L0_gnn_all = _L0_gnn_setup()
    _L0_gnn_in = {k: v for k, v in _L0_gnn_all.items() if k in ('W_src', 'gamma', 'beta')}
    del _L0_gnn_all

    def _L0_ffn_setup():
        import jax, jax.numpy as jnp
        import numpy as np
        C = 256
        HID = 1024
        E = 8
        TEMP = 1.0
        key = jax.random.key(seed)
        ks = jax.random.split(key, 7)
        x = jax.random.normal(ks[0], (8, 1024, C), dtype=jnp.float32)
        W1 = jax.random.normal(ks[1], (C, HID), dtype=jnp.float32) * 0.02
        b1 = jnp.zeros((HID,), dtype=jnp.float32)
        Wg = jax.random.normal(ks[2], (HID, E), dtype=jnp.float32) * 0.02
        bg = jnp.zeros((E,), dtype=jnp.float32)
        Wd = jax.random.normal(ks[3], (E, HID, C), dtype=jnp.float32) * 0.02
        bd = jnp.zeros((E, C), dtype=jnp.float32)
        return {'x': x, 'W1': W1, 'b1': b1, 'Wg': Wg, 'bg': bg, 'Wd': Wd, 'bd': bd}
    _L0_ffn_all = _L0_ffn_setup()
    _L0_ffn_in = {k: v for k, v in _L0_ffn_all.items() if k in ('W1', 'b1', 'Wg', 'bg', 'Wd', 'bd')}
    del _L0_ffn_all

    def _L1_gnn_setup():
        import jax, jax.numpy as jnp
        import numpy as np
        N_NODES = 6250
        N_EDGES = 100000
        D = 256
        key = jax.random.key(seed)
        ks = jax.random.split(key, 8)
        h6_all = jax.random.normal(ks[0], (N_NODES, D), dtype=jnp.float32)
        edge_index = jax.random.randint(ks[1], (2, N_EDGES), 0, N_NODES, dtype=jnp.int64)
        edge_weight = jax.random.uniform(ks[2], (N_EDGES,), dtype=jnp.float32)
        s = 1.0 / np.sqrt(D)
        W = jax.random.normal(ks[3], (D, D), dtype=jnp.float32) * s
        b = jnp.zeros((D,), dtype=jnp.float32)
        W1 = jax.random.normal(ks[4], (D, D), dtype=jnp.float32) * s
        b1 = jnp.zeros((D,), dtype=jnp.float32)
        W2 = jax.random.normal(ks[5], (D, D), dtype=jnp.float32) * s
        b2 = jnp.zeros((D,), dtype=jnp.float32)
        return {'h6_all': h6_all, 'edge_index': edge_index, 'edge_weight': edge_weight, 'W': W, 'b': b, 'W1': W1, 'b1': b1, 'W2': W2, 'b2': b2}
    _L1_gnn_all = _L1_gnn_setup()
    _L1_gnn_in = {k: v for k, v in _L1_gnn_all.items() if k in ('W', 'b', 'W1', 'b1', 'W2', 'b2')}
    del _L1_gnn_all

    def _L1_ffn_setup():
        import jax, jax.numpy as jnp
        import numpy as np
        D_MODEL = 256
        EXPERT_DIM = 512
        NUM_EXPERTS = 8
        TOP_K = 2
        SEQ_LEN = 128
        BATCH = 2
        key = jax.random.key(seed)
        ks = jax.random.split(key, 8)
        s = 0.02
        x = jax.random.normal(ks[0], (SEQ_LEN, BATCH, D_MODEL), dtype=jnp.float32)
        Wg = jax.random.normal(ks[1], (D_MODEL, NUM_EXPERTS), dtype=jnp.float32) * s
        bg = jax.random.normal(ks[2], (NUM_EXPERTS,), dtype=jnp.float32) * s
        bias = jnp.zeros((NUM_EXPERTS,), dtype=jnp.float32)
        W1 = jax.random.normal(ks[3], (NUM_EXPERTS, D_MODEL, EXPERT_DIM), dtype=jnp.float32) * s
        b1 = jax.random.normal(ks[4], (NUM_EXPERTS, EXPERT_DIM), dtype=jnp.float32) * s
        W2 = jax.random.normal(ks[5], (NUM_EXPERTS, EXPERT_DIM, D_MODEL), dtype=jnp.float32) * s
        b2 = jax.random.normal(ks[6], (NUM_EXPERTS, D_MODEL), dtype=jnp.float32) * s
        return {'x': x, 'Wg': Wg, 'bg': bg, 'bias': bias, 'W1': W1, 'b1': b1, 'W2': W2, 'b2': b2}
    _L1_ffn_all = _L1_ffn_setup()
    _L1_ffn_in = {k: v for k, v in _L1_ffn_all.items() if k in ('Wg', 'bg', 'bias', 'W1', 'b1', 'W2', 'b2')}
    del _L1_ffn_all
    return {'x': x, 'src': src, 'dst': dst, 'edge_weight': edge_weight, 'L0_gnn_W_src': _L0_gnn_in['W_src'], 'L0_gnn_gamma': _L0_gnn_in['gamma'], 'L0_gnn_beta': _L0_gnn_in['beta'], 'L0_ffn_W1': _L0_ffn_in['W1'], 'L0_ffn_b1': _L0_ffn_in['b1'], 'L0_ffn_Wg': _L0_ffn_in['Wg'], 'L0_ffn_bg': _L0_ffn_in['bg'], 'L0_ffn_Wd': _L0_ffn_in['Wd'], 'L0_ffn_bd': _L0_ffn_in['bd'], 'L1_gnn_W': _L1_gnn_in['W'], 'L1_gnn_b': _L1_gnn_in['b'], 'L1_gnn_W1': _L1_gnn_in['W1'], 'L1_gnn_b1': _L1_gnn_in['b1'], 'L1_gnn_W2': _L1_gnn_in['W2'], 'L1_gnn_b2': _L1_gnn_in['b2'], 'L1_ffn_Wg': _L1_ffn_in['Wg'], 'L1_ffn_bg': _L1_ffn_in['bg'], 'L1_ffn_bias': _L1_ffn_in['bias'], 'L1_ffn_W1': _L1_ffn_in['W1'], 'L1_ffn_b1': _L1_ffn_in['b1'], 'L1_ffn_W2': _L1_ffn_in['W2'], 'L1_ffn_b2': _L1_ffn_in['b2']}

def reference(x, src, dst, edge_weight, L0_gnn_W_src, L0_gnn_gamma, L0_gnn_beta, L0_ffn_W1, L0_ffn_b1, L0_ffn_Wg, L0_ffn_bg, L0_ffn_Wd, L0_ffn_bd, L1_gnn_W, L1_gnn_b, L1_gnn_W1, L1_gnn_b1, L1_gnn_W2, L1_gnn_b2, L1_ffn_Wg, L1_ffn_bg, L1_ffn_bias, L1_ffn_W1, L1_ffn_b1, L1_ffn_W2, L1_ffn_b2):
    import jax
    import jax.numpy as jnp

    def _L0_gnn_ref(features, src, dst, W_src, gamma, beta):
        import jax, jax.numpy as jnp
        import numpy as np
        N_NODES = 4096
        N_EDGES = 65536
        HEADS = 4
        HEAD_DIM = 64
        DIM = 256
        BN_EPS = 1e-05
        n = features.shape[0]
        feat_src = (features @ W_src).reshape(n, HEADS, HEAD_DIM)
        msgs = feat_src[src]
        sums = jax.ops.segment_sum(msgs, dst, num_segments=n)
        deg = jax.ops.segment_sum(jnp.ones((msgs.shape[0],), dtype=features.dtype), dst, num_segments=n)
        rst = sums / jnp.maximum(deg, 1.0)[:, None, None]
        rst = rst + features.reshape(n, HEADS, HEAD_DIM)
        x = rst.reshape(n, DIM)
        mean = jnp.mean(x, axis=0)
        var = jnp.mean(jnp.square(x - mean), axis=0)
        x = (x - mean) * jax.lax.rsqrt(var + BN_EPS) * gamma + beta
        return jax.nn.relu(x)

    def _L0_ffn_ref(x, W1, b1, Wg, bg, Wd, bd):
        import jax, jax.numpy as jnp
        import numpy as np
        C = 256
        HID = 1024
        E = 8
        TEMP = 1.0
        orig_shape = x.shape
        xf = x.reshape(-1, orig_shape[-1])
        H = jax.nn.gelu(xf @ W1 + b1, approximate=False)
        probs = jax.nn.softmax((H @ Wg + bg) / TEMP, axis=-1)
        assign = jnp.argmax(probs, axis=-1)
        out = jnp.zeros_like(xf)
        for e in range(Wd.shape[0]):
            y = H @ Wd[e] + bd[e]
            sel = (assign == e)[:, None]
            out = out + jnp.where(sel, probs[:, e:e + 1] * y, 0.0)
        return out.reshape(orig_shape)

    def _L1_gnn_ref(h6_all, edge_index, edge_weight, W, b, W1, b1, W2, b2):
        import jax, jax.numpy as jnp
        import numpy as np
        N_NODES = 6250
        N_EDGES = 100000
        D = 256
        'GCNConv(256->256, weighted, self-loops, symmetric norm) + 2-layer MLP head.'
        N = h6_all.shape[0]
        row, col = (edge_index[0], edge_index[1])
        sl = jnp.arange(N, dtype=edge_index.dtype)
        row_sl = jnp.concatenate([row, sl])
        col_sl = jnp.concatenate([col, sl])
        ew_sl = jnp.concatenate([edge_weight, jnp.ones((N,), dtype=edge_weight.dtype)])
        deg = jax.ops.segment_sum(ew_sl, row_sl, num_segments=N)
        dinv = jnp.where(deg > 0, jax.lax.rsqrt(deg), 0.0)
        norm = dinv[row_sl] * ew_sl * dinv[col_sl]
        xw = h6_all @ W
        msgs = xw[col_sl] * norm[:, None]
        h7 = jax.ops.segment_sum(msgs, row_sl, num_segments=N) + b
        h = jax.nn.relu(h7 @ W1 + b1)
        out = h @ W2 + b2
        return out

    def _L1_ffn_ref(x, Wg, bg, bias, W1, b1, W2, b2):
        import jax, jax.numpy as jnp
        import numpy as np
        D_MODEL = 256
        EXPERT_DIM = 512
        NUM_EXPERTS = 8
        TOP_K = 2
        SEQ_LEN = 128
        BATCH = 2
        x_flat = x.reshape(-1, D_MODEL)
        gate_logits = x_flat @ Wg + bg + bias
        topk_vals, topk_idx = jax.lax.top_k(gate_logits, TOP_K)
        topk_w = jax.nn.softmax(topk_vals, axis=-1)
        combine = (jax.nn.one_hot(topk_idx, NUM_EXPERTS, dtype=x.dtype) * topk_w[..., None]).sum(axis=1)
        h = jax.nn.relu(jnp.einsum('td,edh->teh', x_flat, W1) + b1)
        y = jnp.einsum('teh,ehd->ted', h, W2) + b2
        out = jnp.einsum('ted,te->td', y, combine)
        return out.reshape(x.shape)
    edge_index = jnp.stack([src, dst])
    x = x + _L0_gnn_ref(_layernorm(x, axis=-1), src, dst, L0_gnn_W_src, L0_gnn_gamma, L0_gnn_beta)
    x = x + _L0_ffn_ref(_layernorm(x, axis=-1)[None], L0_ffn_W1, L0_ffn_b1, L0_ffn_Wg, L0_ffn_bg, L0_ffn_Wd, L0_ffn_bd)[0]
    x = x + _L1_gnn_ref(_layernorm(x, axis=-1), edge_index, edge_weight, L1_gnn_W, L1_gnn_b, L1_gnn_W1, L1_gnn_b1, L1_gnn_W2, L1_gnn_b2)
    x = x + _L1_ffn_ref(_layernorm(x, axis=-1)[None], L1_ffn_Wg, L1_ffn_bg, L1_ffn_bias, L1_ffn_W1, L1_ffn_b1, L1_ffn_W2, L1_ffn_b2)[0]
    return x

_drawn_inputs = setup_inputs


def setup_inputs(seed=0):
    import zlib

    import numpy as np

    out = dict(_drawn_inputs(seed))
    spreads = {'L0_gnn_gamma': (1.0, 0.2),
     'L0_gnn_beta': (0.0, 0.1),
     'L0_ffn_b1': (0.0, 0.8),
     'L0_ffn_bg': (0.0, 0.562),
     'L0_ffn_bd': (0.0, 0.776),
     'L1_gnn_b': (0.0, 0.27),
     'L1_gnn_b1': (0.0, 0.32),
     'L1_gnn_b2': (0.0, 0.1),
     'L1_ffn_bias': (0.0, 0.403)}
    factors = {'L0_ffn_W1': 3.948,
     'L0_ffn_Wg': 4.243,
     'L0_ffn_Wd': 4.691,
     'L1_ffn_bg': 16.631,
     'L1_ffn_b1': 34.746,
     'L1_ffn_b2': 6.228}
    for name, (base, spread) in spreads.items():
        noise = np.random.default_rng([zlib.crc32(name.encode()), seed]).standard_normal(out[name].shape)
        drawn = base * np.exp(spread * noise) if base else spread * noise
        out[name] = jnp.asarray(drawn.astype(out[name].dtype))
    for name, factor in factors.items():
        out[name] = (out[name] * factor).astype(out[name].dtype)
    return out
```

```python
import numpy as np

import concourse.bass as bass
from concourse import mybir
from concourse.bass import IndirectOffsetOnAxis, ds

F32 = mybir.dt.float32
I32 = mybir.dt.int32
U16 = mybir.dt.uint16
U32 = mybir.dt.uint32
BF16 = mybir.dt.bfloat16
ALU = mybir.AluOpType
ACT = mybir.ActivationFunctionType
AX = mybir.AxisListType
ENG = mybir.EngineType

P = 128
N = 6250
D = 256
T = -(-N // P)
LAST = N - (T - 1) * P
KD = D // P
NE = 100000
EP, EC = 125, 800
CH = -(-NE // P)
ITEMS = CH + T - 1
IJ = -(-ITEMS // P)
AW = D + 1
REC = 3
HID0, E0 = 1024, 8
KH0 = HID0 // P
HID1, E1 = 512, 8
KH1 = HID1 // P
SLOTS0 = (T * P + E0 * (P - 1)) // P
SLOTS1 = (2 * T * P + E1 * (P - 1)) // P
LN_EPS = 1e-5
BN_EPS = 1e-5
RING = 12
G7 = 7
QT = 4


class Queue:

    def __init__(self, nc, engine, name):
        self.e = engine
        self.done = nc.alloc_semaphore(name)
        self.count = 0
        self.last = None
        self.met = {}

    def after(self, *tickets):
        for t in tickets:
            if t is None:
                continue
            if isinstance(t, list):
                self.after(*t)
                continue
            sem, value = t
            if self.met.get(id(sem), 0) < value:
                self.e.wait_ge(sem, value)
                self.met[id(sem)] = value

    def do(self, instruction):
        instruction.then_inc(self.done, 1)
        self.count += 1
        self.last = (self.done, self.count)
        return self.last

    def step(self, instruction):
        t = self.do(instruction)
        self.after(t)
        return t


class Lane:

    def __init__(self, nc, name):
        self.sem = nc.alloc_semaphore(name)
        self.total = 0

    @property
    def ticket(self):
        return (self.sem, self.total) if self.total else None

    def start(self, queue, make, *tickets):
        queue.after(*tickets, self.ticket)
        return self.add(make())

    def add(self, instruction):
        instruction.then_inc(self.sem, 16)
        self.total += 16
        return self.ticket


def build(nc, x, src, dst, edge_weight, g0_w, g0_gamma, g0_beta, f0_w1, f0_b1, f0_wg, f0_bg, f0_wd,
          f0_bd, g1_w, g1_b, g1_w1, g1_b1, g1_w2, g1_b2, f1_wg, f1_bg, f1_bias, f1_w1, f1_b1, f1_w2,
          f1_b2, out):
    V = Queue(nc, nc.vector, "vector_done")
    S = Queue(nc, nc.scalar, "scalar_done")
    M = Queue(nc, nc.tensor, "tensor_done")
    G = Queue(nc, nc.gpsimd, "gpsimd_done")
    Y = Queue(nc, nc.sync, "sync_done")
    v, s, m, g, y = nc.vector, nc.scalar, nc.tensor, nc.gpsimd, nc.sync

    def region(name, nbytes):
        return nc.alloc_sbuf_tensor(name, [P, nbytes // 4], F32)

    def view(reg, off, n, dt=F32, parts=P):
        size = 2 if dt in (BF16, U16) else 4
        v32 = reg[0:parts, off // 4:(off + n * size) // 4]
        return v32 if dt == F32 else v32.bitcast(dt)

    def small(name, n, dt=F32):
        return nc.alloc_sbuf_tensor(name, [P, n], dt)

    def reg_values(engine, ap, most):
        return nc.values_load_multi_w_load_instructions(
            ap, engines=[engine], min_val=0, max_val=most,
            skip_runtime_bounds_check_because="clamped to the last tile or expert where it is computed")[1]

    X = nc.alloc_sbuf_tensor("x_rows", [P, T, D], F32)
    XN = nc.alloc_sbuf_tensor("normed", [P, T * D], F32)
    XNt = XN[:, :].rearrange("p (t d) -> p t d", d=D)
    C = region("acc_or_weights", 4 * E0 * KH0 * D)
    R = region("ring_or_weights", 16384)
    rec1 = nc.alloc_sbuf_tensor("edge_records_by_src", [P, EC, REC], F32)
    posr = region("edge_positions", 4 * EC)
    dloc = small("item_local_node", IJ * P)
    gidx = small("item_other_node", IJ * P, I32)
    wt = small("item_weight", IJ * P)
    iota = small("iota_row", P)
    ident = small("identity", P)
    ones = small("ones", P)
    ones_last = small("ones_of_last_tile", P)
    tri = small("earlier_partitions", P)
    mv = nc.alloc_sbuf_tensor("mean_var", [P, T, 2], F32)
    rstd = small("rstd", T)
    deg = small("node_degree", T)
    stats = nc.alloc_sbuf_tensor("bn_stats_ring", [P, 4, 6], F32)
    toff = small("item_acc_offset", P, I32)
    pos = small("token_slot", 2 * T, I32)
    gate = small("token_gate", 2 * T)
    texp = small("slot_expert_offset", SLOTS1, I32)
    texp2 = texp
    tot = [small(f"tile_edges{k}", T) for k in range(2)]
    incl = [small(f"tile_edge_ends{k}", T) for k in range(2)]
    offs = [small(f"tile_edge_offsets{k}", T) for k in range(2)]
    bcol = small("bias_columns", 16)
    bank = [nc.alloc_psum_tensor(f"bank{k}", [P, 512], F32) for k in range(8)]

    rec_d = [nc.dram_tensor(f"ordered_edges{k}", (CH * P, REC), F32, kind="Internal").ap() for k in range(2)]
    tab = nc.dram_tensor("gather_table", (T * P, D), F32, kind="Internal").ap()
    tab1 = nc.dram_tensor("gather_table1", (T * P, D), F32, kind="Internal").ap()
    slot_x = [nc.dram_tensor(f"slot_rows{k}", (n * P, D), F32, kind="Internal").ap() for k, n in enumerate((SLOTS0, SLOTS1))]
    slot_y = [nc.dram_tensor(f"slot_out{k}", (n * P, D), F32, kind="Internal").ap() for k, n in enumerate((SLOTS0, SLOTS1))]

    raw_src = view(C, 0, EC, I32, EP)
    raw_dst = view(C, 3200, EC, I32, EP)
    raw_w = view(C, 6400, EC, F32, EP)
    rec0 = view(C, 9600, EC * REC).rearrange("p (e r) -> p e r", r=REC)
    idx0 = view(C, 19200, EC, I32)
    int_tmp = view(C, 22400, EC, I32)
    kt0 = view(C, 25600, EC, BF16)
    acc = view(C, 0, T * AW).rearrange("p (t a) -> p t a", a=AW)
    tail = 4 * T * AW
    kt1 = view(C, tail, EC, BF16)
    mask_e = view(C, tail + 1600, EC, BF16)
    ones_e = view(C, tail + 3200, EC, BF16)
    scan_e = view(C, tail + 4800, EC)
    pos_e = view(C, tail + 8000, EC)
    neg_lo = view(C, tail + 11200, EC)
    kt1f = view(posr, 0, EC)
    idx1 = view(posr, 0, EC, I32)

    load_e, load_x, load_c = Lane(nc, "edges_loaded"), Lane(nc, "x_loaded"), Lane(nc, "consts_loaded")
    load_e.add(y.dma_start(raw_dst, dst.rearrange("(p e) -> p e", e=EC)))
    load_e.add(y.dma_start(raw_src, src.rearrange("(p e) -> p e", e=EC)))
    load_e.add(y.dma_start(raw_w, edge_weight.rearrange("(p e) -> p e", e=EC)))
    V.do(v.memset(X[:, T - 1, :], 0.0))
    for a in range(0, T - 1, 8):
        load_x.add(s.dma_start(X[:, a:a + 8, :], x[a * P:(a + 8) * P, :].rearrange("(t p) d -> p t d", p=P)))
    S.after(V.last)
    load_x.add(s.dma_start(X[0:LAST, T - 1, :], x[(T - 1) * P:N, :]))

    V.do(v.memset(ones[:, :], 1.0))
    V.do(v.memset(ident[:, :], 0.0))
    G.do(g.iota(iota[:, :], pattern=[[1, P]], base=0, channel_multiplier=0, allow_small_or_imprecise_dtypes=True))
    G.after(V.last)
    G.do(g.affine_select(out=tri[:, :], in_=ones[:, :], compare_op=ALU.is_gt, fill=0.0, base=0,
                         pattern=[[1, P]], channel_multiplier=-1))
    G.do(g.affine_select(out=ones_last[:, :], in_=ones[:, :], compare_op=ALU.is_gt, fill=0.0, base=LAST,
                         pattern=[[0, P]], channel_multiplier=-1))
    consts = G.do(g.affine_select(out=ident[:, :], in_=ident[:, :], compare_op=ALU.not_equal, fill=1.0, base=0,
                                  pattern=[[-1, P]], channel_multiplier=1))
    for q in (V, S, M):
        q.after(consts)

    V.after(load_e.ticket)
    V.do(v.memset(rec0[:, :, :], -1.0))
    V.do(v.memset(rec1[:, :, :], -1.0))
    V.after(V.last)
    for rec, key, other, kt in ((rec0, raw_dst, raw_src, kt0), (rec1[:, :, :], raw_src, raw_dst, kt1)):
        V.do(v.tensor_copy(rec[0:EP, :, 0], key))
        V.do(v.tensor_copy(rec[0:EP, :, 1], other))
        V.do(v.tensor_copy(rec[0:EP, :, 2], raw_w))
        V.step(v.tensor_scalar(int_tmp[0:EP], key, 7, None, ALU.arith_shift_right))
        V.step(v.tensor_copy(kt[0:EP], int_tmp[0:EP]))
    V.step(v.tensor_copy(scan_e[0:EP], int_tmp[0:EP]))
    V.step(v.scalar_tensor_tensor(neg_lo[0:EP], scan_e[0:EP], float(P), rec1[0:EP, :, 0], ALU.mult, ALU.subtract))
    V.do(v.tensor_copy(kt1f[0:EP], scan_e[0:EP]))
    V.step(v.memset(ones_e, 1.0))

    def count_tiles(kt, k):
        scratch = [mask_e, scan_e.bitcast(BF16)[:, 0:EC]]
        cnt = offs[k]
        before = [None, None]
        for t in range(T):
            V.after(before[t % 2])
            before[t % 2] = V.do(v.tensor_scalar(scratch[t % 2][0:EP], kt[0:EP], float(t), None, ALU.is_equal,
                                                 ALU.add, accum_out=cnt[0:EP, t:t + 1]))
        M.after(V.last)
        M.do(m.matmul(bank[0][:, 0:T], lhsT=ones[0:EP, :], rhs=cnt[0:EP, :], start=True, stop=True))
        M.do(m.matmul(bank[1][:, 0:T], lhsT=tri[0:EP, :], rhs=cnt[0:EP, :], start=True, stop=True))
        V.after(M.last)
        V.step(v.tensor_copy(tot[k][:, :], bank[0][:, 0:T]))
        V.step(v.tensor_tensor_scan(incl[k][:, :], ones[:, 0:T], tot[k][:, :], 0.0, ALU.mult, ALU.add))
        V.step(v.scalar_tensor_tensor(offs[k][:, :], bank[1][:, 0:T], -1.0, incl[k][:, :], ALU.add, ALU.add))
        V.step(v.tensor_tensor(offs[k][:, :], offs[k][:, :], tot[k][:, :], ALU.subtract))

    def place_edges(kt, k, t):
        V.step(v.tensor_scalar(mask_e[0:EP], kt[0:EP], float(t), None, ALU.is_equal))
        V.step(v.tensor_tensor_scan(scan_e[0:EP], ones_e[0:EP], mask_e[0:EP], offs[k][0:EP, t:t + 1],
                                    ALU.mult, ALU.add))
        V.step(v.copy_predicated(pos_e[0:EP], mask_e[0:EP].bitcast(U16), scan_e[0:EP]))

    scatter_lanes = [Lane(nc, f"edge_scatter{k}") for k in range(8)]
    pad_lane = Lane(nc, "edge_padding")

    def scatter_edges(k, rec, idx, c, *tickets):
        G.after(*tickets)
        return scatter_lanes[c % 8].start(
            G, lambda: g.indirect_dma_start(rec_d[k], IndirectOffsetOnAxis(ap=idx[0:EP, c:c + 1], axis=0),
                                            rec[0:EP, c, :], None))

    npad = CH * P - NE
    neg = view(R, 0, REC)
    V.do(v.memset(neg, -1.0))
    Y.after(V.last)
    for k in range(2):
        pad_lane.add(y.dma_start(rec_d[k][NE:CH * P, :], neg[0:npad, :]))

    count_tiles(kt0, 0)
    for t in range(T):
        place_edges(kt0, 0, t)
    placed0 = V.step(v.tensor_copy(idx0[0:EP], pos_e[0:EP]))
    for c in range(EC):
        scatter_edges(0, rec0, idx0, c, placed0)

    table_lane = [Lane(nc, "table_written0"), Lane(nc, "table_written1")]

    def layernorm(scale=None, table=None, lane=None):
        tickets = []
        hist = []
        for a in range(0, T, G7):
            for t in range(a, a + G7):
                if len(hist) >= 4:
                    V.after(hist[-4])
                V.step(v.bn_stats(stats[:, t % 4, :], X[:, t, :]))
                hist.append(V.do(v.bn_aggr(mv[:, t, :], stats[:, t % 4, :])))
            V.after(V.last)
            r = rstd[:, a:a + G7]
            S.after(V.step(v.tensor_scalar(r, mv[:, a:a + G7, 1], LN_EPS, None, ALU.add)))
            V.after(S.do(s.activation(r, r, ACT.Sqrt)))
            V.step(v.reciprocal(r, r))
            if scale is not None:
                V.step(v.tensor_tensor(r, r, scale[:, a:a + G7], ALU.mult))
            for t in range(a, a + G7):
                V.do(v.tensor_scalar(XNt[:, t, :], X[:, t, :], mv[:, t, 0:1], rstd[:, t:t + 1],
                                     ALU.subtract, ALU.mult))
            tickets += [V.last] * G7
            if table is not None:
                Y.after(V.last)
                lane.add(y.dma_start(table[a * P:(a + G7) * P, :].rearrange("(t p) d -> p t d", p=P),
                                     XNt[:, a:a + G7, :]))
        return tickets

    V.after(load_x.ticket)
    layernorm(None, tab, table_lane[0])
    count_tiles(kt1, 1)

    run_lane = Lane(nc, "runs_gathered")

    def make_items(k):
        a = 4 * 2688
        runs = view(R, 0, IJ * P * REC).rearrange("p (j e r) -> p j e r", j=IJ, r=REC)
        tmp = view(R, a, IJ * T).rearrange("p (j t) -> p j t", t=T)
        o = a + 4 * IJ * T
        i_first, i_int, i_end, kcount, shift = [view(R, o + 196 * n, T, I32 if n == 1 else F32) for n in range(5)]
        o += 196 * 5
        item, ti, cf, tb = [view(R, o + 28 * n, IJ) for n in range(4)]
        ci = view(R, o + 28 * 4, IJ, I32)
        G.after(V.last)
        V.after(G.do(g.iota(item, pattern=[[P, IJ]], base=0, channel_multiplier=1, allow_small_or_imprecise_dtypes=True)))
        V.step(v.tensor_tensor(i_int, incl[k][:, :], tot[k][:, :], ALU.subtract))
        V.step(v.tensor_scalar(i_int, i_int, 7, None, ALU.arith_shift_right))
        V.step(v.tensor_copy(i_first, i_int))
        V.step(v.tensor_scalar(i_int, incl[k][:, :], float(P - 1), None, ALU.add))
        V.step(v.tensor_scalar(i_int, i_int, 7, None, ALU.arith_shift_right))
        V.step(v.tensor_tensor(kcount, i_int, i_first, ALU.subtract))
        V.step(v.scalar_tensor_tensor(kcount, tot[k][:, :], 0.0, kcount, ALU.is_gt, ALU.mult))
        V.step(v.tensor_tensor_scan(i_end, ones[:, 0:T], kcount, 0.0, ALU.mult, ALU.add))
        V.step(v.tensor_tensor(shift, i_first, i_end, ALU.subtract))
        V.step(v.tensor_tensor(shift, shift, kcount, ALU.add))
        V.step(v.tensor_tensor(tmp, i_end.unsqueeze(1).broadcast_to([P, IJ, T]),
                               item.unsqueeze(2).broadcast_to([P, IJ, T]), ALU.is_le))
        V.step(v.tensor_reduce(ti, tmp, AX.X, ALU.add))
        V.step(v.tensor_tensor(tmp, iota[:, 0:T].unsqueeze(1).broadcast_to([P, IJ, T]),
                               ti.unsqueeze(2).broadcast_to([P, IJ, T]), ALU.is_equal))
        V.step(v.tensor_tensor(tmp, tmp, shift.unsqueeze(1).broadcast_to([P, IJ, T]), ALU.mult))
        V.step(v.tensor_reduce(cf, tmp, AX.X, ALU.add))
        V.step(v.tensor_tensor(cf, cf, item, ALU.add))
        V.step(v.tensor_scalar(ci, cf, float(CH - 1), 0.0, ALU.min, ALU.max))
        runs_known = V.last
        V.step(v.tensor_scalar(tb, ti, float(P), None, ALU.mult))
        V.step(v.tensor_scalar(cf, ti, float(T - 1), float(AW), ALU.min, ALU.mult))
        M.after(V.last)
        M.do(m.transpose(bank[0][0:IJ, 0:P], cf, ident[:, :]))
        V.after(M.last)
        V.step(v.tensor_copy(toff[0:IJ, :], bank[0][0:IJ, 0:P]))
        G.after(runs_known, pad_lane.ticket, *[l.ticket for l in scatter_lanes])
        by_run = rec_d[k].rearrange("(c e) r -> c (e r)", e=P)
        for j in range(IJ):
            run_lane.add(g.indirect_dma_start(view(R, j * P * REC * 4, P * REC), None, by_run,
                                              IndirectOffsetOnAxis(ap=ci[:, j:j + 1], axis=0)))
        V.after(run_lane.ticket)
        for j in range(IJ):
            V.do(v.tensor_scalar(runs[:, j, :, 0], runs[:, j, :, 0], tb[:, j:j + 1], None, ALU.subtract))
        M.after(V.last)
        copied = {}
        for j in range(IJ):
            M.after(copied.get(j - 4))
            for f in range(REC):
                M.do(m.transpose(bank[j % 4][:, f * P:(f + 1) * P], runs[:, j, :, f], ident[:, :]))
            V.after(M.last)
            for f, to in enumerate((dloc, gidx, wt)):
                copied[j] = V.do(v.tensor_copy(to[:, j * P:(j + 1) * P], bank[j % 4][:, f * P:(f + 1) * P]))
            if j == IJ - 1:
                V.after(V.last)
        V.step(v.tensor_scalar(gidx[:, :], gidx[:, :], 0.0, None, ALU.max))

    make_items(0)

    ring_lanes = [Lane(nc, f"ring{k}") for k in range(RING)]
    ring = view(R, 0, RING * AW).rearrange("p (n a) -> p n a", a=AW)
    o = 4 * RING * AW
    onehot = view(R, o, 4 * P).rearrange("p (n c) -> p n c", c=P)
    lo_hot = view(R, o + 2048, 2 * P).rearrange("p (n c) -> p n c", c=P)
    lo_tmp = view(R, o + 3072, P)
    hi_hot = view(R, o + 3584, 2 * T).rearrange("p (n c) -> p n c", c=T)

    def aggregate(table, width, weighted, ready, extra):
        hot, summed, added = {}, {}, {}

        def one_hot(i):
            if i >= 4:
                V.after(summed[i - 4])
            if weighted:
                hot[i] = V.do(v.tensor_scalar(onehot[:, i % 4, :], iota[:, :], dloc[:, i:i + 1], wt[:, i:i + 1],
                                              ALU.is_equal, ALU.mult))
            else:
                hot[i] = V.do(v.tensor_scalar(onehot[:, i % 4, :], iota[:, :], dloc[:, i:i + 1], None,
                                              ALU.is_equal))

        G.after(*ready)
        one_hot(0)
        one_hot(1)
        regs = None
        for i in range(ITEMS):
            if i >= RING:
                G.after(summed[i - RING])
            rows = ring_lanes[i % RING].start(
                G, lambda: g.indirect_dma_start(ring[:, i % RING, 0:D], None, table,
                                                IndirectOffsetOnAxis(ap=gidx[:, i:i + 1], axis=0)))
            if i + 2 < ITEMS:
                one_hot(i + 2)
            M.after(hot[i], rows, added.get(i - 4))
            summed[i] = M.do(m.matmul(bank[i % 4][:, 0:width], lhsT=onehot[:, i % 4, :],
                                      rhs=ring[:, i % RING, 0:width], start=True, stop=True))
            extra(i)
            if i % 8 == 0:
                n = min(8, ITEMS - i)
                regs = reg_values(ENG.DVE, toff[i // P:i // P + 1, i % P:i % P + n], (T - 1) * AW)
            V.after(summed[i], added.get(i - 1))
            into = view(C, 0, T * AW)[:, ds(regs[i % 8], width)]
            added[i] = V.do(v.tensor_tensor(into, bank[i % 4][:, 0:width], into, ALU.add))
        V.after(V.last)

    deg_done = {}
    lo_done, hi_done = {}, {}

    def beside(i):
        if i < EC:
            S.after(lo_done.get(i - 1), deg_done.get(i - 2))
            S.do(s.activation(lo_tmp[0:EP], iota[0:EP, :], ACT.Abs, bias=neg_lo[0:EP, i:i + 1]))
            S.after(S.last)
            lo_done[i] = S.do(s.activation(lo_hot[0:EP, i % 2, :], lo_tmp[0:EP], ACT.Relu, bias=1.0, scale=-1.0))
            V.after(deg_done.get(i - 2))
            hi_done[i] = V.do(v.tensor_scalar(hi_hot[0:EP, i % 2, :], iota[0:EP, 0:T], kt1f[0:EP, i:i + 1],
                                              rec1[0:EP, i, 2:3], ALU.is_equal, ALU.mult))
            M.after(lo_done[i], hi_done[i])
            deg_done[i] = M.do(m.matmul(bank[7][:, 0:T], lhsT=lo_hot[0:EP, i % 2, :], rhs=hi_hot[0:EP, i % 2, :],
                                        start=i == 0, stop=i == EC - 1))
        if i % 16 == 8 and i // 16 < T:
            place_edges(kt1, 1, i // 16)

    V.after(V.last)
    V.do(v.memset(ring[:, :, D:AW], 1.0))
    V.step(v.memset(view(C, 0, T * AW), 0.0))
    aggregate(tab, AW, False, [V.last, table_lane[0].ticket], beside)

    V.after(deg_done[EC - 1])
    V.step(v.tensor_scalar(deg[:, :], bank[7][:, 0:T], 1.0, None, ALU.add))
    placed1 = V.step(v.tensor_copy(idx1[0:EP], pos_e[0:EP]))
    scatter_next = [0]

    def scatter_more(n):
        for c in range(scatter_next[0], min(EC, scatter_next[0] + n)):
            scatter_edges(1, rec1[:, :, :], idx1, c, placed1)
        scatter_next[0] = min(EC, scatter_next[0] + n)

    scatter_more(400)

    w_lane = Lane(nc, "weights_loaded")
    w0 = view(R, 8192, KD * D).rearrange("p (k n) -> p k n", k=KD)
    gam = view(R, 8192 + 2048, D)
    bet = view(R, 8192 + 3072, D)
    mean_b = view(R, 8192 + 4096, D)
    scale_b = view(R, 8192 + 5120, D)
    shift_b = view(R, 8192 + 6144, D)
    ring_free = [M.last, V.last]
    Y.after(*ring_free)
    w_lane.add(y.dma_start(w0, g0_w.rearrange("(k p) n -> p k n", p=P)))
    w_lane.add(y.dma_start(gam, g0_gamma.partition_broadcast(P)))
    w_lane.add(y.dma_start(bet, g0_beta.partition_broadcast(P)))
    W1a = view(R, 0, KD * HID0).rearrange("p (k n) -> p k n", k=KD)
    f0_lane = Lane(nc, "ffn0_weights_loaded")
    f0_lane.add(y.dma_start(W1a, f0_w1.rearrange("(k p) n -> p k n", p=P)))

    rdeg = view(R, 15360, T)
    V.step(v.tensor_scalar(rdeg, acc[:, :, D], 1.0, None, ALU.max))
    V.step(v.reciprocal(rdeg, rdeg))
    accT = view(C, tail, 2 * D).rearrange("p (n a) -> p n a", n=2)
    sq = view(C, tail + 2048, 2 * D).rearrange("p (n a) -> p n a", n=2)
    M.after(w_lane.ticket)
    copied, prod, rst = {}, {}, {}

    def transpose_rows(rows, to, dest, *tickets):
        M.after(*tickets)
        for k in range(KD):
            M.do(m.transpose(to[:, dest + k * P:dest + (k + 1) * P], rows[:, k * P:(k + 1) * P], ident[:, :]))
        return M.last

    sum_of = {}
    for t in range(T + 2):
        if t < T:
            tr = transpose_rows(acc[:, t, 0:D], bank[t % 2], 0, copied.get(t - 2))
            S.after(tr, prod.get(t - 2))
            copied[t] = S.do(s.activation(accT[:, t % 2, :], bank[t % 2][:, 0:D], ACT.Copy))
        if 1 <= t <= T:
            u = t - 1
            M.after(copied[u], rst.get(u - 2))
            for k in range(KD):
                prod[u] = M.do(m.matmul(bank[2 + u % 2][:, 0:D], lhsT=accT[:, u % 2, k * P:(k + 1) * P],
                                        rhs=w0[:, k, :], start=k == 0, stop=k == KD - 1))
            V.after(prod[u])
            rst[u] = V.do(v.scalar_tensor_tensor(XNt[:, u, :], bank[2 + u % 2][:, 0:D], rdeg[:, u:u + 1],
                                                 XNt[:, u, :], ALU.mult, ALU.add))
        if t >= 2:
            u = t - 2
            M.after(rst[u])
            M.do(m.matmul(bank[4][:, 0:D], lhsT=(ones_last if u == T - 1 else ones)[:, :], rhs=XNt[:, u, :],
                          start=u == 0, stop=u == T - 1))
    V.after(M.last)
    V.step(v.tensor_scalar(mean_b, bank[4][:, 0:D], 1.0 / N, None, ALU.mult))
    diff, sqd, sqm = {}, {}, {}
    for t in range(T):
        V.do(v.tensor_tensor(XNt[:, t, :], XNt[:, t, :], mean_b, ALU.subtract))
        S.after(V.last, sqm.get(t - 2))
        sqd[t] = S.do(s.activation(sq[:, t % 2, :], XNt[:, t, :], ACT.Square))
        M.after(sqd[t])
        sqm[t] = M.do(m.matmul(bank[5][:, 0:D], lhsT=(ones_last if t == T - 1 else ones)[:, :], rhs=sq[:, t % 2, :],
                               start=t == 0, stop=t == T - 1))
    V.after(M.last)
    V.step(v.tensor_scalar(scale_b, bank[5][:, 0:D], 1.0 / N, BN_EPS, ALU.mult, ALU.add))
    S.after(V.last)
    V.after(S.do(s.activation(scale_b, scale_b, ACT.Sqrt)))
    V.step(v.reciprocal(scale_b, scale_b))
    V.step(v.tensor_tensor(scale_b, scale_b, gam, ALU.mult))
    for a in range(0, T, G7):
        part = XNt[:, a:a + G7, :]
        xpart = X[:, a:a + G7, :]
        V.step(v.tensor_tensor(part, part, scale_b.unsqueeze(1).broadcast_to([P, G7, D]), ALU.mult))
        V.step(v.tensor_tensor(part, part, bet.unsqueeze(1).broadcast_to([P, G7, D]), ALU.add))
        V.step(v.scalar_tensor_tensor(xpart, part, 0.0, xpart, ALU.max, ALU.add))

    logits = view(dloc, 0, T * 8).rearrange("p (t e) -> p t e", e=8)
    probs = view(dloc, 4 * T * 8, T * 8).rearrange("p (t e) -> p t e", e=8)
    best = view(gidx[:, :].bitcast(F32), 0, T * 8).rearrange("p (t e) -> p t e", e=8)
    best_at = gidx[:, T * 8:2 * T * 8].rearrange("p (t e) -> p t e", e=8)
    chosen = view(wt, 0, 2 * T)
    rmask = view(wt, 8 * T, 2 * T)
    rscan = view(wt, 16 * T, 2 * T)
    rpos = view(wt, 24 * T, 2 * T)
    rones = view(wt, 32 * T, 2 * T)
    rcnt = view(wt, 40 * T, 8)
    roff = view(wt, 40 * T + 32, 8)
    rn = view(wt, 40 * T + 64, 8, I32)
    rnt = view(wt, 40 * T + 96, 8)
    rend = view(wt, 40 * T + 128, 8)
    rsmall = view(wt, 40 * T + 160, SLOTS1)

    def route(ncol, slots, row):
        V.step(v.memset(rones, 1.0))
        for e in range(8):
            V.step(v.tensor_scalar(rmask[:, 0:ncol], chosen[:, 0:ncol], float(e), None, ALU.is_equal, ALU.add,
                                   accum_out=rcnt[:, e:e + 1]))
        M.after(V.last)
        M.do(m.matmul(bank[0][:, 0:8], lhsT=ones[:, :], rhs=rcnt, start=True, stop=True))
        M.do(m.matmul(bank[1][:, 0:8], lhsT=tri[:, :], rhs=rcnt, start=True, stop=True))
        V.after(M.last)
        V.step(v.tensor_scalar(rn, bank[0][:, 0:8], float(P - 1), None, ALU.add))
        V.step(v.tensor_scalar(rn, rn, 7, None, ALU.arith_shift_right))
        V.step(v.tensor_copy(rnt, rn))
        V.step(v.tensor_tensor_scan(rend, ones[:, 0:8], rnt, 0.0, ALU.mult, ALU.add))
        V.step(v.tensor_tensor(roff, rend, rnt, ALU.subtract))
        V.step(v.tensor_scalar(roff, roff, float(P), -1.0, ALU.mult, ALU.add))
        V.step(v.tensor_tensor(roff, roff, bank[1][:, 0:8], ALU.add))
        for e in range(8):
            V.step(v.tensor_scalar(rmask[:, 0:ncol], chosen[:, 0:ncol], float(e), None, ALU.is_equal))
            V.step(v.tensor_tensor_scan(rscan[:, 0:ncol], rones[:, 0:ncol], rmask[:, 0:ncol], roff[:, e:e + 1],
                                        ALU.mult, ALU.add))
            V.step(v.copy_predicated(rpos[:, 0:ncol], rmask[:, 0:ncol].bitcast(U32), rscan[:, 0:ncol]))
        placed = V.step(v.tensor_copy(pos[:, 0:ncol], rpos[:, 0:ncol]))
        cmp = gidx[0:1, 0:slots * 8].bitcast(F32)
        cmp = cmp.rearrange("p (i e) -> p i e", e=8)
        V.step(v.tensor_tensor(cmp, rend[0:1].unsqueeze(1).broadcast_to([1, slots, 8]),
                               iota[0:1, 0:slots].unsqueeze(2).broadcast_to([1, slots, 8]), ALU.is_le))
        V.step(v.tensor_reduce(rsmall[0:1, 0:slots], cmp, AX.X, ALU.add))
        V.step(v.tensor_scalar(texp[0:1, 0:slots], rsmall[0:1, 0:slots], 7.0, float(row), ALU.min, ALU.mult))
        return placed

    slot_lanes = [Lane(nc, f"slot_scatter{k}") for k in range(8)]

    def scatter_tokens(dest, ncol, placed, more):
        G.after(placed)
        for c in range(ncol):
            slot_lanes[c % 8].start(G, lambda: g.indirect_dma_start(
                dest, IndirectOffsetOnAxis(ap=pos[:, c:c + 1], axis=0), XNt[:, c % T, :], None))
            more(c)

    zero_lane = Lane(nc, "slots_zeroed")
    zrow = view(C, tail, 2 * D)
    V.after(M.last, S.last)
    V.step(v.memset(zrow, 0.0))
    Y.after(V.last)
    for sx, n in zip(slot_x, (SLOTS0, SLOTS1)):
        for a in range(n):
            zero_lane.add(y.dma_start(sx[a * P:(a + 1) * P, :], zrow[:, 0:D]))

    def groups(n):
        return [(a, min(QT, n - a)) for a in range(0, n, QT)]

    def transpose_group(rows_of, a, n, banks, to, free, engines):
        M.after(*free)
        for k in range(KD):
            for j in range(n):
                M.do(m.transpose(banks[k][:, j * P:(j + 1) * P], rows_of(a + j)[:, k * P:(k + 1) * P], ident[:, :]))
        tr = M.last
        res = []
        for k in range(KD):
            q = engines[k % len(engines)]
            q.after(tr)
            if q is S:
                res.append(S.do(s.activation(to[:, k, 0:n * P], banks[k][:, 0:n * P], ACT.Copy)))
            else:
                res.append(V.do(v.tensor_copy(to[:, k, 0:n * P], banks[k][:, 0:n * P])))
        return res

    normed = layernorm()
    bcolw = bcol[:, 0:KH0]
    f0_lane.add(y.dma_start(bcolw, f0_b1.rearrange("(k p) -> p k", p=P), allow_slow_non_contiguous=True))
    wg0 = view(C, 57344, KH0 * 8).rearrange("p (k e) -> p k e", e=8)
    bg0 = view(C, 57344 + 256, 8)
    Y.after(V.last, zero_lane.ticket)
    f0_lane.add(y.dma_start(wg0, f0_wg.rearrange("(k p) e -> p k e", p=P)))
    f0_lane.add(y.dma_start(bg0, f0_bg.partition_broadcast(P)))
    bd = view(R, 8192, E0 * D)
    f0_lane.add(y.dma_start(bd, f0_bd.rearrange("e d -> (e d)").partition_broadcast(P)))

    def hidden(xt, ht, n, chunk, free, mms):
        res = []
        for c in range(KH0):
            b = bank[2 + c % 2]
            M.after(chunk.get(c % 2))
            for k in range(KD):
                M.do(m.matmul(b[:, 0:n * P], lhsT=W1a[:, k, c * P:(c + 1) * P], rhs=xt[:, k, 0:n * P],
                              start=k == 0, stop=k == KD - 1))
            S.after(M.last, *free)
            chunk[c % 2] = S.do(s.activation(ht[:, c, 0:n * P], b[:, 0:n * P], ACT.Gelu, bias=bcol[:, c:c + 1]))
            res.append(chunk[c % 2])
        return res

    XTa = [view(C, 4096 * b, KD * QT * P).rearrange("p (k n) -> p k n", k=KD) for b in range(2)]
    HTa = [view(C, 8192 + 16384 * b, KH0 * QT * P).rearrange("p (k n) -> p k n", k=KH0) for b in range(2)]
    M.after(f0_lane.ticket)
    S.after(f0_lane.ticket)
    V.after(f0_lane.ticket)
    chunk, xt_free, ht_free, tr_free, lg_free = {}, {}, {}, None, {}
    gs = groups(T)
    xt_ready = {}

    def logits_of(gi):
        a, n = gs[gi]
        for j in range(n):
            M.after(lg_free.get(j % 2))
            for c in range(KH0):
                M.do(m.matmul(bank[4 + j % 2][:, 0:8], lhsT=HTa[gi % 2][:, c, j * P:(j + 1) * P], rhs=wg0[:, c, :],
                              start=c == 0, stop=c == KH0 - 1))
            V.after(M.last)
            lg_free[j % 2] = V.do(v.tensor_tensor(logits[:, a + j, :], bank[4 + j % 2][:, 0:8], bg0, ALU.add))
        ht_free[gi] = M.last

    ht_ready = {}
    for gi, (a, n) in enumerate(gs):
        M.after(normed[a + n - 1])
        xt_ready[gi] = transpose_group(lambda t: XNt[:, t, :], a, n, bank[0:2], XTa[gi % 2],
                                       [xt_ready.get(gi - 1), xt_free.get(gi - 2)], [V])
        M.after(*xt_ready[gi])
        ht_ready[gi] = hidden(XTa[gi % 2], HTa[gi % 2], n, chunk, [ht_free.get(gi - 2)], None)
        xt_free[gi] = M.last
        if gi:
            M.after(*ht_ready[gi - 1])
            logits_of(gi - 1)
    M.after(*ht_ready[len(gs) - 1])
    logits_of(len(gs) - 1)
    Wd = view(C, 0, E0 * KH0 * D)
    wd_lane = Lane(nc, "experts_loaded")
    Y.after(M.last, V.last)
    for e in range(E0):
        wd_lane.add(y.dma_start(Wd[:, e * KH0 * D:(e + 1) * KH0 * D].rearrange("p (k n) -> p k n", k=KH0),
                                f0_wd[e].rearrange("(k p) n -> p k n", p=P)))
    V.after(V.last)
    red = view(wt, 0, T)
    V.step(v.tensor_reduce(red, logits, AX.X, ALU.max))
    V.step(v.tensor_tensor(probs, logits, red.unsqueeze(2).broadcast_to([P, T, 8]), ALU.subtract))
    S.after(V.last)
    V.after(S.do(s.activation(probs, probs, ACT.Exp)))
    V.step(v.tensor_reduce(red, probs, AX.X, ALU.add))
    V.step(v.reciprocal(red, red))
    V.step(v.tensor_tensor(probs, probs, red.unsqueeze(2).broadcast_to([P, T, 8]), ALU.mult))
    for t in range(T):
        V.do(v.max(best[:, t, :], probs[:, t, :]))
    V.after(V.last)
    for t in range(T):
        V.do(v.max_index(best_at[:, t, :].bitcast(U32), best[:, t, :], probs[:, t, :]))
    V.after(V.last)
    V.do(v.tensor_copy(gate[:, 0:T], best[:, :, 0]))
    V.step(v.tensor_copy(chosen[:, 0:T], best_at[:, :, 0]))
    placed = route(T, SLOTS0, KH0 * D)
    G.after(zero_lane.ticket, *normed)
    scatter_tokens(slot_x[0], T, placed, lambda c: None)
    scatter_more(300)

    W_ = XN
    def space(off, n, dt=F32):
        return view(W_, off, n, dt)

    xs = [space(4096 * b, QT * D).rearrange("p (t d) -> p t d", d=D) for b in range(2)]
    XTb = space(8192, KD * QT * P).rearrange("p (k n) -> p k n", k=KD)
    HTb = [space(12288 + 16384 * b, KH0 * QT * P).rearrange("p (k n) -> p k n", k=KH0) for b in range(2)]
    ys = [space(45056 + 1024 * b, D) for b in range(4)]
    xs_lane = [Lane(nc, f"slot_rows_loaded{b}") for b in range(2)]
    ys_lane = [Lane(nc, f"slot_out_stored{b}") for b in range(4)]
    gs = groups(SLOTS0)
    Y.after(*[l.ticket for l in slot_lanes])
    scattered0 = [l.ticket for l in slot_lanes]
    M.after(wd_lane.ticket)
    S.after(*scattered0)
    V.after(*scattered0)
    xs_ready, xs_free, ht_free, y_read = {}, {}, {}, {}

    def load_slots(gi):
        a, n = gs[gi]
        xs_ready[gi] = xs_lane[gi % 2].start(Y, lambda: y.dma_start(
            xs[gi % 2][:, 0:n, :], slot_x[0][a * P:(a + n) * P, :].rearrange("(t p) d -> p t d", p=P)), xs_free.get(gi - 2))

    load_slots(0)
    regs_m = regs_v = None
    xt_free_b, chunk = None, {}
    ht_ready = {}

    def experts0(gi):
        a, n = gs[gi]
        regs_m = reg_values(ENG.PE, texp[0:1, a:a + n], 7 * KH0 * D)
        regs_v = reg_values(ENG.DVE, texp[0:1, a:a + n], 7 * KH0 * D)
        for j in range(n):
            i = a + j
            M.after(y_read.get(i - 2))
            for c in range(KH0):
                M.do(m.matmul(bank[4 + i % 2][:, 0:D], lhsT=HTb[gi % 2][:, c, j * P:(j + 1) * P],
                              rhs=Wd[:, ds(regs_m[j] + c * D, D)], start=c == 0, stop=c == KH0 - 1))
            V.after(M.last, ys_lane[i % 4].ticket)
            y_read[i] = V.do(v.tensor_tensor(ys[i % 4], bank[4 + i % 2][:, 0:D], bd[:, ds(regs_v[j] // KH0, D)], ALU.add))
            ys_lane[i % 4].start(Y, lambda: y.dma_start(slot_y[0][i * P:(i + 1) * P, :], ys[i % 4]), y_read[i])
        ht_free[gi] = M.last

    for gi, (a, n) in enumerate(gs):
        if gi + 1 < len(gs):
            load_slots(gi + 1)
        M.after(xs_ready[gi])
        xt_ready = transpose_group(lambda t: xs[gi % 2][:, t, :], 0, n, bank[0:2], XTb, [xt_free_b], [V])
        xs_free[gi] = M.last
        M.after(*xt_ready)
        ht_ready[gi] = hidden(XTb, HTb[gi % 2], n, chunk, [ht_free.get(gi - 2)], None)
        xt_free_b = [M.last] + xt_ready
        V.after(M.last)
        if gi:
            M.after(*ht_ready[gi - 1])
            experts0(gi - 1)
    M.after(*ht_ready[len(gs) - 1])
    experts0(len(gs) - 1)
    ffn0_done = [V.last, M.last]

    comb_lanes = [Lane(nc, f"combine{b}") for b in range(8)]
    comb = [space(1024 * b, D) for b in range(8)]
    G.after(*ffn0_done, *[l.ticket for l in ys_lane])
    used = {}

    def combine(table, cols, finish):
        for n, c in enumerate(cols):
            t = c % T
            ready = comb_lanes[n % 8].start(G, lambda: g.indirect_dma_start(
                comb[n % 8], None, table, IndirectOffsetOnAxis(ap=pos[:, c:c + 1], axis=0)), used.get(n - 8))
            V.after(ready, used.get(n - 1))
            used[n] = V.do(v.scalar_tensor_tensor(X[:, t, :], comb[n % 8], gate[:, c:c + 1], X[:, t, :],
                                                  ALU.mult, ALU.add))
            finish(c)
        V.after(V.last)

    combine(slot_y[0], range(T), lambda c: None)
    scatter_more(EC)

    dm = view(wt, 0, T)
    V.step(v.tensor_scalar(dm, deg[:, :], 0.0, None, ALU.is_gt))
    V.step(v.tensor_scalar(deg[:, :], deg[:, :], 1e-30, None, ALU.max))
    S.after(V.last)
    V.after(S.do(s.activation(deg[:, :], deg[:, :], ACT.Sqrt)))
    V.step(v.reciprocal(deg[:, :], deg[:, :]))
    V.step(v.tensor_tensor(deg[:, :], deg[:, :], dm, ALU.mult))
    layernorm(deg, tab1, table_lane[1])
    V.after(V.last, *ffn0_done)
    V.step(v.tensor_copy(acc[:, :, 0:D], XNt))
    make_items(1)
    V.after(V.last, M.last)
    aggregate(tab1, D, True, [V.last, table_lane[1].ticket], lambda i: None)
    acc_done = V.last

    gw_lane = Lane(nc, "gcn_weights_loaded")
    gcn_w = [view(rec1[:, :, :].rearrange("p e r -> p (e r)"),
                  2048 * n, KD * D).rearrange("p (k n) -> p k n", k=KD) for n in range(3)]
    b2_b = view(rec1[:, :, :].rearrange("p e r -> p (e r)"), 6144, D)
    Y.after(*[l.ticket for l in scatter_lanes], M.last, V.last)
    for w_sb, w in zip(gcn_w, (g1_w, g1_w1, g1_w2)):
        gw_lane.add(y.dma_start(w_sb, w.rearrange("(k p) n -> p k n", p=P)))
    gw_lane.add(y.dma_start(b2_b, g1_b2.partition_broadcast(P)))
    gw_lane.add(y.dma_start(bcol[:, 8:10], g1_b.rearrange("(k p) -> p k", p=P), allow_slow_non_contiguous=True))
    gw_lane.add(y.dma_start(bcol[:, 10:12], g1_b1.rearrange("(k p) -> p k", p=P), allow_slow_non_contiguous=True))
    f1w_lane = Lane(nc, "ffn1_gate_loaded")
    wg1 = view(R, 0, KD * 8).rearrange("p (k e) -> p k e", e=8)
    bg1 = view(R, 64, 8)
    bias1 = view(R, 96, 8)
    for q in (M, S, V):
        q.after(gw_lane.ticket)
    aT = [space(4096 * b, KD * QT * P).rearrange("p (k n) -> p k n", k=KD) for b in range(6)]
    gs = groups(T)
    fin, tr_copied, hb = {}, {}, {}
    for t in range(T):
        V.do(v.tensor_scalar(acc[:, t, 0:D], acc[:, t, 0:D], deg[:, t:t + 1], None, ALU.mult))
    M.after(V.last)
    for gi, (a, n) in enumerate(gs):
        b3 = 3 * (gi % 2)
        tr = transpose_group(lambda t: acc[:, t, 0:D], a, n, bank[0:2], aT[b3], [tr_copied.get(gi - 1), fin.get(gi - 2)], [V])
        tr_copied[gi] = tr
        M.after(*tr)
        prev = aT[b3]
        for layer, (w_sb, col, fn) in enumerate(((gcn_w[0], 8, ACT.Identity), (gcn_w[1], 10, ACT.Relu))):
            nxt = aT[b3 + 1 + layer]
            outs = []
            for c in range(KD):
                M.after(hb.get(c))
                for k in range(KD):
                    M.do(m.matmul(bank[2 + c][:, 0:n * P], lhsT=w_sb[:, k, c * P:(c + 1) * P], rhs=prev[:, k, 0:n * P],
                                  start=k == 0, stop=k == KD - 1))
                S.after(M.last, fin.get(gi - 2))
                hb[c] = S.do(s.activation(nxt[:, c, 0:n * P], bank[2 + c][:, 0:n * P], fn, bias=bcol[:, col + c:col + c + 1]))
                outs.append(hb[c])
            M.after(*outs)
            prev = nxt
        for j in range(n):
            t = a + j
            M.after(y_read.get(("g", t - 2)))
            for k in range(KD):
                M.do(m.matmul(bank[4 + t % 2][:, 0:D], lhsT=prev[:, k, j * P:(j + 1) * P], rhs=gcn_w[2][:, k, :],
                              start=k == 0, stop=k == KD - 1))
            V.after(M.last)
            y_read[("g", t)] = V.do(v.tensor_tensor(X[:, t, :], bank[4 + t % 2][:, 0:D], X[:, t, :], ALU.add))
            V.after(V.last)
            V.do(v.tensor_tensor(X[:, t, :], X[:, t, :], b2_b, ALU.add))
        fin[gi] = M.last
    V.after(V.last, M.last, S.last)
    gcn_done = [V.last, M.last, S.last]

    Y.after(*gcn_done)
    W1b = view(C, 0, E1 * KD * HID1)
    W2b = view(C, 4 * E1 * KD * HID1, E1 * KH1 * D)
    f1w_lane.add(y.dma_start(wg1, f1_wg.rearrange("(k p) e -> p k e", p=P)))
    f1w_lane.add(y.dma_start(bg1, f1_bg.partition_broadcast(P)))
    f1w_lane.add(y.dma_start(bias1, f1_bias.partition_broadcast(P)))
    ew_lane = Lane(nc, "ffn1_experts_loaded")
    for e in range(E1):
        ew_lane.add(y.dma_start(W1b[:, e * KD * HID1:(e + 1) * KD * HID1].rearrange("p (k n) -> p k n", k=KD),
                                f1_w1[e].rearrange("(k p) n -> p k n", p=P)))
        ew_lane.add(y.dma_start(W2b[:, e * KH1 * D:(e + 1) * KH1 * D].rearrange("p (k n) -> p k n", k=KH1),
                                f1_w2[e].rearrange("(k p) n -> p k n", p=P)))
    b2e = view(rec1[:, :, :].rearrange("p e r -> p (e r)"), 0, E1 * D)
    ew_lane.add(y.dma_start(b2e, f1_b2.rearrange("e d -> (e d)").partition_broadcast(P)))
    normed = layernorm()
    M.after(f1w_lane.ticket)
    V.after(f1w_lane.ticket)
    xt2 = view(R, 1024, 2 * D).rearrange("p (n a) -> p n a", n=2)
    copied, prod, rd = {}, {}, {}
    for t in range(T + 1):
        if t < T:
            tr = transpose_rows(XNt[:, t, :], bank[t % 2], 0, copied.get(t - 2), normed[t])
            S.after(tr, prod.get(t - 2))
            copied[t] = S.do(s.activation(xt2[:, t % 2, :], bank[t % 2][:, 0:D], ACT.Copy))
        if t:
            u = t - 1
            M.after(copied[u], rd.get(u - 2))
            for k in range(KD):
                prod[u] = M.do(m.matmul(bank[2 + u % 2][:, 0:8], lhsT=xt2[:, u % 2, k * P:(k + 1) * P], rhs=wg1[:, k, :],
                                        start=k == 0, stop=k == KD - 1))
            V.after(prod[u])
            rd[u] = V.do(v.tensor_tensor(logits[:, u, :], bank[2 + u % 2][:, 0:8], bg1, ALU.add))
    V.after(V.last)
    V.step(v.tensor_tensor(logits, logits, bias1.unsqueeze(1).broadcast_to([P, T, 8]), ALU.add))
    for t in range(T):
        V.do(v.max(best[:, t, :], logits[:, t, :]))
    V.after(V.last)
    for t in range(T):
        V.do(v.max_index(best_at[:, t, :].bitcast(U32), best[:, t, :], logits[:, t, :]))
    V.after(V.last)
    V.step(v.tensor_tensor(gate[:, T:2 * T], best[:, :, 1], best[:, :, 0], ALU.subtract))
    S.after(V.last)
    V.after(S.do(s.activation(gate[:, T:2 * T], gate[:, T:2 * T], ACT.Exp)))
    V.step(v.tensor_scalar(gate[:, 0:T], gate[:, T:2 * T], 1.0, None, ALU.add))
    V.step(v.reciprocal(gate[:, 0:T], gate[:, 0:T]))
    V.step(v.tensor_tensor(gate[:, T:2 * T], gate[:, T:2 * T], gate[:, 0:T], ALU.mult))
    V.do(v.tensor_copy(chosen[:, 0:T], best_at[:, :, 0]))
    V.step(v.tensor_copy(chosen[:, T:2 * T], best_at[:, :, 1]))
    placed = route(2 * T, SLOTS1, KD * HID1)
    b1e = view(R, 0, E1 * HID1)
    Y.after(M.last, S.last, V.last)
    ew_lane.add(y.dma_start(b1e, f1_b1.rearrange("e h -> (e h)").partition_broadcast(P)))
    scatter_tokens(slot_x[1], 2 * T, placed, lambda c: None)

    scattered1 = [l.ticket for l in slot_lanes]
    for q in (Y, V, S, M):
        q.after(*scattered1)
    for q in (V, M, S):
        q.after(ew_lane.ticket)
    NB = 4
    xs1 = [space(1024 * b, D) for b in range(NB)]
    xT1 = [space(4096 + 1024 * b, D) for b in range(2)]
    h1 = [space(6144 + 2048 * b, HID1) for b in range(2)]
    hT1 = [space(10240 + 2048 * b, HID1) for b in range(2)]
    ys1 = [space(14336 + 1024 * b, D) for b in range(4)]
    xs1_lane = [Lane(nc, f"slot_rows1_loaded{b}") for b in range(NB)]
    ys1_lane = [Lane(nc, f"slot_out1_stored{b}") for b in range(4)]
    xs_ready, xs_free = {}, {}
    xT_ready, xT_free, h_ready, h_free, hT_ready, hT_free, y_read = {}, {}, {}, {}, {}, {}, {}
    regs = {}

    def load1(i):
        if i < SLOTS1:
            xs_ready[i] = xs1_lane[i % NB].start(Y, lambda: y.dma_start(
                xs1[i % NB], slot_x[1][i * P:(i + 1) * P, :]), xs_free.get(i - NB))

    for i in range(3):
        load1(i)
    for i in range(SLOTS1 + 2):
        load1(i + 3)
        if i < SLOTS1:
            xs_free[i] = transpose_rows(xs1[i % NB], bank[0], 0, xs_ready[i], xT_ready.get(i - 1))
            S.after(xs_free[i], h_ready.get(i - 2) and regs[("m1", i - 2)])
            xT_ready[i] = S.do(s.activation(xT1[i % 2], bank[0][:, 0:D], ACT.Copy))
            if i % 4 == 0:
                n = min(4, SLOTS1 - i)
                rm = reg_values(ENG.PE, texp[0:1, i:i + n], 7 * KD * HID1)
            regs[i] = rm[i % 4]
        if 0 <= i - 1 < SLOTS1:
            u = i - 1
            M.after(h_ready[u], hT_ready.get(u - 1))
            for c in range(KH1):
                M.do(m.transpose(bank[4][:, c * P:(c + 1) * P], h1[u % 2][:, c * P:(c + 1) * P], ident[:, :]))
            h_free[u] = M.last
            S.after(M.last, hT_free.get(u - 2))
            hT_ready[u] = S.do(s.activation(hT1[u % 2], bank[4][:, :], ACT.Relu))
        if i < SLOTS1:
            M.after(xT_ready[i], h_ready.get(i - 2))
            for k in range(KD):
                M.do(m.matmul(bank[2 + i % 2][:, :], lhsT=xT1[i % 2][:, k * P:(k + 1) * P],
                              rhs=W1b[:, ds(regs[i] + k * HID1, HID1)], start=k == 0, stop=k == KD - 1))
            regs[("m1", i)] = M.last
            if i % 4 == 0:
                rv = reg_values(ENG.DVE, texp[0:1, i:i + n], 7 * KD * HID1)
            V.after(M.last, h_free.get(i - 2))
            h_ready[i] = V.do(v.tensor_tensor(h1[i % 2], bank[2 + i % 2][:, :], b1e[:, ds(rv[i % 4] // KD, HID1)], ALU.add))
            regs[("v", i)] = rv[i % 4]
        if 0 <= i - 1 < SLOTS1:
            u = i - 1
            M.after(hT_ready[u], y_read.get(u - 2))
            for c in range(KH1):
                M.do(m.matmul(bank[5 + u % 2][:, 0:D], lhsT=hT1[u % 2][:, c * P:(c + 1) * P],
                              rhs=W2b[:, ds(regs[u] + c * D, D)], start=c == 0, stop=c == KH1 - 1))
            hT_free[u] = M.last
            V.after(M.last, ys1_lane[u % 4].ticket)
            y_read[u] = V.do(v.tensor_tensor(ys1[u % 4], bank[5 + u % 2][:, 0:D], b2e[:, ds(regs[("v", u)] // KH1, D)], ALU.add))
            ys1_lane[u % 4].start(Y, lambda: y.dma_start(slot_y[1][u * P:(u + 1) * P, :], ys1[u % 4]), y_read[u])

    G.after(V.last, M.last, S.last, *[l.ticket for l in ys1_lane])
    out_lane = Lane(nc, "out_stored")

    def store(c):
        if c >= T:
            t = c - T
            n = P if t < T - 1 else LAST
            Y.after(V.last)
            out_lane.add(y.dma_start(out[t * P:t * P + n, :], X[0:n, t, :]))

    used.clear()
    combine(slot_y[1], [c for t in range(T) for c in (t, T + t)], store)
    Y.after(out_lane.ticket)


_INS = ["x", "src", "dst", "edge_weight", "L0_gnn_W_src", "L0_gnn_gamma", "L0_gnn_beta", "L0_ffn_W1", "L0_ffn_b1",
        "L0_ffn_Wg", "L0_ffn_bg", "L0_ffn_Wd", "L0_ffn_bd", "L1_gnn_W", "L1_gnn_b", "L1_gnn_W1", "L1_gnn_b1",
        "L1_gnn_W2", "L1_gnn_b2", "L1_ffn_Wg", "L1_ffn_bg", "L1_ffn_bias", "L1_ffn_W1", "L1_ffn_b1", "L1_ffn_W2",
        "L1_ffn_b2"]


def kernel(**inputs):
    import concourse.bacc as bacc
    from concourse.bass_utils import run_bass_kernel_spmd

    nc = bacc.Bacc("TRN2", target_bir_lowering=False, num_devices=1)
    arrays, args = {}, []
    for name in _INS:
        a = np.ascontiguousarray(inputs[name])
        arrays[f"in_{name}"] = a
        args.append(nc.dram_tensor(f"in_{name}", a.shape, mybir.dt.from_np(a.dtype), kind="ExternalInput").ap())
    args.append(nc.dram_tensor("out_rows", (N, D), F32, kind="ExternalOutput").ap())
    build(nc, *args)
    r = run_bass_kernel_spmd(nc, [arrays], core_ids=[0])
    return r.results[0]["out_rows"]
```

```python
import numpy as np

import concourse.bass as bass
from concourse import mybir
from concourse.bass import IndirectOffsetOnAxis, ds

F32 = mybir.dt.float32
I32 = mybir.dt.int32
U16 = mybir.dt.uint16
U32 = mybir.dt.uint32
BF16 = mybir.dt.bfloat16
ALU = mybir.AluOpType
ACT = mybir.ActivationFunctionType
AX = mybir.AxisListType
ENG = mybir.EngineType

P = 128
N = 6250
D = 256
T = -(-N // P)
LAST = N - (T - 1) * P
KD = D // P
NE = 100000
EP, EC = 125, 800
CH = -(-NE // P)
ITEMS = CH + T - 1
IJ = -(-ITEMS // P)
AW = D + 1
REC = 3
HID0, E0 = 1024, 8
KH0 = HID0 // P
HID1, E1 = 512, 8
KH1 = HID1 // P
SLOTS0 = (T * P + E0 * (P - 1)) // P
SLOTS1 = (2 * T * P + E1 * (P - 1)) // P
LN_EPS = 1e-5
BN_EPS = 1e-5
BEFORE_SLOTS = 550
PLACE = 14
RING = 12
G7 = 7
G2 = 2
PER_TILE = -(-ITEMS // T)
MARGIN = 24
STEP = 3


class Queue:

    def __init__(self, nc, engine, name):
        self.e = engine
        self.done = nc.alloc_semaphore(name)
        self.count = 0
        self.last = None
        self.met = {}

    def after(self, *tickets):
        for t in tickets:
            if t is None:
                continue
            if isinstance(t, list):
                self.after(*t)
                continue
            sem, value = t
            if self.met.get(id(sem), 0) < value:
                self.e.wait_ge(sem, value)
                self.met[id(sem)] = value

    def state(self):
        return self.count, self.last, dict(self.met)

    def restore(self, state):
        self.count, self.last, self.met = state[0], state[1], dict(state[2])

    def value(self):
        return self.count

    def forget_waits(self, state):
        self.met = dict(state[2])

    def do(self, instruction):
        instruction.then_inc(self.done, 1)
        self.count += 1
        self.last = (self.done, self.count)
        return self.last

    def step(self, instruction):
        t = self.do(instruction)
        self.after(t)
        return t


class Lane:

    def __init__(self, nc, name):
        self.sem = nc.alloc_semaphore(name)
        self.total = 0

    @property
    def ticket(self):
        return (self.sem, self.total) if self.total else None

    def state(self):
        return (self.total,)

    def restore(self, state):
        self.total = state[0]

    def value(self):
        return self.total

    def forget_waits(self, state):
        pass

    def start(self, queue, make, *tickets):
        queue.after(*tickets, self.ticket)
        return self.add(make())

    def add(self, instruction):
        instruction.then_inc(self.sem, 16)
        self.total += 16
        return self.ticket


def build(nc, x, src, dst, edge_weight, g0_w, g0_gamma, g0_beta, f0_w1, f0_b1, f0_wg, f0_bg, f0_wd,
          f0_bd, g1_w, g1_b, g1_w1, g1_b1, g1_w2, g1_b2, f1_wg, f1_bg, f1_bias, f1_w1, f1_b1, f1_w2,
          f1_b2, out):
    V = Queue(nc, nc.vector, "vector_done")
    S = Queue(nc, nc.scalar, "scalar_done")
    M = Queue(nc, nc.tensor, "tensor_done")
    G = Queue(nc, nc.gpsimd, "gpsimd_done")
    Y = Queue(nc, nc.sync, "sync_done")
    v, s, m, g, y = nc.vector, nc.scalar, nc.tensor, nc.gpsimd, nc.sync

    def region(name, nbytes):
        return nc.alloc_sbuf_tensor(name, [P, nbytes // 4], F32)

    def view(reg, off, n, dt=F32, parts=P):
        size = 2 if dt in (BF16, U16) else 4
        v32 = reg[0:parts, off // 4:(off + n * size) // 4]
        return v32 if dt == F32 else v32.bitcast(dt)

    def small(name, n, dt=F32):
        return nc.alloc_sbuf_tensor(name, [P, n], dt)

    def reg_values(engine, ap, most):
        return nc.values_load_multi_w_load_instructions(
            ap, engines=[engine], min_val=0, max_val=most,
            skip_runtime_bounds_check_because="clamped to the last tile or expert where it is computed")[1]

    X = nc.alloc_sbuf_tensor("x_rows", [P, T, D], F32)
    XN = nc.alloc_sbuf_tensor("normed", [P, T * D], F32)
    XNt = XN[:, :].rearrange("p (t d) -> p t d", d=D)
    C = region("acc_or_weights", 4 * E0 * KH0 * D)
    R = region("ring_or_weights", 16384)
    rec1 = nc.alloc_sbuf_tensor("edge_records_by_src", [P, EC, REC], F32)
    posr = region("edge_positions", 4 * EC)
    dloc = small("item_local_node", IJ * P)
    gidx = small("item_other_node", IJ * P, I32)
    wt = small("item_weight", IJ * P)
    iota = small("iota_row", P)
    ident = small("identity", P)
    ones = small("ones", P)
    ones_last = small("ones_of_last_tile", P)
    tri = small("earlier_partitions", P)
    mv = nc.alloc_sbuf_tensor("mean_var", [P, T, 2], F32)
    rstd = small("rstd", T)
    deg = small("node_degree", T)
    stats = nc.alloc_sbuf_tensor("bn_stats_ring", [P, 4, 6], F32)
    toff = small("item_acc_offset", P, I32)
    pos = small("token_slot", 2 * T, I32)
    gate = small("token_gate", 2 * T)
    texp = small("slot_expert_offset", SLOTS1, I32)
    row_id = small("token_row_plus_one", 2 * T)
    tot = small("tile_edges", T)
    incl = small("tile_edge_ends", T)
    offs = small("tile_edge_offsets", T)
    unordered = small("unordered_partitions", 1, I32)
    late = small("is_late", 1, I32)
    small_f = small("has_fall", 1)
    bcol = small("bias_columns", 4)
    bank = [nc.alloc_psum_tensor(f"bank{k}", [P, 512], F32) for k in range(8)]

    rec_d = [nc.dram_tensor(f"ordered_edges{k}", (CH * P, REC), F32, kind="Internal").ap() for k in range(2)]
    tab = nc.dram_tensor("gather_table", (T * P, D), F32, kind="Internal").ap()
    tab1 = nc.dram_tensor("gather_table1", (T * P, D), F32, kind="Internal").ap()
    hid_d = nc.dram_tensor("hidden_rows", (T * P, HID0), F32, kind="Internal").ap()
    tab2 = nc.dram_tensor("gather_table2", (T * P, D), F32, kind="Internal").ap()
    tok_y = [nc.dram_tensor(f"expert_out{k}", (n * T * P, D), F32, kind="Internal").ap() for k, n in enumerate((1, 2))]

    raw_src = view(C, 0, EC, I32, EP)
    raw_dst = view(C, 3200, EC, I32, EP)
    raw_w = view(C, 6400, EC, F32, EP)
    rec0 = view(C, 9600, EC * REC).rearrange("p (e r) -> p e r", r=REC)
    idx0 = view(C, 19200, EC, I32)
    raw_next = view(C, 27200, EC, I32, EP)
    falls = view(C, 30400, EC)
    int_tmp = view(C, 22400, EC, I32)
    kt0 = view(C, 25600, EC, BF16)
    acc = view(C, 0, T * AW).rearrange("p (t a) -> p t a", a=AW)
    tail = 4 * T * AW
    kt1 = view(C, tail, EC, BF16)
    mask_e = view(C, tail + 1600, EC, BF16)
    ones_e = view(C, tail + 3200, EC, BF16)
    scan_e = view(C, tail + 4800, EC)
    pos_e = view(C, tail + 8000, EC)
    neg_lo = view(C, tail + 11200, EC)
    kt1f = view(posr, 0, EC)
    idx1 = view(posr, 0, EC, I32)

    load_e, load_x, load_c = Lane(nc, "edges_loaded"), Lane(nc, "x_loaded"), Lane(nc, "consts_loaded")
    load_e.add(y.dma_start(raw_dst, dst.rearrange("(p e) -> p e", e=EC)))
    load_e.add(y.dma_start(raw_src, src.rearrange("(p e) -> p e", e=EC)))
    load_e.add(y.dma_start(raw_w, edge_weight.rearrange("(p e) -> p e", e=EC)))
    V.do(v.memset(raw_next, 1 << 20))
    Y.after(V.last)
    body = (EP - 1) * EC
    load_e.add(y.dma_start(raw_next[0:EP - 1], dst[1:body + 1].rearrange("(p e) -> p e", e=EC)))
    load_e.add(y.dma_start(raw_next[EP - 1:EP, 0:EC - 1], dst[body + 1:NE].rearrange("(p e) -> p e", p=1)))
    V.do(v.memset(X[:, T - 1, :], 0.0))
    for a in range(0, T - 1, 8):
        load_x.add(s.dma_start(X[:, a:a + 8, :], x[a * P:(a + 8) * P, :].rearrange("(t p) d -> p t d", p=P)))
    S.after(V.last)
    load_x.add(s.dma_start(X[0:LAST, T - 1, :], x[(T - 1) * P:N, :]))

    V.do(v.memset(ones[:, :], 1.0))
    V.do(v.memset(ident[:, :], 0.0))
    G.do(g.iota(iota[:, :], pattern=[[1, P]], base=0, channel_multiplier=0, allow_small_or_imprecise_dtypes=True))
    G.do(g.iota(row_id[:, :], pattern=[[P, 2 * T]], base=1, channel_multiplier=1, allow_small_or_imprecise_dtypes=True))
    G.after(V.last)
    G.do(g.affine_select(out=tri[:, :], in_=ones[:, :], compare_op=ALU.is_gt, fill=0.0, base=0,
                         pattern=[[1, P]], channel_multiplier=-1))
    G.do(g.affine_select(out=ones_last[:, :], in_=ones[:, :], compare_op=ALU.is_gt, fill=0.0, base=LAST,
                         pattern=[[0, P]], channel_multiplier=-1))
    consts = G.do(g.affine_select(out=ident[:, :], in_=ident[:, :], compare_op=ALU.not_equal, fill=1.0, base=0,
                                  pattern=[[-1, P]], channel_multiplier=1))
    for q in (V, S, M):
        q.after(consts)

    V.after(load_e.ticket)
    V.do(v.memset(rec0[:, :, :], -1.0))
    V.do(v.memset(rec1[:, :, :], -1.0))
    V.after(V.last)
    for rec, key, other, kt in ((rec0, raw_dst, raw_src, kt0), (rec1[:, :, :], raw_src, raw_dst, kt1)):
        V.do(v.tensor_copy(rec[0:EP, :, 0], key))
        V.do(v.tensor_copy(rec[0:EP, :, 1], other))
        V.do(v.tensor_copy(rec[0:EP, :, 2], raw_w))
        V.step(v.tensor_scalar(int_tmp[0:EP], key, 7, None, ALU.arith_shift_right))
        V.step(v.tensor_copy(kt[0:EP], int_tmp[0:EP]))
    V.step(v.tensor_copy(scan_e[0:EP], int_tmp[0:EP]))
    V.step(v.scalar_tensor_tensor(neg_lo[0:EP], scan_e[0:EP], float(P), rec1[0:EP, :, 0], ALU.mult, ALU.subtract))
    V.do(v.tensor_copy(kt1f[0:EP], scan_e[0:EP]))
    V.step(v.memset(ones_e, 1.0))

    count_scratch = [mask_e, scan_e.bitcast(BF16)[:, 0:EC]]

    counted = {}

    def count_tile(kt, k, t):
        V.after(counted.get(t - 2))
        counted[t] = V.do(v.tensor_scalar(count_scratch[t % 2][0:EP], kt[0:EP], float(t), None, ALU.is_equal,
                                          ALU.add, accum_out=offs[0:EP, t:t + 1]))

    def count_ends(k, all_bank, before_bank):
        V.after(V.last)
        M.after(V.last)
        M.do(m.matmul(all_bank[:, 0:T], lhsT=ones[0:EP, :], rhs=offs[0:EP, :], start=True, stop=True))
        M.do(m.matmul(before_bank[:, 0:T], lhsT=tri[0:EP, :], rhs=offs[0:EP, :], start=True, stop=True))
        V.after(M.last)
        V.step(v.tensor_copy(tot[:, :], all_bank[:, 0:T]))
        V.step(v.tensor_tensor_scan(incl[:, :], ones[:, 0:T], tot[:, :], 0.0, ALU.mult, ALU.add))
        V.step(v.scalar_tensor_tensor(offs[:, :], before_bank[:, 0:T], -1.0, incl[:, :], ALU.add, ALU.add))
        V.step(v.tensor_tensor(offs[:, :], offs[:, :], tot[:, :], ALU.subtract))
        counted.clear()

    def place_edges(q, kt, k, t):
        q.step(v.tensor_scalar(mask_e[0:EP], kt[0:EP], float(t), None, ALU.is_equal))
        q.step(v.tensor_tensor_scan(scan_e[0:EP], ones_e[0:EP], mask_e[0:EP], offs[0:EP, t:t + 1],
                                    ALU.mult, ALU.add))
        q.step(v.copy_predicated(pos_e[0:EP], mask_e[0:EP].bitcast(U16), scan_e[0:EP]))

    pad_lane = Lane(nc, "edge_padding")

    def scatter_edges(q, lanes, k, rec, idx, c, *tickets):
        return lanes[c % 8].start(
            q, lambda: g.indirect_dma_start(rec_d[k], IndirectOffsetOnAxis(ap=idx[0:EP, c:c + 1], axis=0),
                                            rec[0:EP, c, :], None), *tickets)

    npad = CH * P - NE
    neg = view(R, 0, REC)
    V.do(v.memset(neg, -1.0))
    Y.after(V.last)
    for k in range(2):
        pad_lane.add(y.dma_start(rec_d[k][NE:CH * P, :], neg[0:npad, :]))

    for t in range(T):
        count_tile(kt0, 0, t)
    count_ends(0, bank[0], bank[1])

    V.step(v.tensor_tensor(falls[0:EP], raw_dst, raw_next, ALU.is_gt))
    V.step(v.tensor_reduce(small_f[0:EP, :], falls[0:EP], AX.X, ALU.max))
    M.after(V.last)
    M.do(m.matmul(bank[2][:, 0:1], lhsT=ones[0:EP, :], rhs=small_f[0:EP, :], start=True, stop=True))
    V.after(M.last)
    counted0 = V.step(v.tensor_copy(unordered[:, :], bank[2][:, 0:1]))

    VS = Queue(nc, nc.vector, "sort_vector_done")
    GS = Queue(nc, nc.gpsimd, "sort_gpsimd_done")
    sort_lanes = [Lane(nc, f"sort_scatter{k}") for k in range(8)]
    copy_lane = Lane(nc, "records_copied")
    with nc.Block() as block:
        @block.vector
        def _(e):
            e.wait_ge(*counted0)
            flag = reg_values(ENG.DVE, unordered[0:1, 0:1], P)[0]
            with e.If(flag > 0):
                for t in range(T):
                    place_edges(VS, kt0, 0, t)
                VS.step(v.tensor_copy(idx0[0:EP], pos_e[0:EP]))

        @block.gpsimd
        def _(e):
            e.wait_ge(*counted0)
            flag = reg_values(ENG.Pool, unordered[0:1, 0:1], P)[0]
            with e.If(flag > 0):
                for c in range(EC):
                    scatter_edges(GS, sort_lanes, 0, rec0, idx0, c, VS.last)
                GS.after(*[l.ticket for l in sort_lanes])
            with e.Else():
                copy_lane.add(g.dma_start(rec_d[0][0:NE, :].rearrange("(p e) r -> p (e r)", e=EC),
                                          rec0[0:EP].rearrange("p e r -> p (e r)")))
                e.wait_ge(*copy_lane.ticket)

    table_lane = [Lane(nc, f"table_written{k}") for k in range(2)]

    def norm_stats(a, b, scale=None):
        for t in range(a, b + 1):
            if t < b:
                V.after(read_stats.get(t % 4))
                stat = V.do(v.bn_stats(stats[:, t % 4, :], X[:, t, :]))
            if t > a:
                V.after(wrote_stats)
                read_stats[(t - 1) % 4] = V.do(v.bn_aggr(mv[:, t - 1, :], stats[:, (t - 1) % 4, :]))
            wrote_stats = stat
        V.after(V.last)
        r = rstd[:, a:b]
        S.after(V.step(v.tensor_scalar(r, mv[:, a:b, 1], LN_EPS, None, ALU.add)))
        rooted = S.do(s.activation(r, r, ACT.Sqrt))
        return rooted, a, b, scale

    def norm_finish(stage):
        rooted, a, b, scale = stage
        V.after(rooted)
        V.step(v.reciprocal(rstd[:, a:b], rstd[:, a:b]))
        if scale is not None:
            V.step(v.tensor_tensor(rstd[:, a:b], rstd[:, a:b], scale[:, a:b], ALU.mult))

    def norm_apply(t, to):
        return V.do(v.tensor_scalar(to, X[:, t, :], mv[:, t, 0:1], rstd[:, t:t + 1], ALU.subtract, ALU.mult))

    read_stats = {}

    def norm_tiles(to, scale, table, lane, before):
        stage = {}
        for a in range(0, T + G7, G7):
            if a < T:
                before(a)
                stage[a] = norm_stats(a, a + G7, scale)
            if a:
                norm_finish(stage[a - G7])
                for t in range(a - G7, a):
                    norm_apply(t, to[:, t, 0:D])
                Y.after(V.last)
                lane.add(y.dma_start(table[(a - G7) * P:a * P, :].rearrange("(t p) d -> p t d", p=P),
                                     to[:, a - G7:a, 0:D]))

    V.after(load_x.ticket)
    norm_tiles(XNt, None, tab, table_lane[0], lambda a: None)

    run_lane = Lane(nc, "runs_gathered")

    def make_items(k, ordered):
        a = 4 * 2688
        runs = view(R, 0, IJ * P * REC).rearrange("p (j e r) -> p j e r", j=IJ, r=REC)
        tmp = view(R, a, IJ * T).rearrange("p (j t) -> p j t", t=T)
        o = a + 4 * IJ * T
        i_first, i_int, i_end, kcount, shift = [view(R, o + 196 * n, T, I32 if n == 1 else F32) for n in range(5)]
        o += 196 * 5
        item, ti, cf, tb = [view(R, o + 28 * n, IJ) for n in range(4)]
        ci = view(R, o + 28 * 4, IJ, I32)
        G.after(V.last)
        V.after(G.do(g.iota(item, pattern=[[P, IJ]], base=0, channel_multiplier=1, allow_small_or_imprecise_dtypes=True)))
        V.step(v.tensor_tensor(i_int, incl[:, :], tot[:, :], ALU.subtract))
        V.step(v.tensor_scalar(i_int, i_int, 7, None, ALU.arith_shift_right))
        V.step(v.tensor_copy(i_first, i_int))
        V.step(v.tensor_scalar(i_int, incl[:, :], float(P - 1), None, ALU.add))
        V.step(v.tensor_scalar(i_int, i_int, 7, None, ALU.arith_shift_right))
        V.step(v.tensor_tensor(kcount, i_int, i_first, ALU.subtract))
        V.step(v.scalar_tensor_tensor(kcount, tot[:, :], 0.0, kcount, ALU.is_gt, ALU.mult))
        V.step(v.tensor_tensor_scan(i_end, ones[:, 0:T], kcount, 0.0, ALU.mult, ALU.add))
        V.step(v.tensor_tensor(shift, i_first, i_end, ALU.subtract))
        V.step(v.tensor_tensor(shift, shift, kcount, ALU.add))
        V.step(v.tensor_scalar(i_int.bitcast(F32), iota[:, 0:T], float(PER_TILE), float(PER_TILE + MARGIN),
                               ALU.mult, ALU.add))
        V.step(v.tensor_tensor(i_int.bitcast(F32), i_end, i_int.bitcast(F32), ALU.is_gt))
        V.step(v.tensor_reduce(late[:, :], i_int.bitcast(F32), AX.X, ALU.max))
        V.step(v.tensor_tensor(tmp, i_end.unsqueeze(1).broadcast_to([P, IJ, T]),
                               item.unsqueeze(2).broadcast_to([P, IJ, T]), ALU.is_le))
        V.step(v.tensor_reduce(ti, tmp, AX.X, ALU.add))
        V.step(v.tensor_tensor(tmp, iota[:, 0:T].unsqueeze(1).broadcast_to([P, IJ, T]),
                               ti.unsqueeze(2).broadcast_to([P, IJ, T]), ALU.is_equal))
        V.step(v.tensor_tensor(tmp, tmp, shift.unsqueeze(1).broadcast_to([P, IJ, T]), ALU.mult))
        V.step(v.tensor_reduce(cf, tmp, AX.X, ALU.add))
        V.step(v.tensor_tensor(cf, cf, item, ALU.add))
        V.step(v.tensor_scalar(ci, cf, float(CH - 1), 0.0, ALU.min, ALU.max))
        runs_known = V.last
        V.step(v.tensor_scalar(tb, ti, float(P), None, ALU.mult))
        V.step(v.tensor_scalar(cf, ti, float(T - 1), float(AW), ALU.min, ALU.mult))
        M.after(V.last)
        M.do(m.transpose(bank[0][0:IJ, 0:P], cf, ident[:, :]))
        V.after(M.last)
        V.step(v.tensor_copy(toff[0:IJ, :], bank[0][0:IJ, 0:P]))
        G.after(runs_known, pad_lane.ticket, *ordered)
        by_run = rec_d[k].rearrange("(c e) r -> c (e r)", e=P)
        for j in range(IJ):
            run_lane.add(g.indirect_dma_start(view(R, j * P * REC * 4, P * REC), None, by_run,
                                              IndirectOffsetOnAxis(ap=ci[:, j:j + 1], axis=0)))
        V.after(run_lane.ticket)
        for j in range(IJ):
            V.do(v.tensor_scalar(runs[:, j, :, 0], runs[:, j, :, 0], tb[:, j:j + 1], None, ALU.subtract))
        M.after(V.last)
        copied = {}
        for j in range(IJ):
            M.after(copied.get(j - 4))
            for f in range(REC):
                M.do(m.transpose(bank[j % 4][:, f * P:(f + 1) * P], runs[:, j, :, f], ident[:, :]))
            V.after(M.last)
            for f, to in enumerate((dloc, gidx, wt)):
                copied[j] = V.do(v.tensor_copy(to[:, j * P:(j + 1) * P], bank[j % 4][:, f * P:(f + 1) * P]))
            if j == IJ - 1:
                V.after(V.last)
        V.step(v.tensor_scalar(gidx[:, :], gidx[:, :], 0.0, None, ALU.max))

    make_items(0, [])

    scatter_lanes = [Lane(nc, f"edge_scatter{k}") for k in range(8)]
    ring_lanes = [Lane(nc, f"ring{k}") for k in range(RING)]
    ring = view(R, 0, RING * AW).rearrange("p (n a) -> p n a", a=AW)
    o = 4 * RING * AW
    onehot = view(R, o, 4 * P).rearrange("p (n c) -> p n c", c=P)
    lo_hot = view(R, o + 2048, 2 * P).rearrange("p (n c) -> p n c", c=P)
    lo_tmp = view(R, o + 3072, P)
    hi_hot = view(R, o + 3584, 2 * T).rearrange("p (n c) -> p n c", c=T)

    def aggregate(table, width, weighted, nbank, ready, extra):
        hot, summed, added = {}, {}, {}

        def one_hot(i):
            if i >= 4:
                V.after(summed[i - 4])
            if weighted:
                hot[i] = V.do(v.tensor_scalar(onehot[:, i % 4, :], iota[:, :], dloc[:, i:i + 1], wt[:, i:i + 1],
                                              ALU.is_equal, ALU.mult))
            else:
                hot[i] = V.do(v.tensor_scalar(onehot[:, i % 4, :], iota[:, :], dloc[:, i:i + 1], None,
                                              ALU.is_equal))

        def add(i):
            V.after(summed[i], added.get(i - 1))
            into = view(C, 0, T * AW)[:, ds(regs[i // 8][i % 8], width)]
            added[i] = V.do(v.tensor_tensor(into, bank[i % nbank][:, 0:width], into, ALU.add))

        G.after(*ready)
        one_hot(0)
        one_hot(1)
        regs = {}
        for i in range(ITEMS):
            if i >= RING:
                G.after(summed[i - RING])
            rows = ring_lanes[i % RING].start(
                G, lambda: g.indirect_dma_start(ring[:, i % RING, 0:D], None, table,
                                                IndirectOffsetOnAxis(ap=gidx[:, i:i + 1], axis=0)))
            if i + 2 < ITEMS:
                one_hot(i + 2)
            M.after(hot[i], rows, added.get(i - nbank))
            summed[i] = M.do(m.matmul(bank[i % nbank][:, 0:width], lhsT=onehot[:, i % 4, :],
                                      rhs=ring[:, i % RING, 0:width], start=True, stop=True))
            extra(i)
            if i % 8 == 0:
                n = min(8, ITEMS - i)
                regs[i // 8] = reg_values(ENG.DVE, toff[i // P:i // P + 1, i % P:i % P + n], (T - 1) * AW)
            if i:
                add(i - 1)
        add(ITEMS - 1)
        V.after(V.last)

    deg_done = {}
    lo_done, hi_done = {}, {}

    def beside_first(i):
        if i < EC:
            S.after(lo_done.get(i - 1), deg_done.get(i - 2))
            S.do(s.activation(lo_tmp[0:EP], iota[0:EP, :], ACT.Abs, bias=neg_lo[0:EP, i:i + 1]))
            S.after(S.last)
            lo_done[i] = S.do(s.activation(lo_hot[0:EP, i % 2, :], lo_tmp[0:EP], ACT.Relu, bias=1.0, scale=-1.0))
            V.after(deg_done.get(i - 2))
            hi_done[i] = V.do(v.tensor_scalar(hi_hot[0:EP, i % 2, :], iota[0:EP, 0:T], kt1f[0:EP, i:i + 1],
                                              rec1[0:EP, i, 2:3], ALU.is_equal, ALU.mult))
        j = i - 1
        if 0 <= j < EC:
            M.after(lo_done[j], hi_done[j])
            deg_done[j] = M.do(m.matmul(bank[7][:, 0:T], lhsT=lo_hot[0:EP, j % 2, :], rhs=hi_hot[0:EP, j % 2, :],
                                        start=j == 0, stop=j == EC - 1))
        if i % 2 == 0 and i // 2 < T:
            count_tile(kt1, 1, i // 2)
        if i == 2 * T:
            count_ends(1, bank[5], bank[6])
        c = i - 2 * T - 2
        if c >= 0 and c % PLACE == 0 and c // PLACE < T:
            place_edges(V, kt1, 1, c // PLACE)

    V.after(V.last)
    V.do(v.memset(ring[:, :, D:AW], 1.0))
    V.step(v.memset(view(C, 0, T * AW), 0.0))
    aggregate(tab, AW, False, 4, [V.last, table_lane[0].ticket], beside_first)

    V.after(deg_done[EC - 1])
    V.step(v.tensor_scalar(deg[:, :], bank[7][:, 0:T], 1.0, None, ALU.add))
    placed1 = V.step(v.tensor_copy(idx1[0:EP], pos_e[0:EP]))
    scatter_next = [0]

    def scatter_more(n):
        for c in range(scatter_next[0], min(EC, scatter_next[0] + n)):
            scatter_edges(G, scatter_lanes, 1, rec1, idx1, c, placed1)
        scatter_next[0] = min(EC, scatter_next[0] + n)

    scatter_more(BEFORE_SLOTS)

    def space(off, n, dt=F32):
        return view(XN, off, n, dt)

    w_lane, f0_lane = Lane(nc, "gnn0_weights_loaded"), Lane(nc, "ffn0_weights_loaded")
    w0 = view(R, 8192, KD * D).rearrange("p (k n) -> p k n", k=KD)
    gam = view(R, 8192 + 2048, D)
    bet = view(R, 8192 + 3072, D)
    mean_b = view(R, 8192 + 4096, D)
    scale_b = view(R, 8192 + 5120, D)
    rdeg = view(R, 8192 + 6144, T)
    w1a = view(R, 0, KD * HID0).rearrange("p (k n) -> p k n", k=KD)
    Y.after(M.last, V.last)
    w_lane.add(y.dma_start(w0, g0_w.rearrange("(k p) n -> p k n", p=P)))
    w_lane.add(y.dma_start(gam, g0_gamma.partition_broadcast(P)))
    w_lane.add(y.dma_start(bet, g0_beta.partition_broadcast(P)))
    f0_lane.add(y.dma_start(w1a, f0_w1.rearrange("(k p) n -> p k n", p=P)))

    V.step(v.tensor_scalar(rdeg, acc[:, :, D], 1.0, None, ALU.max))
    V.step(v.reciprocal(rdeg, rdeg))
    acc_t = view(C, tail, 3 * D).rearrange("p (n a) -> p n a", n=3)
    sq = view(C, tail + 3072, 2 * D).rearrange("p (n a) -> p n a", n=2)
    M.after(w_lane.ticket)
    V.after(w_lane.ticket)

    def transpose_rows(rows, to, *tickets):
        M.after(*tickets)
        for k in range(rows.shape[1] // P):
            M.do(m.transpose(to[:, k * P:(k + 1) * P], rows[:, k * P:(k + 1) * P], ident[:, :]))
        return M.last

    copied, prod, rst = {}, {}, {}
    for t in range(T + 2):
        if t < T:
            tr = transpose_rows(acc[:, t, 0:D], bank[t % 2], copied.get(t - 2))
            S.after(tr, prod.get(t - 3))
            copied[t] = S.do(s.activation(acc_t[:, t % 3, :], bank[t % 2][:, 0:D], ACT.Copy))
        if 1 <= t <= T:
            u = t - 1
            M.after(copied[u], rst.get(u - 2))
            for k in range(KD):
                prod[u] = M.do(m.matmul(bank[2 + u % 2][:, 0:D], lhsT=acc_t[:, u % 3, k * P:(k + 1) * P],
                                        rhs=w0[:, k, :], start=k == 0, stop=k == KD - 1))
            V.after(prod[u])
            rst[u] = V.do(v.scalar_tensor_tensor(XNt[:, u, :], bank[2 + u % 2][:, 0:D], rdeg[:, u:u + 1],
                                                 XNt[:, u, :], ALU.mult, ALU.add))
        if t >= 2:
            u = t - 2
            M.after(rst[u])
            M.do(m.matmul(bank[4][:, 0:D], lhsT=(ones_last if u == T - 1 else ones)[:, :], rhs=XNt[:, u, :],
                          start=u == 0, stop=u == T - 1))
    V.after(M.last)
    V.step(v.tensor_scalar(mean_b, bank[4][:, 0:D], 1.0 / N, None, ALU.mult))
    squared, summed_sq = {}, {}
    for t in range(T):
        V.do(v.tensor_tensor(XNt[:, t, :], XNt[:, t, :], mean_b, ALU.subtract))
        S.after(V.last, summed_sq.get(t - 2))
        squared[t] = S.do(s.activation(sq[:, t % 2, :], XNt[:, t, :], ACT.Square))
        M.after(squared[t])
        summed_sq[t] = M.do(m.matmul(bank[5][:, 0:D], lhsT=(ones_last if t == T - 1 else ones)[:, :],
                                     rhs=sq[:, t % 2, :], start=t == 0, stop=t == T - 1))
    wd = view(C, 0, E0 * KH0 * D)
    wd_lane = Lane(nc, "experts0_loaded")
    Y.after(M.last)
    for e in range(E0):
        wd_lane.add(y.dma_start(wd[:, e * KH0 * D:(e + 1) * KH0 * D].rearrange("p (k n) -> p k n", k=KH0),
                                f0_wd[e].rearrange("(k p) n -> p k n", p=P)))
    V.after(M.last)
    V.step(v.tensor_scalar(scale_b, bank[5][:, 0:D], 1.0 / N, BN_EPS, ALU.mult, ALU.add))
    S.after(V.last)
    V.after(S.do(s.activation(scale_b, scale_b, ACT.Sqrt)))
    V.step(v.reciprocal(scale_b, scale_b))
    V.step(v.tensor_tensor(scale_b, scale_b, gam, ALU.mult))
    stage = {}
    for a in range(0, T, G7):
        part = XNt[:, a:a + G7, :]
        xpart = X[:, a:a + G7, :]
        V.step(v.tensor_tensor(part, part, scale_b.unsqueeze(1).broadcast_to([P, G7, D]), ALU.mult))
        V.step(v.tensor_tensor(part, part, bet.unsqueeze(1).broadcast_to([P, G7, D]), ALU.add))
        V.step(v.scalar_tensor_tensor(xpart, part, 0.0, xpart, ALU.max, ALU.add))
        stage[a] = norm_stats(a, a + G7)
        if a:
            norm_finish(stage[a - G7])
    norm_finish(stage[T - G7])
    bn_done = V.last

    logits = view(dloc, 0, T * 8).rearrange("p (t e) -> p t e", e=8)
    probs = view(dloc, 4 * T * 8, T * 8).rearrange("p (t e) -> p t e", e=8)
    best = view(gidx[:, :].bitcast(F32), 0, T * 8).rearrange("p (t e) -> p t e", e=8)
    best_at = gidx[:, T * 8:2 * T * 8].rearrange("p (t e) -> p t e", e=8)
    chosen = view(wt, 0, 2 * T)
    r_mask = view(wt, 8 * T, 2 * T)
    r_scan = view(wt, 16 * T, 2 * T)
    r_pos = view(wt, 24 * T, 2 * T)
    r_ones = view(wt, 32 * T, 2 * T)
    r_cnt = view(wt, 40 * T, 8)
    r_off = view(wt, 40 * T + 32, 8)
    r_int = view(wt, 40 * T + 64, 8, I32)
    r_tiles = view(wt, 40 * T + 96, 8)
    r_end = view(wt, 40 * T + 128, 8)
    r_row = view(wt, 40 * T + 160, SLOTS1)
    from_row = view(wt, 40 * T + 160 + 4 * SLOTS1, SLOTS1, I32)
    to_row = view(wt, 40 * T + 160 + 8 * SLOTS1, SLOTS1, I32)
    beyond = float(1 << 20)

    def route(ncol, slots, row, at):
        V.step(v.memset(r_ones, 1.0))
        for e in range(8):
            V.step(v.tensor_scalar(r_mask[:, 0:ncol], chosen[:, 0:ncol], float(e), None, ALU.is_equal, ALU.add,
                                   accum_out=r_cnt[:, e:e + 1]))
        M.after(V.last)
        M.do(m.matmul(bank[0][:, 0:8], lhsT=ones[:, :], rhs=r_cnt, start=True, stop=True))
        M.do(m.matmul(bank[1][:, 0:8], lhsT=tri[:, :], rhs=r_cnt, start=True, stop=True))
        V.after(M.last)
        V.step(v.tensor_scalar(r_int, bank[0][:, 0:8], float(P - 1), None, ALU.add))
        V.step(v.tensor_scalar(r_int, r_int, 7, None, ALU.arith_shift_right))
        V.step(v.tensor_copy(r_tiles, r_int))
        V.step(v.tensor_tensor_scan(r_end, ones[:, 0:8], r_tiles, 0.0, ALU.mult, ALU.add))
        V.step(v.tensor_tensor(r_off, r_end, r_tiles, ALU.subtract))
        V.step(v.tensor_scalar(r_off, r_off, float(P), -1.0, ALU.mult, ALU.add))
        V.step(v.tensor_tensor(r_off, r_off, bank[1][:, 0:8], ALU.add))
        for e in range(8):
            V.step(v.tensor_scalar(r_mask[:, 0:ncol], chosen[:, 0:ncol], float(e), None, ALU.is_equal))
            V.step(v.tensor_tensor_scan(r_scan[:, 0:ncol], r_ones[:, 0:ncol], r_mask[:, 0:ncol],
                                        r_off[:, e:e + 1], ALU.mult, ALU.add))
            V.step(v.copy_predicated(r_pos[:, 0:ncol], r_mask[:, 0:ncol].bitcast(U32), r_scan[:, 0:ncol]))
        hi, lo, whole = r_mask[:, 0:ncol], r_pos[:, 0:ncol], pos[:, 0:ncol]
        V.step(v.tensor_copy(whole, r_pos[:, 0:ncol]))
        V.step(v.tensor_scalar(whole, whole, 7, None, ALU.arith_shift_right))
        V.step(v.tensor_copy(hi, whole))
        V.step(v.scalar_tensor_tensor(lo, hi, -float(P), r_pos[:, 0:ncol], ALU.mult, ALU.add))
        lo_row = space(at, 4 * P).rearrange("p (n c) -> p n c", c=P)
        hi_row = space(at + 2048, 4 * P).rearrange("p (n c) -> p n c", c=P)
        used = {}
        for c in range(ncol):
            V.after(used.get(c - 4))
            V.do(v.tensor_scalar(lo_row[:, c % 4, :], iota[:, :], r_pos[:, c:c + 1], row_id[:, c:c + 1],
                                 ALU.is_equal, ALU.mult))
            V.do(v.tensor_scalar(hi_row[:, c % 4, 0:slots], iota[:, 0:slots], r_mask[:, c:c + 1], None, ALU.is_equal))
            M.after(V.last)
            used[c] = M.do(m.matmul(bank[2][:, 0:slots], lhsT=lo_row[:, c % 4, :], rhs=hi_row[:, c % 4, 0:slots],
                                    start=c == 0, stop=c == ncol - 1))
        cmp = gidx[0:1, 0:slots * 8].bitcast(F32).rearrange("p (i e) -> p i e", e=8)
        V.step(v.tensor_tensor(cmp, r_end[0:1].unsqueeze(1).broadcast_to([1, slots, 8]),
                               iota[0:1, 0:slots].unsqueeze(2).broadcast_to([1, slots, 8]), ALU.is_le))
        V.step(v.tensor_reduce(r_row[0:1, 0:slots], cmp, AX.X, ALU.add))
        V.step(v.tensor_scalar(texp[0:1, 0:slots], r_row[0:1, 0:slots], 7.0, float(row), ALU.min, ALU.mult))
        V.after(M.last)
        got = lo_row[:, 0, 0:slots]
        empty = lo_row[:, 1, 0:slots]
        V.step(v.tensor_copy(got, bank[2][:, 0:slots]))
        V.step(v.tensor_scalar(empty, got, 0.0, beyond, ALU.is_equal, ALU.mult))
        V.step(v.scalar_tensor_tensor(to_row[:, 0:slots], got, -1.0, empty, ALU.add, ALU.add))
        V.step(v.tensor_scalar(got, got, -1.0, 0.0, ALU.add, ALU.max))
        V.step(v.tensor_scalar(empty, got, float(T * P), -float(T * P), ALU.is_ge, ALU.mult))
        return V.step(v.tensor_tensor(from_row[:, 0:slots], got, empty, ALU.add))

    y_lanes = [Lane(nc, f"expert_rows_scattered{k}") for k in range(4)]

    def scatter_out(k, i, rows, *tickets):
        return y_lanes[i % 4].start(G, lambda: g.indirect_dma_start(
            tok_y[k], IndirectOffsetOnAxis(ap=to_row[:, i:i + 1], axis=0), rows, None,
            bounds_check=tok_y[k].shape[0] - 1, oob_is_err=False), *tickets)

    comb_lanes = [Lane(nc, f"outputs_loaded{k}") for k in range(4)]
    comb_read = {}

    def combine_group(k, nchoice, a):
        for j in range(nchoice):
            n = (a // G7) * nchoice + j
            b = n % 4
            buf = space(b * G7 * D * 4, G7 * D).rearrange("p (t d) -> p t d", d=D)
            rows = tok_y[k][(j * T + a) * P:(j * T + a + G7) * P, :].rearrange("(t p) d -> p t d", p=P)
            q = (Y, S)[n % 2]
            ready = comb_lanes[b].start(q, lambda: q.e.dma_start(buf, rows), comb_read.get(b))
            comb_wait[n] = (ready, buf, j, b)

    comb_wait = {}

    def combine_apply(nchoice, a):
        for j in range(nchoice):
            ready, buf, jj, b = comb_wait[(a // G7) * nchoice + j]
            V.after(ready, V.last)
            for t in range(a, a + G7):
                c = jj * T + t
                V.do(v.scalar_tensor_tensor(X[:, t, :], buf[:, t - a, :], gate[:, c:c + 1], X[:, t, :],
                                            ALU.mult, ALU.add))
            comb_read[b] = V.last

    xr = space(0, 4 * D).rearrange("p (n d) -> p n d", d=D)
    xt = space(4096, 2 * D).rearrange("p (n d) -> p n d", d=D)
    hr = space(6144, 3 * HID0).rearrange("p (n h) -> p n h", h=HID0)
    ht = space(18432, 2 * HID0).rearrange("p (n h) -> p n h", h=HID0)
    b1b = space(26624, HID0)
    wg0 = space(30720, KH0 * 8).rearrange("p (k e) -> p k e", e=8)
    bg0 = space(30720 + 256, 8)
    bd = view(R, 8192, E0 * D)
    Y.after(bn_done)
    f0_lane.add(y.dma_start(b1b, f0_b1.partition_broadcast(P)))
    f0_lane.add(y.dma_start(wg0, f0_wg.rearrange("(k p) e -> p k e", p=P)))
    f0_lane.add(y.dma_start(bg0, f0_bg.partition_broadcast(P)))
    f0_lane.add(y.dma_start(bd, f0_bd.rearrange("e d -> (e d)").partition_broadcast(P)))
    for q in (M, V):
        q.after(f0_lane.ticket)
    hid_lanes = [Lane(nc, f"hidden_stored{k}") for k in range(3)]
    x_in, x_tr, xt_in, biased, gelud, h_tr, ht_in, lg_mm, lg_out = ({} for _ in range(9))
    for t in range(T + 3):
        if t < T:
            V.after(x_tr.get(t - 4))
            x_in[t] = norm_apply(t, xr[:, t % 4, :])
            x_tr[t] = transpose_rows(xr[:, t % 4, :], bank[t % 2], x_in[t], xt_in.get(t - 2))
            S.after(x_tr[t], h_tr.get(("mm", t - 2)))
            xt_in[t] = S.do(s.activation(xt[:, t % 2, :], bank[t % 2][:, 0:D], ACT.Copy))
        u = t - 1
        if 0 <= u < T:
            M.after(xt_in[u])
            V.after(hid_lanes[u % 3].ticket)
            for half in range(2):
                M.after(biased.get(2 * u + half - 2))
                cols = slice(half * 512, half * 512 + 512)
                for k in range(KD):
                    M.do(m.matmul(bank[2 + half][:, :], lhsT=xt[:, u % 2, k * P:(k + 1) * P], rhs=w1a[:, k, cols],
                                  start=k == 0, stop=k == KD - 1))
                V.after(M.last, h_tr.get(u - 3))
                biased[2 * u + half] = V.do(v.tensor_tensor(hr[:, u % 3, cols], bank[2 + half][:, :], b1b[:, cols],
                                                            ALU.add))
                S.after(V.last)
                gelud[u, half] = S.do(s.activation(hr[:, u % 3, cols], hr[:, u % 3, cols], ACT.Gelu))
            h_tr["mm", u] = M.last
            hid_lanes[u % 3].start(Y, lambda: y.dma_start(hid_d[u * P:(u + 1) * P, :], hr[:, u % 3, :]), gelud[u, 1])
        u = t - 2
        if 0 <= u < T:
            for half in range(2):
                transpose_rows(hr[:, u % 3, half * 512:half * 512 + 512], bank[4 + half], gelud[u, half],
                               ht_in.get((u - 1, half)))
                q = (S, V)[half]
                q.after(M.last, lg_mm.get(u - 2))
                dst_h = ht[:, u % 2, half * 512:half * 512 + 512]
                ht_in[u, half] = (S.do(s.activation(dst_h, bank[4][:, :], ACT.Copy)) if half == 0 else
                                  V.do(v.tensor_copy(dst_h, bank[5][:, :])))
            h_tr[u] = M.last
        u = t - 3
        if 0 <= u < T:
            M.after(ht_in[u, 0], ht_in[u, 1], lg_out.get(u - 2))
            for c in range(KH0):
                M.do(m.matmul(bank[6 + u % 2][:, 0:8], lhsT=ht[:, u % 2, c * P:(c + 1) * P], rhs=wg0[:, c, :],
                              start=c == 0, stop=c == KH0 - 1))
            lg_mm[u] = M.last
            V.after(M.last)
            lg_out[u] = V.do(v.tensor_tensor(logits[:, u, :], bank[6 + u % 2][:, 0:8], bg0, ALU.add))
    V.after(V.last)
    red = view(wt, 0, T)
    V.step(v.tensor_reduce(red, logits, AX.X, ALU.max))
    V.step(v.tensor_tensor(probs, logits, red.unsqueeze(2).broadcast_to([P, T, 8]), ALU.subtract))
    S.after(V.last)
    V.after(S.do(s.activation(probs, probs, ACT.Exp)))
    V.step(v.tensor_reduce(red, probs, AX.X, ALU.add))
    V.step(v.reciprocal(red, red))
    V.step(v.tensor_tensor(probs, probs, red.unsqueeze(2).broadcast_to([P, T, 8]), ALU.mult))
    for t in range(T):
        V.do(v.max(best[:, t, :], probs[:, t, :]))
    V.after(V.last)
    for t in range(T):
        V.do(v.max_index(best_at[:, t, :].bitcast(U32), best[:, t, :], probs[:, t, :]))
    V.after(V.last)
    V.do(v.tensor_copy(gate[:, 0:T], best[:, :, 0]))
    V.step(v.tensor_copy(chosen[:, 0:T], best_at[:, :, 0]))
    routed = route(T, SLOTS0, KH0 * D, 34816)

    NG = 4
    hg = space(0, NG * HID0).rearrange("p (n h) -> p n h", h=HID0)
    ys = space(30720, 4 * D).rearrange("p (n d) -> p n d", d=D)
    hg_lanes = [Lane(nc, f"hidden_gathered{k}") for k in range(NG)]
    M.after(wd_lane.ticket, routed)
    G.after(routed, *[l.ticket for l in hid_lanes])
    hg_in, h_tr, ht_in, mm2, y_in = ({} for _ in range(5))

    def gather_hidden(i):
        if i < SLOTS0:
            hg_in[i] = hg_lanes[i % NG].start(G, lambda: g.indirect_dma_start(
                hg[:, i % NG, :], None, hid_d, IndirectOffsetOnAxis(ap=from_row[:, i:i + 1], axis=0)), h_tr.get(i - NG))

    for i in range(3):
        gather_hidden(i)
    regs_m, regs_v = {}, {}
    for i in range(SLOTS0 + 1):
        if i < SLOTS0:
            if i % 4 == 0:
                regs_m[i // 4] = reg_values(ENG.PE, texp[0:1, i:i + 4], 7 * KH0 * D)
                regs_v[i // 4] = reg_values(ENG.DVE, texp[0:1, i:i + 4], 7 * KH0 * D)
            for half in range(2):
                b = bank[2 * (i % 2) + half]
                transpose_rows(hg[:, i % NG, half * 512:half * 512 + 512], b, hg_in[i], ht_in.get((i - 2, half)))
                q = (S, V)[half]
                q.after(M.last, mm2.get(i - 2))
                dst_h = ht[:, i % 2, half * 512:half * 512 + 512]
                ht_in[i, half] = (S.do(s.activation(dst_h, b[:, :], ACT.Copy)) if half == 0 else
                                  V.do(v.tensor_copy(dst_h, b[:, :])))
            h_tr[i] = M.last
            gather_hidden(i + 3)
            scatter_more(2)
        u = i - 1
        if u >= 0:
            M.after(ht_in[u, 0], ht_in[u, 1], y_in.get(u - 2))
            for c in range(KH0):
                M.do(m.matmul(bank[4 + u % 2][:, 0:D], lhsT=ht[:, u % 2, c * P:(c + 1) * P],
                              rhs=wd[:, ds(regs_m[u // 4][u % 4] + c * D, D)], start=c == 0, stop=c == KH0 - 1))
            mm2[u] = M.last
            V.after(M.last, y_lanes[u % 4].ticket)
            y_in[u] = V.do(v.tensor_tensor(ys[:, u % 4, :], bank[4 + u % 2][:, 0:D],
                                           bd[:, ds(regs_v[u // 4][u % 4] // KH0, D)], ALU.add))
            scatter_out(0, u, ys[:, u % 4, :], y_in[u])
    scattered = [l.ticket for l in y_lanes]
    scatter_more(EC)

    dm = view(wt, 0, T)
    V.after(G.last, *scattered)
    V.step(v.tensor_scalar(dm, deg[:, :], 0.0, None, ALU.is_gt))
    V.step(v.tensor_scalar(deg[:, :], deg[:, :], 1e-30, None, ALU.max))
    S.after(V.last)
    V.after(S.do(s.activation(deg[:, :], deg[:, :], ACT.Sqrt)))
    V.step(v.reciprocal(deg[:, :], deg[:, :]))
    V.step(v.tensor_tensor(deg[:, :], deg[:, :], dm, ALU.mult))

    def combined(k, nchoice):
        def before(a):
            if a == 0:
                combine_group(k, nchoice, 0)
            if a + G7 < T:
                combine_group(k, nchoice, a + G7)
            combine_apply(nchoice, a)
            V.after(V.last)
        return before

    Y.after(V.last, M.last, *scattered)
    S.after(V.last, M.last, *scattered)
    V.after(M.last)
    norm_tiles(acc, deg, tab1, table_lane[1], combined(0, 1))
    make_items(1, [l.ticket for l in scatter_lanes])

    gw_lane = Lane(nc, "gcn_weights_loaded")
    rec_space = rec1[:, :, :].rearrange("p e r -> p (e r)")
    gcn_w = [view(rec_space, 2048 * n, KD * D).rearrange("p (k n) -> p k n", k=KD) for n in range(3)]
    b2_b = view(rec_space, 6144, D)
    wg1 = view(rec_space, 7168, KD * 8).rearrange("p (k e) -> p k e", e=8)
    bg1 = view(rec_space, 7232, 8)
    bias1 = view(rec_space, 7264, 8)
    Y.after(*[l.ticket for l in scatter_lanes])
    for w_sb, w in zip(gcn_w, (g1_w, g1_w1, g1_w2)):
        gw_lane.add(y.dma_start(w_sb, w.rearrange("(k p) n -> p k n", p=P)))
    gw_lane.add(y.dma_start(b2_b, g1_b2.partition_broadcast(P)))
    gw_lane.add(y.dma_start(bcol[:, 0:2], g1_b.rearrange("(k p) -> p k", p=P), allow_slow_non_contiguous=True))
    gw_lane.add(y.dma_start(bcol[:, 2:4], g1_b1.rearrange("(k p) -> p k", p=P), allow_slow_non_contiguous=True))
    gw_lane.add(y.dma_start(wg1, f1_wg.rearrange("(k p) e -> p k e", p=P)))
    gw_lane.add(y.dma_start(bg1, f1_bg.partition_broadcast(P)))
    gw_lane.add(y.dma_start(bias1, f1_bias.partition_broadcast(P)))

    def beside_second(i):
        if i == 16:
            V.step(v.tensor_tensor(bg1, bg1, bias1, ALU.add))
        if i >= 20 and i % 8 == 0 and (i - 20) // 8 < T:
            t = (i - 20) // 8
            V.do(v.tensor_tensor(X[:, t, :], X[:, t, :], b2_b, ALU.add))

    def pair(n):
        return space(2048 * n, KD * G2 * P).rearrange("p (k n) -> p k n", k=KD)

    at_b, bt_b, ct_b = [pair(0), pair(1)], [pair(2), pair(3)], [pair(4), pair(5)]
    xt2 = space(12288, 2 * G2 * D).rearrange("p (n a) -> p n a", n=2)
    norm2 = space(16384, 3 * G2 * D).rearrange("p (n t d) -> p n t d", n=3, d=D)
    logits1 = space(40960, T * 8).rearrange("p (t e) -> p t e", e=8)
    best1 = space(43008, T * 8).rearrange("p (t e) -> p t e", e=8)
    best_at1 = space(45056, T * 8, I32).rearrange("p (t e) -> p t e", e=8)
    pairs = [(a, min(G2, T - a)) for a in range(0, T, G2)]
    norm_lanes = [Lane(nc, f"normed_stored{k}") for k in range(3)]

    def head_stages():
        scaled, a_tr, a_in, b_mm, b_in, c_mm, c_in, x_mm, x_out, stage, applied = ({} for _ in range(11))
        g_tr, g_in, g_mm, g_out = {}, {}, {}, {}

        def scale(gi, a, n):
            V.after(V.last)
            for t in range(a, a + n):
                scaled[gi] = V.do(v.tensor_scalar(acc[:, t, 0:D], acc[:, t, 0:D], deg[:, t:t + 1], None, ALU.mult))

        def transpose_sums(gi, a, n):
            M.after(scaled[gi], a_in.get(gi - 1))
            for k in range(KD):
                for j in range(n):
                    a_tr[gi] = M.do(m.transpose(bank[2][:, (k * G2 + j) * P:(k * G2 + j + 1) * P],
                                                acc[:, a + j, k * P:(k + 1) * P], ident[:, :]))

        def copy_sums(gi, a, n):
            V.after(a_tr[gi], b_mm.get(gi - 2))
            src_b = bank[2][:, :].rearrange("p (k n) -> p k n", k=KD)
            a_in[gi] = V.do(v.tensor_copy(at_b[gi % 2][:, :, 0:n * P], src_b[:, :, 0:n * P]))

        def product(b, w_sb, frm, to, ready, mm, done, free, col, fn):
            def run(gi, a, n):
                M.after(ready[gi], done.get(gi - 1))
                for c in range(KD):
                    for k in range(KD):
                        mm[gi] = M.do(m.matmul(bank[b][:, c * G2 * P:c * G2 * P + n * P],
                                               lhsT=w_sb[:, k, c * P:(c + 1) * P], rhs=frm[gi % 2][:, k, 0:n * P],
                                               start=k == 0, stop=k == KD - 1))
                S.after(mm[gi], free.get(gi - 2))
                for c in range(KD):
                    done[gi] = S.do(s.activation(to[gi % 2][:, c, 0:n * P],
                                                 bank[b][:, c * G2 * P:c * G2 * P + n * P],
                                                 fn, bias=bcol[:, col + c:col + c + 1]))
            return run

        def last_product(gi, a, n):
            M.after(c_in[gi], x_out.get(gi - 1))
            for j in range(n):
                for k in range(KD):
                    x_mm[gi] = M.do(m.matmul(bank[5][:, j * D:(j + 1) * D],
                                             lhsT=ct_b[gi % 2][:, k, j * P:(j + 1) * P], rhs=gcn_w[2][:, k, :],
                                             start=k == 0, stop=k == KD - 1))

        def residual(gi, a, n):
            V.after(x_mm[gi], V.last)
            x_out[gi] = V.step(v.tensor_tensor(X[:, a:a + n, :], bank[5][:, 0:n * D].rearrange("p (t d) -> p t d", d=D),
                                               X[:, a:a + n, :], ALU.add))
            stage[gi] = norm_stats(a, a + n)

        def norm(gi, a, n):
            norm_finish(stage[gi])
            V.after(g_tr.get(gi - 3), norm_lanes[gi % 3].ticket)
            for j in range(n):
                applied[gi] = norm_apply(a + j, norm2[:, gi % 3, j, :])
            norm_lanes[gi % 3].start(Y, lambda: y.dma_start(
                tab2[a * P:(a + n) * P, :].rearrange("(t p) d -> p t d", p=P), norm2[:, gi % 3, 0:n, :]), applied[gi])

        def transpose_normed(gi, a, n):
            M.after(applied[gi], g_in.get(gi - 1))
            for j in range(n):
                g_tr[gi] = transpose_rows(norm2[:, gi % 3, j, :], bank[6][:, j * D:(j + 1) * D])
            S.after(g_tr[gi], g_mm.get(gi - 2))
            g_in[gi] = S.do(s.activation(xt2[:, gi % 2, 0:n * D], bank[6][:, 0:n * D], ACT.Copy))

        def gate_product(gi, a, n):
            M.after(g_in[gi], g_out.get(gi - 1))
            for j in range(n):
                for k in range(KD):
                    g_mm[gi] = M.do(m.matmul(bank[7][:, j * 8:(j + 1) * 8],
                                             lhsT=xt2[:, gi % 2, j * D + k * P:j * D + (k + 1) * P],
                                             rhs=wg1[:, k, :], start=k == 0, stop=k == KD - 1))

        def two_best(gi, a, n):
            V.after(g_mm[gi])
            g_out[gi] = V.step(v.tensor_tensor(logits1[:, a:a + n, :],
                                               bank[7][:, 0:n * 8].rearrange("p (t e) -> p t e", e=8),
                                               bg1.unsqueeze(1).broadcast_to([P, n, 8]), ALU.add))
            for t in range(a, a + n):
                V.do(v.max(best1[:, t, :], logits1[:, t, :]))
            V.after(V.last)
            for t in range(a, a + n):
                V.do(v.max_index(best_at1[:, t, :].bitcast(U32), best1[:, t, :], logits1[:, t, :]))

        return (scale, transpose_sums, copy_sums,
                product(3, gcn_w[0], at_b, bt_b, a_in, b_mm, b_in, c_mm, 0, ACT.Identity),
                product(4, gcn_w[1], bt_b, ct_b, b_in, c_mm, c_in, x_mm, 2, ACT.Relu),
                last_product, residual, norm, transpose_normed, gate_product, two_best)

    def second_layer(start, step):
        stages = head_stages()
        order = sorted((start(gi) + n * step, -n, gi) for gi in range(len(pairs)) for n in range(len(stages)))

        def run_until(i):
            while order and order[0][0] <= i:
                _, n, gi = order.pop(0)
                stages[-n](gi, *pairs[gi])

        def beside(i):
            beside_second(i)
            run_until(i)

        read_stats.clear()
        aggregate(tab1, D, True, 2, [V.last, table_lane[1].ticket], beside)
        run_until(order[-1][0])

    for q in (V, S, M, G, Y):
        q.after(V.last, M.last, gw_lane.ticket)
    is_late = nc.values_load_multi_w_load_instructions(
        late[0:1, 0:1], engines=[ENG.DVE, ENG.Activation, ENG.PE, ENG.Pool, ENG.SP], min_val=0, max_val=1,
        skip_runtime_bounds_check_because="a comparison's result")[1][0]
    counters = [V, S, M, G, Y, *ring_lanes, *norm_lanes]
    before = [c.state() for c in counters]
    with nc.If(is_late > 0):
        second_layer(lambda gi: ITEMS + gi, 1)
    ends = [c.state() for c in counters]
    for c, state in zip(counters, before):
        c.restore(state)
    with nc.Else():
        second_layer(lambda gi: PER_TILE * min(T, G2 * (gi + 1)) + MARGIN + 1, STEP)
    assert [c.value() for c in counters] == [e[0] for e in ends]
    for c, state in zip(counters, before):
        c.forget_waits(state)
    read_stats.clear()
    normed_stored = [l.ticket for l in norm_lanes]

    w1e = view(C, 0, E1 * KD * HID1)
    w2e = view(C, 4 * E1 * KD * HID1, E1 * KH1 * D)
    b1e = view(R, 0, E1 * HID1)
    b2e = view(rec_space, 0, E1 * D)
    ew_lane = Lane(nc, "experts1_loaded")
    Y.after(V.last, M.last, S.last)
    S.after(V.last, M.last)
    for e in range(E1):
        ew_lane.add(y.dma_start(w1e[:, e * KD * HID1:(e + 1) * KD * HID1].rearrange("p (k n) -> p k n", k=KD),
                                f1_w1[e].rearrange("(k p) n -> p k n", p=P)))
        ew_lane.add(y.dma_start(w2e[:, e * KH1 * D:(e + 1) * KH1 * D].rearrange("p (k n) -> p k n", k=KH1),
                                f1_w2[e].rearrange("(k p) n -> p k n", p=P)))
    ew_lane.add(y.dma_start(b1e, f1_b1.rearrange("e h -> (e h)").partition_broadcast(P)))
    ew_lane.add(y.dma_start(b2e, f1_b2.rearrange("e d -> (e d)").partition_broadcast(P)))
    V.after(V.last)
    V.step(v.tensor_tensor(gate[:, T:2 * T], best1[:, :, 1], best1[:, :, 0], ALU.subtract))
    S.after(V.last)
    V.after(S.do(s.activation(gate[:, T:2 * T], gate[:, T:2 * T], ACT.Exp)))
    V.step(v.tensor_scalar(gate[:, 0:T], gate[:, T:2 * T], 1.0, None, ALU.add))
    V.step(v.reciprocal(gate[:, 0:T], gate[:, 0:T]))
    V.step(v.tensor_tensor(gate[:, T:2 * T], gate[:, T:2 * T], gate[:, 0:T], ALU.mult))
    V.do(v.tensor_copy(chosen[:, 0:T], best_at1[:, :, 0]))
    V.step(v.tensor_copy(chosen[:, T:2 * T], best_at1[:, :, 1]))
    V.after(*normed_stored)
    routed = route(2 * T, SLOTS1, KD * HID1, 34816)

    NX = 5
    xg = space(0, NX * D).rearrange("p (n d) -> p n d", d=D)
    xt3 = space(5120, 3 * D).rearrange("p (n d) -> p n d", d=D)
    h1 = space(8192, 2 * HID1).rearrange("p (n h) -> p n h", h=HID1)
    h1t = space(12288, 2 * HID1).rearrange("p (n h) -> p n h", h=HID1)
    ys1 = space(16384, 4 * D).rearrange("p (n d) -> p n d", d=D)
    xg_lanes = [Lane(nc, f"slot_rows_gathered{k}") for k in range(NX)]
    for q in (M, V):
        q.after(ew_lane.ticket, routed)
    G.after(routed, *normed_stored)
    xg_in, x_tr, xt_in, mm1, h_in, h_tr, ht_in, mm2, y_in = ({} for _ in range(9))
    regs_m, regs_v = {}, {}

    def gather_rows(i):
        if i < SLOTS1:
            xg_in[i] = xg_lanes[i % NX].start(G, lambda: g.indirect_dma_start(
                xg[:, i % NX, :], None, tab2, IndirectOffsetOnAxis(ap=from_row[:, i:i + 1], axis=0)), x_tr.get(i - NX))

    def slot_rows_transposed(i):
        if i < SLOTS1:
            x_tr[i] = transpose_rows(xg[:, i % NX, :], bank[i % 2], xg_in[i], xt_in.get(i - 2))
            S.after(x_tr[i], mm1.get(i - 3))
            xt_in[i] = S.do(s.activation(xt3[:, i % 3, :], bank[i % 2][:, 0:D], ACT.Copy))

    for i in range(4):
        gather_rows(i)
    slot_rows_transposed(0)
    for i in range(SLOTS1 + 1):
        slot_rows_transposed(i + 1)
        gather_rows(i + 4)
        if i < SLOTS1 and i % 4 == 0:
            n = min(4, SLOTS1 - i)
            regs_m[i // 4] = reg_values(ENG.PE, texp[0:1, i:i + n], 7 * KD * HID1)
            regs_v[i // 4] = reg_values(ENG.DVE, texp[0:1, i:i + n], 7 * KD * HID1)
        u = i - 1
        if u >= 0:
            h_tr[u] = transpose_rows(h1[:, u % 2, :], bank[4], h_in[u], ht_in.get(u - 1))
            S.after(M.last, mm2.get(u - 2))
            ht_in[u] = S.do(s.activation(h1t[:, u % 2, :], bank[4][:, :], ACT.Relu))
        if i < SLOTS1:
            M.after(xt_in[i], h_in.get(i - 2))
            for k in range(KD):
                M.do(m.matmul(bank[2 + i % 2][:, :], lhsT=xt3[:, i % 3, k * P:(k + 1) * P],
                              rhs=w1e[:, ds(regs_m[i // 4][i % 4] + k * HID1, HID1)], start=k == 0, stop=k == KD - 1))
            mm1[i] = M.last
            V.after(M.last, h_tr.get(i - 2))
            h_in[i] = V.do(v.tensor_tensor(h1[:, i % 2, :], bank[2 + i % 2][:, :],
                                           b1e[:, ds(regs_v[i // 4][i % 4] // KD, HID1)], ALU.add))
        if u >= 0:
            M.after(ht_in[u], y_in.get(u - 2))
            for c in range(KH1):
                M.do(m.matmul(bank[5 + u % 2][:, 0:D], lhsT=h1t[:, u % 2, c * P:(c + 1) * P],
                              rhs=w2e[:, ds(regs_m[u // 4][u % 4] + c * D, D)], start=c == 0, stop=c == KH1 - 1))
            mm2[u] = M.last
            V.after(M.last, y_lanes[u % 4].ticket)
            y_in[u] = V.do(v.tensor_tensor(ys1[:, u % 4, :], bank[5 + u % 2][:, 0:D],
                                           b2e[:, ds(regs_v[u // 4][u % 4] // KH1, D)], ALU.add))
            scatter_out(1, u, ys1[:, u % 4, :], y_in[u])

    out_lane = Lane(nc, "out_stored")
    scattered = [l.ticket for l in y_lanes]
    for q in (Y, S):
        q.after(V.last, M.last, *scattered)
    comb_read.clear()
    comb_wait.clear()
    before = combined(1, 2)
    for a in range(0, T, G7):
        before(a)
        Y.after(V.last)
        full = G7 if a + G7 < T else G7 - 1
        out_lane.add(y.dma_start(out[a * P:(a + full) * P, :].rearrange("(t p) d -> p t d", p=P), X[:, a:a + full, :]))
    out_lane.add(y.dma_start(out[(T - 1) * P:N, :], X[0:LAST, T - 1, :]))
    Y.after(out_lane.ticket)


_INS = ["x", "src", "dst", "edge_weight", "L0_gnn_W_src", "L0_gnn_gamma", "L0_gnn_beta", "L0_ffn_W1", "L0_ffn_b1",
        "L0_ffn_Wg", "L0_ffn_bg", "L0_ffn_Wd", "L0_ffn_bd", "L1_gnn_W", "L1_gnn_b", "L1_gnn_W1", "L1_gnn_b1",
        "L1_gnn_W2", "L1_gnn_b2", "L1_ffn_Wg", "L1_ffn_bg", "L1_ffn_bias", "L1_ffn_W1", "L1_ffn_b1", "L1_ffn_W2",
        "L1_ffn_b2"]


def kernel(**inputs):
    import concourse.bacc as bacc
    from concourse.bass_utils import run_bass_kernel_spmd

    nc = bacc.Bacc("TRN2", target_bir_lowering=False, num_devices=1)
    arrays, args = {}, []
    for name in _INS:
        a = np.ascontiguousarray(inputs[name])
        arrays[f"in_{name}"] = a
        args.append(nc.dram_tensor(f"in_{name}", a.shape, mybir.dt.from_np(a.dtype), kind="ExternalInput").ap())
    args.append(nc.dram_tensor("out_rows", (N, D), F32, kind="ExternalOutput").ap())
    build(nc, *args)
    r = run_bass_kernel_spmd(nc, [arrays], core_ids=[0])
    return r.results[0]["out_rows"]
```

```python
import numpy as np

import concourse.bass as bass
from concourse import mybir
from concourse.bass import IndirectOffsetOnAxis, ds

F32 = mybir.dt.float32
I32 = mybir.dt.int32
U16 = mybir.dt.uint16
U32 = mybir.dt.uint32
BF16 = mybir.dt.bfloat16
ALU = mybir.AluOpType
ACT = mybir.ActivationFunctionType
AX = mybir.AxisListType
ENG = mybir.EngineType

P = 128
N = 6250
D = 256
T = -(-N // P)
LAST = N - (T - 1) * P
KD = D // P
NE = 100000
CH = -(-NE // P)
EC = CH
EL = NE - (P - 1) * EC
ITEMS = CH + T - 1
IJ = -(-ITEMS // P)
AW = D + 1
REC = 3
HID0, E0 = 1024, 8
KH0 = HID0 // P
HID1, E1 = 512, 8
KH1 = HID1 // P
SLOTS0 = (T * P + E0 * (P - 1)) // P
SLOTS1 = (2 * T * P + E1 * (P - 1)) // P
LN_EPS = 1e-5
BN_EPS = 1e-5
BEFORE_SLOTS = 600
PLACE = 14
RING = 12
NCB = 3
G7 = 7
G2 = 2
PER_TILE = -(-ITEMS // T)
MARGIN = 10
STEP = 3


class Queue:

    def __init__(self, nc, engine, name):
        self.e = engine
        self.done = nc.alloc_semaphore(name)
        self.count = 0
        self.last = None
        self.met = {}

    def after(self, *tickets):
        for t in tickets:
            if t is None:
                continue
            if isinstance(t, list):
                self.after(*t)
                continue
            sem, value = t
            if self.met.get(id(sem), 0) < value:
                self.e.wait_ge(sem, value)
                self.met[id(sem)] = value

    def state(self):
        return self.count, self.last, dict(self.met)

    def restore(self, state):
        self.count, self.last, self.met = state[0], state[1], dict(state[2])

    def value(self):
        return self.count

    def forget_waits(self, state):
        self.met = dict(state[2])

    def do(self, instruction):
        instruction.then_inc(self.done, 1)
        self.count += 1
        self.last = (self.done, self.count)
        return self.last

    def step(self, instruction):
        t = self.do(instruction)
        self.after(t)
        return t


class Lane:

    def __init__(self, nc, name):
        self.sem = nc.alloc_semaphore(name)
        self.total = 0

    @property
    def ticket(self):
        return (self.sem, self.total) if self.total else None

    def state(self):
        return (self.total,)

    def restore(self, state):
        self.total = state[0]

    def value(self):
        return self.total

    def forget_waits(self, state):
        pass

    def start(self, queue, make, *tickets):
        queue.after(*tickets, self.ticket)
        return self.add(make())

    def add(self, instruction):
        instruction.then_inc(self.sem, 16)
        self.total += 16
        return self.ticket


def build(nc, x, src, dst, edge_weight, g0_w, g0_gamma, g0_beta, f0_w1, f0_b1, f0_wg, f0_bg, f0_wd,
          f0_bd, g1_w, g1_b, g1_w1, g1_b1, g1_w2, g1_b2, f1_wg, f1_bg, f1_bias, f1_w1, f1_b1, f1_w2,
          f1_b2, out):
    V = Queue(nc, nc.vector, "vector_done")
    S = Queue(nc, nc.scalar, "scalar_done")
    M = Queue(nc, nc.tensor, "tensor_done")
    G = Queue(nc, nc.gpsimd, "gpsimd_done")
    Y = Queue(nc, nc.sync, "sync_done")
    v, s, m, g, y = nc.vector, nc.scalar, nc.tensor, nc.gpsimd, nc.sync

    def region(name, nbytes):
        return nc.alloc_sbuf_tensor(name, [P, nbytes // 4], F32)

    def view(reg, off, n, dt=F32, parts=P):
        size = 2 if dt in (BF16, U16) else 4
        v32 = reg[0:parts, off // 4:(off + n * size) // 4]
        return v32 if dt == F32 else v32.bitcast(dt)

    def small(name, n, dt=F32):
        return nc.alloc_sbuf_tensor(name, [P, n], dt)

    def reg_values(engine, ap, most):
        return nc.values_load_multi_w_load_instructions(
            ap, engines=[engine], min_val=0, max_val=most,
            skip_runtime_bounds_check_because="clamped to the last tile or expert where it is computed")[1]

    X = nc.alloc_sbuf_tensor("x_rows", [P, T, D], F32)
    XN = nc.alloc_sbuf_tensor("normed", [P, T * D], F32)
    XNt = XN[:, :].rearrange("p (t d) -> p t d", d=D)
    C = region("acc_or_weights", 4 * E0 * KH0 * D)
    R = region("ring_or_weights", 16384)
    rec1 = nc.alloc_sbuf_tensor("edge_records_by_src", [P, EC, REC], F32)
    posr = region("edge_positions", 4 * EC)
    dloc = small("item_local_node", IJ * P)
    gidx = small("item_other_node", IJ * P, I32)
    wt = small("item_weight", IJ * P)
    iota = small("iota_row", P)
    ident = small("identity", P)
    ones = small("ones", P)
    ones_last = small("ones_of_last_tile", P)
    tri = small("earlier_partitions", P)
    mv = nc.alloc_sbuf_tensor("mean_var", [P, T, 2], F32)
    rstd = small("rstd", T)
    deg = small("node_degree", T)
    stats = nc.alloc_sbuf_tensor("bn_stats_ring", [P, 4, 6], F32)
    toff = small("item_acc_offset", P, I32)
    pos = small("token_slot", 2 * T, I32)
    gate = small("token_gate", 2 * T)
    texp = small("slot_expert_offset", SLOTS1, I32)
    row_id = small("token_row_plus_one", 2 * T)
    tot = small("tile_edges", T)
    incl = small("tile_edge_ends", T)
    offs = small("tile_edge_offsets", T)
    unordered = small("unordered_partitions", 1, I32)
    late = small("is_late", 1, I32)
    small_f = small("has_fall", 1)
    shift = small("norm_shift", T)
    bcol = small("bias_columns", 4)
    bank = [nc.alloc_psum_tensor(f"bank{k}", [P, 512], F32) for k in range(8)]

    rec_d = [nc.dram_tensor(f"ordered_edges{k}", (CH * P, REC), F32, kind="Internal").ap() for k in range(2)]
    tab = nc.dram_tensor("gather_table", (T * P, D), F32, kind="Internal").ap()
    tab1 = nc.dram_tensor("gather_table1", (T * P, D), F32, kind="Internal").ap()
    hid_d = nc.dram_tensor("hidden_rows", (T * P, HID0), F32, kind="Internal").ap()
    tab2 = nc.dram_tensor("gather_table2", (T * P, D), F32, kind="Internal").ap()
    tok_y = nc.dram_tensor("expert_out", (T * P, D), F32, kind="Internal").ap()
    gate_d = nc.dram_tensor("gates", (2 * T * P, 1), F32, kind="Internal").ap()

    raw_src = view(C, 0, EC, I32)
    raw_dst = view(C, 3200, EC, I32)
    raw_w = view(C, 6400, EC)
    rec0 = view(C, 9600, EC * REC).rearrange("p (e r) -> p e r", r=REC)
    idx0 = view(C, 19200, EC, I32)
    raw_next = view(C, 27200, EC, I32)
    falls = view(C, 30400, EC)
    int_tmp = view(C, 22400, EC, I32)
    kt0 = view(C, 25600, EC, BF16)
    raw_end = 33600
    acc = view(C, 0, T * AW).rearrange("p (t a) -> p t a", a=AW)
    tail = 4 * T * AW
    kt1 = view(C, tail, EC, BF16)
    mask_e = view(C, tail + 1600, EC, BF16)
    ones_e = view(C, tail + 3200, EC, BF16)
    scan_e = view(C, tail + 4800, EC)
    pos_e = view(C, tail + 8000, EC)
    neg_lo = view(C, tail + 11200, EC)
    kt1f = view(posr, 0, EC)
    idx1 = view(posr, 0, EC, I32)

    load_dst, load_src, load_w, load_next = [Lane(nc, f"edges_loaded{k}") for k in range(4)]
    load_x = Lane(nc, "x_loaded")
    V.do(v.memset(raw_dst[:, EL:EC], T * P))
    V.do(v.memset(raw_src[:, EL:EC], T * P))
    V.do(v.memset(raw_w[:, EL:EC], 0.0))
    V.do(v.memset(raw_next[:, EL - 1:EC], 1 << 20))
    Y.after(V.last)
    body = (P - 1) * EC

    def load_edges(lane, to, frm, first, last):
        lane.add(y.dma_start(to[0:P - 1], frm[first:first + body].rearrange("(p e) -> p e", e=EC)))
        lane.add(y.dma_start(to[P - 1:P, 0:last], frm[first + body:first + body + last].rearrange("(p e) -> p e", p=1)))

    load_edges(load_dst, raw_dst, dst, 0, EL)
    load_edges(load_next, raw_next, dst, 1, EL - 1)
    load_edges(load_src, raw_src, src, 0, EL)
    load_edges(load_w, raw_w, edge_weight, 0, EL)
    V.do(v.memset(X[:, T - 1, :], 0.0))
    V.do(v.memset(view(C, raw_end, (4 * T * AW - raw_end) // 4), 0.0))
    S.after(load_dst.ticket, V.last)
    for a in range(0, T - 1, 8):
        load_x.add(s.dma_start(X[:, a:a + 8, :], x[a * P:(a + 8) * P, :].rearrange("(t p) d -> p t d", p=P)))
    load_x.add(s.dma_start(X[0:LAST, T - 1, :], x[(T - 1) * P:N, :]))

    V.do(v.memset(ones[:, :], 1.0))
    V.do(v.memset(ident[:, :], 0.0))
    G.do(g.iota(iota[:, :], pattern=[[1, P]], base=0, channel_multiplier=0, allow_small_or_imprecise_dtypes=True))
    G.do(g.iota(row_id[:, :], pattern=[[P, 2 * T]], base=1, channel_multiplier=1, allow_small_or_imprecise_dtypes=True))
    G.after(V.last)
    G.do(g.affine_select(out=tri[:, :], in_=ones[:, :], compare_op=ALU.is_gt, fill=0.0, base=0,
                         pattern=[[1, P]], channel_multiplier=-1))
    G.do(g.affine_select(out=ones_last[:, :], in_=ones[:, :], compare_op=ALU.is_gt, fill=0.0, base=LAST,
                         pattern=[[0, P]], channel_multiplier=-1))
    consts = G.do(g.affine_select(out=ident[:, :], in_=ident[:, :], compare_op=ALU.not_equal, fill=1.0, base=0,
                                  pattern=[[-1, P]], channel_multiplier=1))
    for q in (V, S, M):
        q.after(consts)

    V.after(load_dst.ticket)
    V.step(v.tensor_scalar(int_tmp, raw_dst, 7, None, ALU.arith_shift_right))
    V.step(v.tensor_copy(kt0, int_tmp))
    S.after(load_src.ticket, load_w.ticket, load_next.ticket)
    for rec, key, other in ((rec0, raw_dst, raw_src), (rec1[:, :, :], raw_src, raw_dst)):
        S.do(s.activation(rec[:, :, 0], key, ACT.Copy))
        S.do(s.activation(rec[:, :, 1], other, ACT.Copy))
        S.do(s.activation(rec[:, :, 2], raw_w, ACT.Copy))
    records = S.last

    count_scratch = [mask_e, scan_e.bitcast(BF16)[:, 0:EC]]

    counted = {}

    def count_tile(kt, k, t):
        V.after(counted.get(t - 2))
        counted[t] = V.do(v.tensor_scalar(count_scratch[t % 2][0:P], kt, float(t), None, ALU.is_equal,
                                          ALU.add, accum_out=offs[0:P, t:t + 1]))

    def count_ends(k, all_bank, before_bank):
        V.after(V.last)
        M.after(V.last)
        M.do(m.matmul(all_bank[:, 0:T], lhsT=ones[0:P, :], rhs=offs[0:P, :], start=True, stop=True))
        M.do(m.matmul(before_bank[:, 0:T], lhsT=tri[0:P, :], rhs=offs[0:P, :], start=True, stop=True))
        V.after(M.last)
        V.step(v.tensor_copy(tot[:, :], all_bank[:, 0:T]))
        V.step(v.tensor_tensor_scan(incl[:, :], ones[:, 0:T], tot[:, :], 0.0, ALU.mult, ALU.add))
        V.step(v.scalar_tensor_tensor(offs[:, :], before_bank[:, 0:T], -1.0, incl[:, :], ALU.add, ALU.add))
        V.step(v.tensor_tensor(offs[:, :], offs[:, :], tot[:, :], ALU.subtract))
        counted.clear()

    def place_edges(q, kt, k, t):
        q.step(v.tensor_scalar(mask_e, kt, float(t), None, ALU.is_equal))
        q.step(v.tensor_tensor_scan(scan_e, ones_e, mask_e, offs[0:P, t:t + 1],
                                    ALU.mult, ALU.add))
        q.step(v.copy_predicated(pos_e, mask_e.bitcast(U16), scan_e))

    def scatter_edges(q, lanes, k, rec, idx, c, *tickets):
        return lanes[c % len(lanes)].start(
            q, lambda: g.indirect_dma_start(rec_d[k], IndirectOffsetOnAxis(ap=idx[0:P, c:c + 1], axis=0),
                                            rec[0:P, c, :], None), *tickets)

    for t in range(T):
        count_tile(kt0, 0, t)
    count_ends(0, bank[0], bank[1])

    V.after(load_next.ticket)
    V.step(v.tensor_tensor(falls, raw_dst, raw_next, ALU.is_gt))
    V.step(v.tensor_reduce(small_f[:, :], falls, AX.X, ALU.max))
    M.after(V.last)
    M.do(m.matmul(bank[2][:, 0:1], lhsT=ones[:, :], rhs=small_f[:, :], start=True, stop=True))
    V.after(M.last)
    V.step(v.tensor_copy(unordered[:, :], bank[2][:, 0:1]))
    V.step(v.memset(ones_e, 1.0))
    G.after(V.last)
    ready0 = G.do(g.iota(pos_e, pattern=[[1, EC]], base=NE - EL, channel_multiplier=0,
                         allow_small_or_imprecise_dtypes=True))
    for q in (V, G):
        q.after(ready0, records)

    VS = Queue(nc, nc.vector, "sort_vector_done")
    GS = Queue(nc, nc.gpsimd, "sort_gpsimd_done")
    sort_lanes = [Lane(nc, f"sort_scatter{k}") for k in range(8)]
    copy_lane = Lane(nc, "records_copied")
    is_unordered = nc.values_load_multi_w_load_instructions(
        unordered[0:1, 0:1], engines=[ENG.DVE, ENG.Pool], min_val=0, max_val=P,
        skip_runtime_bounds_check_because="a count of partitions")[1][0]
    with nc.If(is_unordered > 0):
        for t in range(T):
            place_edges(VS, kt0, 0, t)
        VS.step(v.tensor_copy(idx0, pos_e))
        for c in range(EC):
            scatter_edges(GS, sort_lanes, 0, rec0, idx0, c, VS.last)
        GS.after(*[l.ticket for l in sort_lanes])
    with nc.Else():
        copy_lane.add(g.dma_start(rec_d[0].rearrange("(p e) r -> p (e r)", e=EC),
                                  rec0.rearrange("p e r -> p (e r)")))
        g.wait_ge(*copy_lane.ticket)

    table_lane = [Lane(nc, f"table_written{k}") for k in range(2)]

    def norm_stats(a, b, scale=None):
        for t in range(a, b + 1):
            if t < b:
                V.after(read_stats.get(t % 4))
                stat = V.do(v.bn_stats(stats[:, t % 4, :], X[:, t, :]))
            if t > a:
                V.after(wrote_stats)
                read_stats[(t - 1) % 4] = V.do(v.bn_aggr(mv[:, t - 1, :], stats[:, (t - 1) % 4, :]))
            wrote_stats = stat
        V.after(V.last)
        r = rstd[:, a:b]
        S.after(V.step(v.tensor_scalar(r, mv[:, a:b, 1], LN_EPS, None, ALU.add)))
        rooted = S.do(s.activation(r, r, ACT.Sqrt))
        return rooted, a, b, scale

    def norm_finish(stage, shift=None):
        rooted, a, b, scale = stage
        V.after(rooted)
        V.step(v.reciprocal(rstd[:, a:b], rstd[:, a:b]))
        if scale is not None:
            V.step(v.tensor_tensor(rstd[:, a:b], rstd[:, a:b], scale[:, a:b], ALU.mult))
        if shift is not None:
            V.step(v.scalar_tensor_tensor(shift[:, a:b], mv[:, a:b, 0], -1.0, rstd[:, a:b], ALU.mult, ALU.mult))

    def norm_apply(t, to):
        return V.do(v.tensor_scalar(to, X[:, t, :], mv[:, t, 0:1], rstd[:, t:t + 1], ALU.subtract, ALU.mult))

    read_stats = {}

    def norm_tiles(to, scale, table, lane, before):
        stage = {}
        for a in range(0, T + G7, G7):
            if a < T:
                before(a)
                stage[a] = norm_stats(a, a + G7, scale)
            if a:
                norm_finish(stage[a - G7], shift)
                S.after(V.last)
                norm_apply(a - G7, to[:, a - G7, 0:D])
                for t in range(a - G7 + 1, a):
                    S.do(s.activation(to[:, t, 0:D], X[:, t, :], ACT.Identity, bias=shift[:, t:t + 1],
                                      scale=rstd[:, t:t + 1]))
                Y.after(V.last, S.last)
                lane.add(y.dma_start(table[(a - G7) * P:a * P, :].rearrange("(t p) d -> p t d", p=P),
                                     to[:, a - G7:a, 0:D]))

    run_lane = Lane(nc, "runs_gathered")

    runs = view(R, 0, IJ * P * REC).rearrange("p (j e r) -> p j e r", j=IJ, r=REC)
    tb = view(R, 4 * IJ * P * REC, IJ)

    def find_items(k, ordered):
        a = 4 * IJ * P * REC + 4 * IJ
        tmp = view(R, a, IJ * T).rearrange("p (j t) -> p j t", t=T)
        o = a + 4 * IJ * T
        i_first, i_int, i_end, kcount, shift = [view(R, o + 196 * n, T, I32 if n == 1 else F32) for n in range(5)]
        o += 196 * 5
        ti, cf = [view(R, o + 28 * n, IJ) for n in range(2)]
        item_plus_one = row_id[:, 0:IJ]
        ci = view(R, o + 28 * 2, IJ, I32)
        V.step(v.tensor_tensor(i_int, incl[:, :], tot[:, :], ALU.subtract))
        V.step(v.tensor_scalar(i_int, i_int, 7, None, ALU.arith_shift_right))
        V.step(v.tensor_copy(i_first, i_int))
        V.step(v.tensor_scalar(i_int, incl[:, :], float(P - 1), None, ALU.add))
        V.step(v.tensor_scalar(i_int, i_int, 7, None, ALU.arith_shift_right))
        V.step(v.tensor_tensor(kcount, i_int, i_first, ALU.subtract))
        V.step(v.scalar_tensor_tensor(kcount, tot[:, :], 0.0, kcount, ALU.is_gt, ALU.mult))
        V.step(v.tensor_tensor_scan(i_end, ones[:, 0:T], kcount, 0.0, ALU.mult, ALU.add))
        V.step(v.tensor_tensor(shift, i_first, i_end, ALU.subtract))
        V.step(v.tensor_tensor(shift, shift, kcount, ALU.add))
        V.step(v.tensor_scalar(i_int.bitcast(F32), iota[:, 0:T], float(PER_TILE), float(PER_TILE + MARGIN),
                               ALU.mult, ALU.add))
        V.step(v.tensor_tensor(i_int.bitcast(F32), i_end, i_int.bitcast(F32), ALU.is_gt))
        late_known = V.step(v.tensor_reduce(late[:, :], i_int.bitcast(F32), AX.X, ALU.max))
        V.step(v.tensor_tensor(tmp, i_end.unsqueeze(1).broadcast_to([P, IJ, T]),
                               item_plus_one.unsqueeze(2).broadcast_to([P, IJ, T]), ALU.is_lt))
        V.step(v.tensor_reduce(ti, tmp, AX.X, ALU.add))
        V.step(v.tensor_tensor(tmp, iota[:, 0:T].unsqueeze(1).broadcast_to([P, IJ, T]),
                               ti.unsqueeze(2).broadcast_to([P, IJ, T]), ALU.is_equal))
        V.step(v.tensor_tensor(tmp, tmp, shift.unsqueeze(1).broadcast_to([P, IJ, T]), ALU.mult))
        V.step(v.tensor_reduce(cf, tmp, AX.X, ALU.add))
        V.step(v.scalar_tensor_tensor(cf, cf, -1.0, item_plus_one, ALU.add, ALU.add))
        V.step(v.tensor_scalar(ci, cf, float(CH - 1), 0.0, ALU.min, ALU.max))
        runs_known = V.last
        V.step(v.tensor_scalar(tb, ti, float(P), None, ALU.mult))
        V.step(v.tensor_scalar(cf, ti, float(T - 1), float(AW), ALU.min, ALU.mult))
        M.after(V.last)
        M.do(m.transpose(bank[0][0:IJ, 0:P], cf, ident[:, :]))
        V.after(M.last)
        V.step(v.tensor_copy(toff[0:IJ, :], bank[0][0:IJ, 0:P]))
        G.after(runs_known, *ordered)
        by_run = rec_d[k].rearrange("(c e) r -> c (e r)", e=P)
        for j in range(IJ):
            run_lane.add(g.indirect_dma_start(view(R, j * P * REC * 4, P * REC), None, by_run,
                                              IndirectOffsetOnAxis(ap=ci[:, j:j + 1], axis=0)))
        return late_known

    def take_items():
        V.after(run_lane.ticket)
        V.step(v.tensor_tensor(runs[:, :, :, 0], runs[:, :, :, 0], tb.unsqueeze(2).broadcast_to([P, IJ, P]),
                               ALU.subtract))
        copied = {}
        M.after(run_lane.ticket)
        for f in (1, 0, 2):
            if f == 0:
                M.after(V.last)
            for j in range(IJ):
                M.do(m.transpose(bank[2 * f + j // 4][:, j % 4 * P:(j % 4 + 1) * P], runs[:, j, :, f], ident[:, :]))
            for j in range(0, IJ, 4):
                cols = slice(j * P, min(IJ, j + 4) * P)
                read = bank[2 * f + j // 4][:, 0:cols.stop - cols.start]
                if f == 2:
                    S.after(M.last)
                    S.do(s.activation(wt[:, cols], read, ACT.Copy))
                elif f == 0:
                    V.after(M.last)
                    V.do(v.tensor_copy(dloc[:, cols], read))
                else:
                    V.after(M.last)
                    gathered = V.do(v.tensor_scalar(gidx[:, cols], read, float(T * P - 1), None, ALU.min))
        V.after(V.last, S.last, M.last)
        return [gathered, M.last]

    find_items(0, [])
    V.after(load_x.ticket)
    norm_tiles(XNt, None, tab, table_lane[0], lambda a: None)

    items_ready = take_items()

    scatter_lanes = [Lane(nc, f"edge_scatter{k}") for k in range(16)]
    ring_lanes = [Lane(nc, f"ring{k}") for k in range(RING)]
    ring = view(R, 0, RING * AW).rearrange("p (n a) -> p n a", a=AW)
    o = 4 * RING * AW
    onehot = view(R, o, 4 * P).rearrange("p (n c) -> p n c", c=P)
    lo_hot = view(R, o + 2048, 2 * P).rearrange("p (n c) -> p n c", c=P)
    lo_tmp = view(R, o + 3072, P)
    hi_hot = view(R, o + 3584, 2 * T).rearrange("p (n c) -> p n c", c=T)

    def aggregate(table, width, weighted, nbank, ready, extra):
        hot, summed, added = {}, {}, {}

        def one_hot(i):
            if i >= 4:
                V.after(summed[i - 4])
            if weighted:
                hot[i] = V.do(v.tensor_scalar(onehot[:, i % 4, :], iota[:, :], dloc[:, i:i + 1], wt[:, i:i + 1],
                                              ALU.is_equal, ALU.mult))
            else:
                hot[i] = V.do(v.tensor_scalar(onehot[:, i % 4, :], iota[:, :], dloc[:, i:i + 1], None,
                                              ALU.is_equal))

        def add(i):
            V.after(summed[i], added.get(i - 1))
            into = view(C, 0, T * AW)[:, ds(regs[i // 8][i % 8], width)]
            added[i] = V.do(v.tensor_tensor(into, bank[i % nbank][:, 0:width], into, ALU.add))

        G.after(*ready)
        one_hot(0)
        one_hot(1)
        regs = {}
        for i in range(ITEMS):
            if i >= RING:
                G.after(summed[i - RING])
            rows = ring_lanes[i % RING].start(
                G, lambda: g.indirect_dma_start(ring[:, i % RING, 0:D], None, table,
                                                IndirectOffsetOnAxis(ap=gidx[:, i:i + 1], axis=0)))
            if i + 2 < ITEMS:
                one_hot(i + 2)
            M.after(hot[i], rows, added.get(i - nbank))
            summed[i] = M.do(m.matmul(bank[i % nbank][:, 0:width], lhsT=onehot[:, i % 4, :],
                                      rhs=ring[:, i % RING, 0:width], start=True, stop=True))
            extra(i)
            if i % 8 == 0:
                n = min(8, ITEMS - i)
                regs[i // 8] = reg_values(ENG.DVE, toff[i // P:i // P + 1, i % P:i % P + n], (T - 1) * AW)
            if i:
                add(i - 1)
        add(ITEMS - 1)
        V.after(V.last)

    deg_done = {}
    lo_done, hi_done = {}, {}

    def beside_first(i):
        if i < EC:
            S.after(lo_done.get(i - 1), deg_done.get(i - 2))
            S.do(s.activation(lo_tmp[0:P], iota[0:P, :], ACT.Abs, bias=neg_lo[0:P, i:i + 1]))
            S.after(S.last)
            lo_done[i] = S.do(s.activation(lo_hot[0:P, i % 2, :], lo_tmp[0:P], ACT.Relu, bias=1.0, scale=-1.0))
            V.after(deg_done.get(i - 2))
            hi_done[i] = V.do(v.tensor_scalar(hi_hot[0:P, i % 2, :], iota[0:P, 0:T], kt1f[0:P, i:i + 1],
                                              rec1[0:P, i, 2:3], ALU.is_equal, ALU.mult))
        j = i - 1
        if 0 <= j < EC:
            M.after(lo_done[j], hi_done[j])
            deg_done[j] = M.do(m.matmul(bank[7][:, 0:T], lhsT=lo_hot[0:P, j % 2, :], rhs=hi_hot[0:P, j % 2, :],
                                        start=j == 0, stop=j == EC - 1))
        if i % 2 == 0 and i // 2 < T:
            count_tile(kt1, 1, i // 2)
        if i == 2 * T:
            count_ends(1, bank[5], bank[6])
        c = i - 2 * T - 2
        if c >= 0 and c % PLACE == 0 and c // PLACE < T:
            place_edges(V, kt1, 1, c // PLACE)

    V.after(load_src.ticket)
    V.step(v.tensor_scalar(int_tmp, raw_src, 7, None, ALU.arith_shift_right))
    V.step(v.tensor_copy(kt1, int_tmp))
    V.step(v.tensor_copy(kt1f, int_tmp))
    V.after(records)
    S.after(V.step(v.scalar_tensor_tensor(neg_lo, kt1f, float(P), rec1[:, :, 0], ALU.mult, ALU.subtract)))
    V.after(V.last)
    V.do(v.memset(ring[:, :, D:AW], 1.0))
    V.step(v.memset(view(C, 0, raw_end // 4), 0.0))
    aggregate(tab, AW, False, 4, [*items_ready, table_lane[0].ticket], beside_first)

    V.after(deg_done[EC - 1])
    V.step(v.tensor_scalar(deg[:, :], bank[7][:, 0:T], 1.0, None, ALU.add))
    placed1 = V.step(v.tensor_copy(idx1, pos_e))
    scatter_next = [0]

    def scatter_more(n):
        for c in range(scatter_next[0], min(EC, scatter_next[0] + n)):
            scatter_edges(G, scatter_lanes, 1, rec1, idx1, c, placed1)
        scatter_next[0] = min(EC, scatter_next[0] + n)

    scatter_more(BEFORE_SLOTS)

    def space(off, n, dt=F32, parts=P):
        return view(XN, off, n, dt, parts)

    w_lane, f0_lane = Lane(nc, "gnn0_weights_loaded"), Lane(nc, "ffn0_weights_loaded")
    w0 = view(R, 8192, KD * D).rearrange("p (k n) -> p k n", k=KD)
    gam = view(R, 8192 + 2048, D)
    bet = view(R, 8192 + 3072, D)
    mean_b = view(R, 8192 + 4096, D)
    scale_b = view(R, 8192 + 5120, D)
    rdeg = view(R, 8192 + 6144, T)
    w1a = view(R, 0, KD * HID0).rearrange("p (k n) -> p k n", k=KD)
    Y.after(M.last, V.last)
    w_lane.add(y.dma_start(w0, g0_w.rearrange("(k p) n -> p k n", p=P)))
    w_lane.add(y.dma_start(gam, g0_gamma.partition_broadcast(P)))
    w_lane.add(y.dma_start(bet, g0_beta.partition_broadcast(P)))
    f0_lane.add(y.dma_start(w1a, f0_w1.rearrange("(k p) n -> p k n", p=P)))

    V.step(v.tensor_scalar(rdeg, acc[:, :, D], 1.0, None, ALU.max))
    V.step(v.reciprocal(rdeg, rdeg))
    acc_t = view(C, tail, 3 * D).rearrange("p (n a) -> p n a", n=3)
    sq = view(C, tail + 3072, 2 * D).rearrange("p (n a) -> p n a", n=2)
    M.after(w_lane.ticket)
    V.after(w_lane.ticket)

    def transpose_rows(rows, to, *tickets):
        M.after(*tickets)
        for k in range(rows.shape[1] // P):
            M.do(m.transpose(to[:, k * P:(k + 1) * P], rows[:, k * P:(k + 1) * P], ident[:, :]))
        return M.last

    copied, prod, rst = {}, {}, {}
    for t in range(T + 2):
        if t < T:
            tr = transpose_rows(acc[:, t, 0:D], bank[t % 2], copied.get(t - 2))
            S.after(tr, prod.get(t - 3))
            copied[t] = S.do(s.activation(acc_t[:, t % 3, :], bank[t % 2][:, 0:D], ACT.Copy))
        if 1 <= t <= T:
            u = t - 1
            M.after(copied[u], rst.get(u - 2))
            for k in range(KD):
                prod[u] = M.do(m.matmul(bank[2 + u % 2][:, 0:D], lhsT=acc_t[:, u % 3, k * P:(k + 1) * P],
                                        rhs=w0[:, k, :], start=k == 0, stop=k == KD - 1))
            V.after(prod[u])
            rst[u] = V.do(v.scalar_tensor_tensor(XNt[:, u, :], bank[2 + u % 2][:, 0:D], rdeg[:, u:u + 1],
                                                 XNt[:, u, :], ALU.mult, ALU.add))
        if t >= 2:
            u = t - 2
            M.after(rst[u])
            M.do(m.matmul(bank[4][:, 0:D], lhsT=(ones_last if u == T - 1 else ones)[:, :], rhs=XNt[:, u, :],
                          start=u == 0, stop=u == T - 1))
    V.after(M.last)
    V.step(v.tensor_scalar(mean_b, bank[4][:, 0:D], 1.0 / N, None, ALU.mult))
    squared, summed_sq = {}, {}
    for t in range(T):
        V.do(v.tensor_tensor(XNt[:, t, :], XNt[:, t, :], mean_b, ALU.subtract))
        S.after(V.last, summed_sq.get(t - 2))
        squared[t] = S.do(s.activation(sq[:, t % 2, :], XNt[:, t, :], ACT.Square))
        M.after(squared[t])
        summed_sq[t] = M.do(m.matmul(bank[5][:, 0:D], lhsT=(ones_last if t == T - 1 else ones)[:, :],
                                     rhs=sq[:, t % 2, :], start=t == 0, stop=t == T - 1))
    wd = view(C, 0, E0 * KH0 * D)
    wd_lane = Lane(nc, "experts0_loaded")
    Y.after(M.last)
    for e in range(E0):
        wd_lane.add(y.dma_start(wd[:, e * KH0 * D:(e + 1) * KH0 * D].rearrange("p (k n) -> p k n", k=KH0),
                                f0_wd[e].rearrange("(k p) n -> p k n", p=P)))
    V.after(M.last)
    V.step(v.tensor_scalar(scale_b, bank[5][:, 0:D], 1.0 / N, BN_EPS, ALU.mult, ALU.add))
    S.after(V.last)
    V.after(S.do(s.activation(scale_b, scale_b, ACT.Sqrt)))
    V.step(v.reciprocal(scale_b, scale_b))
    V.step(v.tensor_tensor(scale_b, scale_b, gam, ALU.mult))
    stage = {}
    for a in range(0, T, G7):
        part = XNt[:, a:a + G7, :]
        xpart = X[:, a:a + G7, :]
        V.step(v.tensor_tensor(part, part, scale_b.unsqueeze(1).broadcast_to([P, G7, D]), ALU.mult))
        V.step(v.tensor_tensor(part, part, bet.unsqueeze(1).broadcast_to([P, G7, D]), ALU.add))
        V.step(v.scalar_tensor_tensor(xpart, part, 0.0, xpart, ALU.max, ALU.add))
        stage[a] = norm_stats(a, a + G7)
        if a:
            norm_finish(stage[a - G7])
    norm_finish(stage[T - G7])
    bn_done = V.last

    logits = view(dloc, 0, T * 8).rearrange("p (t e) -> p t e", e=8)
    probs = view(dloc, 4 * T * 8, T * 8).rearrange("p (t e) -> p t e", e=8)
    best = view(gidx[:, :].bitcast(F32), 0, T * 8).rearrange("p (t e) -> p t e", e=8)
    best_at = gidx[:, T * 8:2 * T * 8].rearrange("p (t e) -> p t e", e=8)
    chosen = view(wt, 0, 2 * T)
    r_mask = view(wt, 8 * T, 2 * T)
    r_scan = view(wt, 16 * T, 2 * T)
    r_pos = view(wt, 24 * T, 2 * T)
    r_ones = view(wt, 32 * T, 2 * T)
    r_cnt = view(wt, 40 * T, 8)
    r_off = view(wt, 40 * T + 32, 8)
    r_int = view(wt, 40 * T + 64, 8, I32)
    r_tiles = view(wt, 40 * T + 96, 8)
    r_end = view(wt, 40 * T + 128, 8)
    r_row = view(wt, 40 * T + 160, SLOTS1)
    from_row = view(wt, 40 * T + 160 + 4 * SLOTS1, SLOTS1, I32)
    gate_row = view(dloc, 64 * T, SLOTS1, I32)
    to_row = view(wt, 40 * T + 160 + 8 * SLOTS1, SLOTS1, I32)
    beyond = float(1 << 20)

    def route(ncol, slots, row, at, helped):
        V.step(v.memset(r_ones, 1.0))
        for e in range(8):
            V.step(v.tensor_scalar(r_mask[:, 0:ncol], chosen[:, 0:ncol], float(e), None, ALU.is_equal, ALU.add,
                                   accum_out=r_cnt[:, e:e + 1]))
        M.after(V.last)
        M.do(m.matmul(bank[0][:, 0:8], lhsT=ones[:, :], rhs=r_cnt, start=True, stop=True))
        M.do(m.matmul(bank[1][:, 0:8], lhsT=tri[:, :], rhs=r_cnt, start=True, stop=True))
        V.after(M.last)
        V.step(v.tensor_scalar(r_int, bank[0][:, 0:8], float(P - 1), None, ALU.add))
        V.step(v.tensor_scalar(r_int, r_int, 7, None, ALU.arith_shift_right))
        V.step(v.tensor_copy(r_tiles, r_int))
        V.step(v.tensor_tensor_scan(r_end, ones[:, 0:8], r_tiles, 0.0, ALU.mult, ALU.add))
        V.step(v.tensor_tensor(r_off, r_end, r_tiles, ALU.subtract))
        V.step(v.tensor_scalar(r_off, r_off, float(P), -1.0, ALU.mult, ALU.add))
        V.step(v.tensor_tensor(r_off, r_off, bank[1][:, 0:8], ALU.add))
        for e in range(8):
            V.step(v.tensor_scalar(r_mask[:, 0:ncol], chosen[:, 0:ncol], float(e), None, ALU.is_equal))
            V.step(v.tensor_tensor_scan(r_scan[:, 0:ncol], r_ones[:, 0:ncol], r_mask[:, 0:ncol],
                                        r_off[:, e:e + 1], ALU.mult, ALU.add))
            V.step(v.copy_predicated(r_pos[:, 0:ncol], r_mask[:, 0:ncol].bitcast(U32), r_scan[:, 0:ncol]))
        hi, lo, whole = r_mask[:, 0:ncol], r_pos[:, 0:ncol], pos[:, 0:ncol]
        V.step(v.tensor_copy(whole, r_pos[:, 0:ncol]))
        V.step(v.tensor_scalar(whole, whole, 7, None, ALU.arith_shift_right))
        V.step(v.tensor_copy(hi, whole))
        V.step(v.scalar_tensor_tensor(lo, hi, -float(P), r_pos[:, 0:ncol], ALU.mult, ALU.add))
        lo_row = space(at, 4 * P).rearrange("p (n c) -> p n c", c=P)
        hi_row = space(at + 2048, 4 * P).rearrange("p (n c) -> p n c", c=P)
        used = {}
        ready = V.last
        for c in range(ncol):
            q = G if helped and c % 5 in (0, 2, 4) else V
            V.after(used.get(c - 4))
            q.after(ready, used.get(c - 4))
            lo_in = V.do(v.tensor_scalar(lo_row[:, c % 4, :], iota[:, :], r_pos[:, c:c + 1], row_id[:, c:c + 1],
                                         ALU.is_equal, ALU.mult))
            hi_in = q.do(q.e.tensor_scalar(hi_row[:, c % 4, 0:slots], iota[:, 0:slots],
                                           r_mask[:, c:c + 1], None, ALU.is_equal))
            M.after(lo_in, hi_in)
            used[c] = M.do(m.matmul(bank[2][:, 0:slots], lhsT=lo_row[:, c % 4, :], rhs=hi_row[:, c % 4, 0:slots],
                                    start=c == 0, stop=c == ncol - 1))
        cmp = gidx[0:1, 0:slots * 8].bitcast(F32).rearrange("p (i e) -> p i e", e=8)
        V.step(v.tensor_tensor(cmp, r_end[0:1].unsqueeze(1).broadcast_to([1, slots, 8]),
                               iota[0:1, 0:slots].unsqueeze(2).broadcast_to([1, slots, 8]), ALU.is_le))
        V.step(v.tensor_reduce(r_row[0:1, 0:slots], cmp, AX.X, ALU.add))
        V.step(v.tensor_scalar(texp[0:1, 0:slots], r_row[0:1, 0:slots], 7.0, float(row), ALU.min, ALU.mult))
        V.after(M.last)
        got = lo_row[:, 0, 0:slots]
        empty = lo_row[:, 1, 0:slots]
        second = lo_row[:, 2, 0:slots]
        V.step(v.tensor_copy(got, bank[2][:, 0:slots]))
        V.step(v.tensor_scalar(empty, got, 0.0, beyond, ALU.is_equal, ALU.mult))
        V.step(v.tensor_scalar(got, got, -1.0, 0.0, ALU.add, ALU.max))
        V.step(v.tensor_copy(gate_row[:, 0:slots], got))
        V.step(v.tensor_scalar(second, got, float(T * P), -float(T * P), ALU.is_ge, ALU.mult))
        V.step(v.tensor_tensor(got, got, second, ALU.add))
        V.do(v.tensor_tensor(to_row[:, 0:slots], got, empty, ALU.add))
        return V.step(v.tensor_copy(from_row[:, 0:slots], got))

    y_lanes = [Lane(nc, f"expert_rows_scattered{k}") for k in range(4)]

    def scatter_out(i, rows, *tickets):
        return y_lanes[i % 4].start(G, lambda: g.indirect_dma_start(
            tok_y, IndirectOffsetOnAxis(ap=to_row[:, i:i + 1], axis=0), rows, None,
            bounds_check=T * P - 1, oob_is_err=False), *tickets)

    comb_lanes = [Lane(nc, f"outputs_loaded{k}") for k in range(NCB)]
    comb_read = {}

    comb_rows = {}

    def combine_load(a):
        b = (a // G7) % NCB
        buf = space(b * G7 * D * 4, G7 * D).rearrange("p (t d) -> p t d", d=D)
        rows = tok_y[a * P:(a + G7) * P, :].rearrange("(t p) d -> p t d", p=P)
        q = (Y, S)[(a // G7) % 2]
        comb_rows[a] = comb_lanes[b].start(q, lambda: q.e.dma_start(buf, rows), comb_read.get(b)), buf, b

    def combine(a):
        if a == 0:
            for ahead in range(0, NCB - 1):
                combine_load(ahead * G7)
        if a + (NCB - 1) * G7 < T:
            combine_load(a + (NCB - 1) * G7)
        loaded, buf, b = comb_rows[a]
        V.after(loaded, V.last)
        for t in range(a, a + G7):
            V.do(v.scalar_tensor_tensor(X[:, t, :], buf[:, t - a, :], gate[:, t:t + 1], X[:, t, :],
                                        ALU.mult, ALU.add))
        comb_read[b] = V.last
        V.after(V.last)

    xr = space(0, 4 * D).rearrange("p (n d) -> p n d", d=D)
    xt = space(4096, 2 * D).rearrange("p (n d) -> p n d", d=D)
    hr = space(6144, 3 * HID0).rearrange("p (n h) -> p n h", h=HID0)
    ht = space(18432, 2 * HID0).rearrange("p (n h) -> p n h", h=HID0)
    b1b = space(26624, HID0)
    wg0 = space(30720, KH0 * 8).rearrange("p (k e) -> p k e", e=8)
    bg0 = space(30720 + 256, 8)
    bd = view(R, 8192, E0 * D)
    Y.after(bn_done)
    f0_lane.add(y.dma_start(b1b, f0_b1.partition_broadcast(P)))
    f0_lane.add(y.dma_start(wg0, f0_wg.rearrange("(k p) e -> p k e", p=P)))
    f0_lane.add(y.dma_start(bg0, f0_bg.partition_broadcast(P)))
    f0_lane.add(y.dma_start(bd, f0_bd.rearrange("e d -> (e d)").partition_broadcast(P)))
    for q in (M, V):
        q.after(f0_lane.ticket)
    hid_lanes = [Lane(nc, f"hidden_stored{k}") for k in range(3)]
    x_in, x_tr, xt_in, biased, gelud, h_tr, ht_in, lg_mm, lg_out = ({} for _ in range(9))
    for t in range(T + 3):
        if t < T:
            V.after(x_tr.get(t - 4))
            x_in[t] = norm_apply(t, xr[:, t % 4, :])
            x_tr[t] = transpose_rows(xr[:, t % 4, :], bank[t % 2], x_in[t], xt_in.get(t - 2))
            S.after(x_tr[t], h_tr.get(("mm", t - 2)))
            xt_in[t] = S.do(s.activation(xt[:, t % 2, :], bank[t % 2][:, 0:D], ACT.Copy))
        u = t - 1
        if 0 <= u < T:
            M.after(xt_in[u])
            V.after(hid_lanes[u % 3].ticket)
            for half in range(2):
                M.after(biased.get(2 * u + half - 2))
                cols = slice(half * 512, half * 512 + 512)
                for k in range(KD):
                    M.do(m.matmul(bank[2 + half][:, :], lhsT=xt[:, u % 2, k * P:(k + 1) * P], rhs=w1a[:, k, cols],
                                  start=k == 0, stop=k == KD - 1))
                V.after(M.last, h_tr.get(u - 3))
                biased[2 * u + half] = V.do(v.tensor_tensor(hr[:, u % 3, cols], bank[2 + half][:, :], b1b[:, cols],
                                                            ALU.add))
                S.after(V.last)
                gelud[u, half] = S.do(s.activation(hr[:, u % 3, cols], hr[:, u % 3, cols], ACT.Gelu))
            h_tr["mm", u] = M.last
            hid_lanes[u % 3].start(Y, lambda: y.dma_start(hid_d[u * P:(u + 1) * P, :], hr[:, u % 3, :]), gelud[u, 1])
        u = t - 2
        if 0 <= u < T:
            for half in range(2):
                transpose_rows(hr[:, u % 3, half * 512:half * 512 + 512], bank[4 + half], gelud[u, half],
                               ht_in.get((u - 1, half)))
                q = (S, V)[half]
                q.after(M.last, lg_mm.get(u - 2))
                dst_h = ht[:, u % 2, half * 512:half * 512 + 512]
                ht_in[u, half] = (S.do(s.activation(dst_h, bank[4][:, :], ACT.Copy)) if half == 0 else
                                  V.do(v.tensor_copy(dst_h, bank[5][:, :])))
            h_tr[u] = M.last
        u = t - 3
        if 0 <= u < T:
            M.after(ht_in[u, 0], ht_in[u, 1], lg_out.get(u - 2))
            for c in range(KH0):
                M.do(m.matmul(bank[6 + u % 2][:, 0:8], lhsT=ht[:, u % 2, c * P:(c + 1) * P], rhs=wg0[:, c, :],
                              start=c == 0, stop=c == KH0 - 1))
            lg_mm[u] = M.last
            V.after(M.last)
            lg_out[u] = V.do(v.tensor_tensor(logits[:, u, :], bank[6 + u % 2][:, 0:8], bg0, ALU.add))
    V.after(V.last)
    red = view(wt, 0, T)
    V.step(v.tensor_reduce(red, logits, AX.X, ALU.max))
    V.step(v.tensor_tensor(probs, logits, red.unsqueeze(2).broadcast_to([P, T, 8]), ALU.subtract))
    S.after(V.last)
    V.after(S.do(s.activation(probs, probs, ACT.Exp)))
    V.step(v.tensor_reduce(red, probs, AX.X, ALU.add))
    V.step(v.reciprocal(red, red))
    V.step(v.tensor_tensor(probs, probs, red.unsqueeze(2).broadcast_to([P, T, 8]), ALU.mult))
    for t in range(T):
        V.do(v.max(best[:, t, :], probs[:, t, :]))
    V.after(V.last)
    for t in range(T):
        V.do(v.max_index(best_at[:, t, :].bitcast(U32), best[:, t, :], probs[:, t, :]))
    V.after(V.last)
    V.do(v.tensor_copy(gate[:, 0:T], best[:, :, 0]))
    V.step(v.tensor_copy(chosen[:, 0:T], best_at[:, :, 0]))
    routed = route(T, SLOTS0, KH0 * D, 34816, False)

    NG = 4
    hg = space(0, NG * HID0).rearrange("p (n h) -> p n h", h=HID0)
    ys = space(30720, 4 * D).rearrange("p (n d) -> p n d", d=D)
    hg_lanes = [Lane(nc, f"hidden_gathered{k}") for k in range(NG)]
    M.after(wd_lane.ticket, routed)
    G.after(routed, *[l.ticket for l in hid_lanes])
    hg_in, h_tr, ht_in, mm2, y_in = ({} for _ in range(5))

    def gather_hidden(i):
        if i < SLOTS0:
            hg_in[i] = hg_lanes[i % NG].start(G, lambda: g.indirect_dma_start(
                hg[:, i % NG, :], None, hid_d, IndirectOffsetOnAxis(ap=from_row[:, i:i + 1], axis=0)), h_tr.get(i - NG))

    for i in range(3):
        gather_hidden(i)
    regs_m, regs_v = {}, {}
    for i in range(SLOTS0 + 1):
        if i < SLOTS0:
            if i % 4 == 0:
                regs_m[i // 4] = reg_values(ENG.PE, texp[0:1, i:i + 4], 7 * KH0 * D)
                regs_v[i // 4] = reg_values(ENG.DVE, texp[0:1, i:i + 4], 7 * KH0 * D)
            for half in range(2):
                b = bank[2 * (i % 2) + half]
                transpose_rows(hg[:, i % NG, half * 512:half * 512 + 512], b, hg_in[i], ht_in.get((i - 2, half)))
                q = (S, V)[half]
                q.after(M.last, mm2.get(i - 2))
                dst_h = ht[:, i % 2, half * 512:half * 512 + 512]
                ht_in[i, half] = (S.do(s.activation(dst_h, b[:, :], ACT.Copy)) if half == 0 else
                                  V.do(v.tensor_copy(dst_h, b[:, :])))
            h_tr[i] = M.last
            gather_hidden(i + 3)
            scatter_more(2)
        u = i - 1
        if u >= 0:
            M.after(ht_in[u, 0], ht_in[u, 1], y_in.get(u - 2))
            for c in range(KH0):
                M.do(m.matmul(bank[4 + u % 2][:, 0:D], lhsT=ht[:, u % 2, c * P:(c + 1) * P],
                              rhs=wd[:, ds(regs_m[u // 4][u % 4] + c * D, D)], start=c == 0, stop=c == KH0 - 1))
            mm2[u] = M.last
            V.after(M.last, y_lanes[u % 4].ticket)
            y_in[u] = V.do(v.tensor_tensor(ys[:, u % 4, :], bank[4 + u % 2][:, 0:D],
                                           bd[:, ds(regs_v[u // 4][u % 4] // KH0, D)], ALU.add))
            scatter_out(u, ys[:, u % 4, :], y_in[u])
    scattered = [l.ticket for l in y_lanes]
    scatter_more(EC)

    dm = view(wt, 0, T)
    V.after(G.last, *scattered)
    V.step(v.tensor_scalar(dm, deg[:, :], 0.0, None, ALU.is_gt))
    V.step(v.tensor_scalar(deg[:, :], deg[:, :], 1e-30, None, ALU.max))
    S.after(V.last)
    V.after(S.do(s.activation(deg[:, :], deg[:, :], ACT.Sqrt)))
    V.step(v.reciprocal(deg[:, :], deg[:, :]))
    V.step(v.tensor_tensor(deg[:, :], deg[:, :], dm, ALU.mult))

    Y.after(V.last, M.last, *scattered)
    S.after(V.last, M.last, *scattered)
    V.after(M.last)
    norm_tiles(acc, deg, tab1, table_lane[1], combine)
    late_known = find_items(1, [l.ticket for l in scatter_lanes])
    items_ready = take_items()

    gw_lane = Lane(nc, "gcn_weights_loaded")
    rec_space = rec1[:, :, :].rearrange("p e r -> p (e r)")
    gcn_w = [view(rec_space, 2048 * n, KD * D).rearrange("p (k n) -> p k n", k=KD) for n in range(3)]
    b2_b = view(rec_space, 6144, D)
    wg1 = view(rec_space, 7168, KD * 8).rearrange("p (k e) -> p k e", e=8)
    bg1 = view(rec_space, 7232, 8)
    bias1 = view(rec_space, 7264, 8)
    Y.after(*[l.ticket for l in scatter_lanes])
    for w_sb, w in zip(gcn_w, (g1_w, g1_w1, g1_w2)):
        gw_lane.add(y.dma_start(w_sb, w.rearrange("(k p) n -> p k n", p=P)))
    gw_lane.add(y.dma_start(b2_b, g1_b2.partition_broadcast(P)))
    gw_lane.add(y.dma_start(bcol[:, 0:2], g1_b.rearrange("(k p) -> p k", p=P), allow_slow_non_contiguous=True))
    gw_lane.add(y.dma_start(bcol[:, 2:4], g1_b1.rearrange("(k p) -> p k", p=P), allow_slow_non_contiguous=True))
    gw_lane.add(y.dma_start(wg1, f1_wg.rearrange("(k p) e -> p k e", p=P)))
    gw_lane.add(y.dma_start(bg1, f1_bg.partition_broadcast(P)))
    gw_lane.add(y.dma_start(bias1, f1_bias.partition_broadcast(P)))

    def beside_second(i):
        if i == 16:
            V.step(v.tensor_tensor(bg1, bg1, bias1, ALU.add))
        if i >= 20 and i % 8 == 0 and (i - 20) // 8 < T:
            t = (i - 20) // 8
            V.do(v.tensor_tensor(X[:, t, :], X[:, t, :], b2_b, ALU.add))

    def pair(n):
        return space(2048 * n, KD * G2 * P).rearrange("p (k n) -> p k n", k=KD)

    at_b, bt_b, ct_b = [pair(0), pair(1)], [pair(2), pair(3)], [pair(4), pair(5)]
    xt2 = space(12288, 2 * G2 * D).rearrange("p (n a) -> p n a", n=2)
    norm2 = space(16384, 3 * G2 * D).rearrange("p (n t d) -> p n t d", n=3, d=D)
    logits1 = space(40960, T * 8).rearrange("p (t e) -> p t e", e=8)
    best1 = space(43008, T * 8).rearrange("p (t e) -> p t e", e=8)
    best_at1 = space(45056, T * 8, I32).rearrange("p (t e) -> p t e", e=8)
    pairs = [(a, min(G2, T - a)) for a in range(0, T, G2)]
    norm_lanes = [Lane(nc, f"normed_stored{k}") for k in range(3)]
    out_lanes = [Lane(nc, f"x_stored{k}") for k in range(3)]

    def head_stages():
        scaled, a_tr, a_in, b_mm, b_in, c_mm, c_in, x_mm, x_out, stage, applied = ({} for _ in range(11))
        g_tr, g_in, g_mm, g_out = {}, {}, {}, {}

        def scale(gi, a, n):
            V.after(V.last)
            for t in range(a, a + n):
                scaled[gi] = V.do(v.tensor_scalar(acc[:, t, 0:D], acc[:, t, 0:D], deg[:, t:t + 1], None, ALU.mult))

        def transpose_sums(gi, a, n):
            M.after(scaled[gi], a_in.get(gi - 1))
            for k in range(KD):
                for j in range(n):
                    a_tr[gi] = M.do(m.transpose(bank[2][:, (k * G2 + j) * P:(k * G2 + j + 1) * P],
                                                acc[:, a + j, k * P:(k + 1) * P], ident[:, :]))

        def copy_sums(gi, a, n):
            V.after(a_tr[gi], b_mm.get(gi - 2))
            src_b = bank[2][:, :].rearrange("p (k n) -> p k n", k=KD)
            a_in[gi] = V.do(v.tensor_copy(at_b[gi % 2][:, :, 0:n * P], src_b[:, :, 0:n * P]))

        def product(b, w_sb, frm, to, ready, mm, done, free, col, fn):
            def run(gi, a, n):
                M.after(ready[gi], done.get(gi - 1))
                for c in range(KD):
                    for k in range(KD):
                        mm[gi] = M.do(m.matmul(bank[b][:, c * G2 * P:c * G2 * P + n * P],
                                               lhsT=w_sb[:, k, c * P:(c + 1) * P], rhs=frm[gi % 2][:, k, 0:n * P],
                                               start=k == 0, stop=k == KD - 1))
                S.after(mm[gi], free.get(gi - 2))
                for c in range(KD):
                    done[gi] = S.do(s.activation(to[gi % 2][:, c, 0:n * P],
                                                 bank[b][:, c * G2 * P:c * G2 * P + n * P],
                                                 fn, bias=bcol[:, col + c:col + c + 1]))
            return run

        def last_product(gi, a, n):
            M.after(c_in[gi], x_out.get(gi - 1))
            for j in range(n):
                for k in range(KD):
                    x_mm[gi] = M.do(m.matmul(bank[5][:, j * D:(j + 1) * D],
                                             lhsT=ct_b[gi % 2][:, k, j * P:(j + 1) * P], rhs=gcn_w[2][:, k, :],
                                             start=k == 0, stop=k == KD - 1))

        def residual(gi, a, n):
            V.after(x_mm[gi], V.last)
            x_out[gi] = V.step(v.tensor_tensor(X[:, a:a + n, :], bank[5][:, 0:n * D].rearrange("p (t d) -> p t d", d=D),
                                               X[:, a:a + n, :], ALU.add))
            stage[gi] = norm_stats(a, a + n)

        def norm(gi, a, n):
            norm_finish(stage[gi])
            V.after(g_tr.get(gi - 3), norm_lanes[gi % 3].ticket)
            for j in range(n):
                applied[gi] = norm_apply(a + j, norm2[:, gi % 3, j, :])
            norm_lanes[gi % 3].start(Y, lambda: y.dma_start(
                tab2[a * P:(a + n) * P, :].rearrange("(t p) d -> p t d", p=P), norm2[:, gi % 3, 0:n, :]), applied[gi])

            full = n if a + n < T else n - 1
            if full:
                out_lanes[gi % 3].start(Y, lambda: y.dma_start(
                    out[a * P:(a + full) * P, :].rearrange("(t p) d -> p t d", p=P), X[:, a:a + full, :]), x_out[gi])
            if full < n:
                out_lanes[gi % 3].start(Y, lambda: y.dma_start(out[(T - 1) * P:N, :], X[0:LAST, T - 1, :]), x_out[gi])

        def transpose_normed(gi, a, n):
            M.after(applied[gi], g_in.get(gi - 1))
            for j in range(n):
                g_tr[gi] = transpose_rows(norm2[:, gi % 3, j, :], bank[6][:, j * D:(j + 1) * D])
            S.after(g_tr[gi], g_mm.get(gi - 2))
            g_in[gi] = S.do(s.activation(xt2[:, gi % 2, 0:n * D], bank[6][:, 0:n * D], ACT.Copy))

        def gate_product(gi, a, n):
            M.after(g_in[gi], g_out.get(gi - 1))
            for j in range(n):
                for k in range(KD):
                    g_mm[gi] = M.do(m.matmul(bank[7][:, j * 8:(j + 1) * 8],
                                             lhsT=xt2[:, gi % 2, j * D + k * P:j * D + (k + 1) * P],
                                             rhs=wg1[:, k, :], start=k == 0, stop=k == KD - 1))

        def two_best(gi, a, n):
            V.after(g_mm[gi])
            g_out[gi] = V.step(v.tensor_tensor(logits1[:, a:a + n, :],
                                               bank[7][:, 0:n * 8].rearrange("p (t e) -> p t e", e=8),
                                               bg1.unsqueeze(1).broadcast_to([P, n, 8]), ALU.add))
            for t in range(a, a + n):
                V.do(v.max(best1[:, t, :], logits1[:, t, :]))
            V.after(V.last)
            for t in range(a, a + n):
                V.do(v.max_index(best_at1[:, t, :].bitcast(U32), best1[:, t, :], logits1[:, t, :]))

        return (scale, transpose_sums, copy_sums,
                product(3, gcn_w[0], at_b, bt_b, a_in, b_mm, b_in, c_mm, 0, ACT.Identity),
                product(4, gcn_w[1], bt_b, ct_b, b_in, c_mm, c_in, x_mm, 2, ACT.Relu),
                last_product, residual, norm, transpose_normed, gate_product, two_best)

    def second_layer(start, step):
        stages = head_stages()
        order = sorted((start(gi) + n * step, -n, gi) for gi in range(len(pairs)) for n in range(len(stages)))

        def run_until(i):
            while order and order[0][0] <= i:
                _, n, gi = order.pop(0)
                stages[-n](gi, *pairs[gi])

        def beside(i):
            beside_second(i)
            run_until(i)

        read_stats.clear()
        aggregate(tab1, D, True, 2, [*items_ready, table_lane[1].ticket], beside)
        run_until(order[-1][0])

    for q in (V, S, M, G, Y):
        q.after(gw_lane.ticket, late_known)
    is_late = nc.values_load_multi_w_load_instructions(
        late[0:1, 0:1], engines=[ENG.DVE, ENG.Activation, ENG.PE, ENG.Pool, ENG.SP], min_val=0, max_val=1,
        skip_runtime_bounds_check_because="a comparison's result")[1][0]
    counters = [V, S, M, G, Y, *ring_lanes, *norm_lanes, *out_lanes]
    before = [c.state() for c in counters]
    with nc.If(is_late > 0):
        second_layer(lambda gi: ITEMS + gi, 1)
    ends = [c.state() for c in counters]
    for c, state in zip(counters, before):
        c.restore(state)
    with nc.Else():
        second_layer(lambda gi: PER_TILE * min(T, G2 * (gi + 1)) + MARGIN + 1, STEP)
    assert [c.value() for c in counters] == [e[0] for e in ends]
    for c, state in zip(counters, before):
        c.forget_waits(state)
    read_stats.clear()
    normed_stored = [l.ticket for l in norm_lanes]

    w1e = view(C, 0, E1 * KD * HID1)
    w2e = view(C, 4 * E1 * KD * HID1, E1 * KH1 * D)
    b1e = view(R, 0, E1 * HID1)
    b2e = view(rec_space, 0, E1 * D)
    ew_lane = Lane(nc, "experts1_loaded")
    Y.after(V.last, M.last, S.last)
    S.after(V.last, M.last)
    for e in range(E1):
        ew_lane.add(y.dma_start(w1e[:, e * KD * HID1:(e + 1) * KD * HID1].rearrange("p (k n) -> p k n", k=KD),
                                f1_w1[e].rearrange("(k p) n -> p k n", p=P)))
        ew_lane.add(y.dma_start(w2e[:, e * KH1 * D:(e + 1) * KH1 * D].rearrange("p (k n) -> p k n", k=KH1),
                                f1_w2[e].rearrange("(k p) n -> p k n", p=P)))
    ew_lane.add(y.dma_start(b1e, f1_b1.rearrange("e h -> (e h)").partition_broadcast(P)))
    ew_lane.add(y.dma_start(b2e, f1_b2.rearrange("e d -> (e d)").partition_broadcast(P)))
    V.after(V.last)
    V.step(v.tensor_tensor(gate[:, T:2 * T], best1[:, :, 1], best1[:, :, 0], ALU.subtract))
    S.after(V.last)
    V.after(S.do(s.activation(gate[:, T:2 * T], gate[:, T:2 * T], ACT.Exp)))
    V.step(v.tensor_scalar(gate[:, 0:T], gate[:, T:2 * T], 1.0, None, ALU.add))
    V.step(v.reciprocal(gate[:, 0:T], gate[:, 0:T]))
    V.step(v.tensor_tensor(gate[:, T:2 * T], gate[:, T:2 * T], gate[:, 0:T], ALU.mult))
    gate_t = space(41984, P, F32, 2 * T)
    M.after(V.last)
    M.do(m.transpose(bank[3][0:2 * T, 0:P], gate[:, :], ident[:, :]))
    S.after(M.last)
    S.do(s.activation(gate_t, bank[3][0:2 * T, 0:P], ACT.Copy))
    gate_lane = Lane(nc, "gates_stored")
    gate_lane.start(Y, lambda: y.dma_start(gate_d.rearrange("(c p) o -> c (p o)", p=P), gate_t), S.last)
    V.do(v.tensor_copy(chosen[:, 0:T], best_at1[:, :, 0]))
    V.step(v.tensor_copy(chosen[:, T:2 * T], best_at1[:, :, 1]))
    V.after(*normed_stored)
    routed = route(2 * T, SLOTS1, KD * HID1, 34816, True)

    NX = 5
    xg = space(0, NX * D).rearrange("p (n d) -> p n d", d=D)
    xt3 = space(5120, 3 * D).rearrange("p (n d) -> p n d", d=D)
    h1 = space(8192, 2 * HID1).rearrange("p (n h) -> p n h", h=HID1)
    h1t = space(12288, 2 * HID1).rearrange("p (n h) -> p n h", h=HID1)
    ys1 = space(16384, 4 * D).rearrange("p (n d) -> p n d", d=D)
    NGATE = 8
    slot_gate = space(20480, NGATE).rearrange("p (n o) -> p n o", o=1)
    xg_lanes = [Lane(nc, f"slot_rows_gathered{k}") for k in range(NX)]
    gate_lanes = [Lane(nc, f"slot_gates_gathered{k}") for k in range(NGATE)]
    added_out = Lane(nc, "expert_rows_added")
    gate_in, y_out, added = {}, {}, {}

    def add_out(i, *tickets):
        return added_out.start(G, lambda: g.indirect_dma_start(
            out, IndirectOffsetOnAxis(ap=to_row[:, i:i + 1], axis=0), ys1[:, i % 4, :], None,
            bounds_check=N - 1, oob_is_err=False, compute_op=ALU.add), *tickets)

    for q in (M, V):
        q.after(ew_lane.ticket, routed)
    G.after(routed, *normed_stored, gate_lane.ticket, *[l.ticket for l in out_lanes])
    xg_in, x_tr, xt_in, mm1, h_in, h_tr, ht_in, mm2, y_in = ({} for _ in range(9))
    regs_m, regs_v = {}, {}

    def gather_rows(i):
        if i < SLOTS1:
            xg_in[i] = xg_lanes[i % NX].start(G, lambda: g.indirect_dma_start(
                xg[:, i % NX, :], None, tab2, IndirectOffsetOnAxis(ap=from_row[:, i:i + 1], axis=0)), x_tr.get(i - NX))
            gate_in[i] = gate_lanes[i % NGATE].start(G, lambda: g.indirect_dma_start(
                slot_gate[:, i % NGATE, :], None, gate_d, IndirectOffsetOnAxis(ap=gate_row[:, i:i + 1], axis=0)),
                y_out.get(i - NGATE))

    def slot_rows_transposed(i):
        if i < SLOTS1:
            x_tr[i] = transpose_rows(xg[:, i % NX, :], bank[i % 2], xg_in[i], xt_in.get(i - 2))
            S.after(x_tr[i], mm1.get(i - 3))
            xt_in[i] = S.do(s.activation(xt3[:, i % 3, :], bank[i % 2][:, 0:D], ACT.Copy))

    for i in range(4):
        gather_rows(i)
    slot_rows_transposed(0)
    for i in range(SLOTS1 + 1):
        slot_rows_transposed(i + 1)
        gather_rows(i + 4)
        if i < SLOTS1 and i % 4 == 0:
            n = min(4, SLOTS1 - i)
            regs_m[i // 4] = reg_values(ENG.PE, texp[0:1, i:i + n], 7 * KD * HID1)
            regs_v[i // 4] = reg_values(ENG.DVE, texp[0:1, i:i + n], 7 * KD * HID1)
        u = i - 1
        if u >= 0:
            h_tr[u] = transpose_rows(h1[:, u % 2, :], bank[4], h_in[u], ht_in.get(u - 1))
            S.after(M.last, mm2.get(u - 2))
            ht_in[u] = S.do(s.activation(h1t[:, u % 2, :], bank[4][:, :], ACT.Relu))
        if i < SLOTS1:
            M.after(xt_in[i], h_in.get(i - 2))
            for k in range(KD):
                M.do(m.matmul(bank[2 + i % 2][:, :], lhsT=xt3[:, i % 3, k * P:(k + 1) * P],
                              rhs=w1e[:, ds(regs_m[i // 4][i % 4] + k * HID1, HID1)], start=k == 0, stop=k == KD - 1))
            mm1[i] = M.last
            V.after(M.last, h_tr.get(i - 2))
            h_in[i] = V.do(v.tensor_tensor(h1[:, i % 2, :], bank[2 + i % 2][:, :],
                                           b1e[:, ds(regs_v[i // 4][i % 4] // KD, HID1)], ALU.add))
        if u >= 0:
            M.after(ht_in[u], y_in.get(u - 2))
            for c in range(KH1):
                M.do(m.matmul(bank[5 + u % 2][:, 0:D], lhsT=h1t[:, u % 2, c * P:(c + 1) * P],
                              rhs=w2e[:, ds(regs_m[u // 4][u % 4] + c * D, D)], start=c == 0, stop=c == KH1 - 1))
            mm2[u] = M.last
            V.after(M.last, added.get(u - 4))
            y_in[u] = V.do(v.tensor_tensor(ys1[:, u % 4, :], bank[5 + u % 2][:, 0:D],
                                           b2e[:, ds(regs_v[u // 4][u % 4] // KH1, D)], ALU.add))
            V.after(y_in[u], gate_in[u])
            y_out[u] = V.do(v.tensor_scalar(ys1[:, u % 4, :], ys1[:, u % 4, :], slot_gate[:, u % NGATE, :], None,
                                            ALU.mult))
            added[u] = add_out(u, y_out[u])

    for q in (G, Y):
        q.after(added_out.ticket)


_INS = ["x", "src", "dst", "edge_weight", "L0_gnn_W_src", "L0_gnn_gamma", "L0_gnn_beta", "L0_ffn_W1", "L0_ffn_b1",
        "L0_ffn_Wg", "L0_ffn_bg", "L0_ffn_Wd", "L0_ffn_bd", "L1_gnn_W", "L1_gnn_b", "L1_gnn_W1", "L1_gnn_b1",
        "L1_gnn_W2", "L1_gnn_b2", "L1_ffn_Wg", "L1_ffn_bg", "L1_ffn_bias", "L1_ffn_W1", "L1_ffn_b1", "L1_ffn_W2",
        "L1_ffn_b2"]


def kernel(**inputs):
    import concourse.bacc as bacc
    from concourse.bass_utils import run_bass_kernel_spmd

    nc = bacc.Bacc("TRN2", target_bir_lowering=False, num_devices=1)
    arrays, args = {}, []
    for name in _INS:
        a = np.ascontiguousarray(inputs[name])
        arrays[f"in_{name}"] = a
        args.append(nc.dram_tensor(f"in_{name}", a.shape, mybir.dt.from_np(a.dtype), kind="ExternalInput").ap())
    args.append(nc.dram_tensor("out_rows", (N, D), F32, kind="ExternalOutput").ap())
    build(nc, *args)
    r = run_bass_kernel_spmd(nc, [arrays], core_ids=[0])
    return r.results[0]["out_rows"]
```
